# Optimizing a Trainium2 kernel written in Bass

```python
import numpy as np
import jax
import jax.numpy as jnp

def _softmax(x, axis=-1):
    return jax.nn.softmax(x, axis=axis)

def _gelu(x):
    return jax.nn.gelu(x, approximate=True)

def _silu(x):
    return jax.nn.silu(x)

def _sigmoid(x):
    return jax.nn.sigmoid(x)

def _layernorm(x, axis=-1, eps=1e-05):
    m = jnp.mean(x, axis=axis, keepdims=True)
    v = jnp.var(x, axis=axis, keepdims=True)
    return (x - m) / jnp.sqrt(v + eps)

def _scatter_add(tgt, idx, src, axis=0):
    return tgt.at[idx].add(src)

def _segment_sum(src, seg, n):
    return jax.ops.segment_sum(src, seg, n)
kernel_name = 'mk_seq_postln_d2_jaxref_r8_128fe3'

def setup_inputs(seed: int=0):
    np.random.seed(seed)
    _w = jnp.asarray

    def _L0_attn_setup():
        import jax, jax.numpy as jnp
        import numpy as np
        EPS = 1e-08

        def rms_norm(x, scale):
            d = x.shape[-1]
            norm = jnp.linalg.norm(x, ord=2, axis=-1, keepdims=True)
            rms = norm * d ** (-0.5)
            return scale * (x / (rms + EPS))
        key = jax.random.key(seed)
        ks = jax.random.split(key, 4)
        B, N, C, H = (2, 256, 128, 16)
        hd = C // H
        x = jax.random.normal(ks[0], (B, N, C), dtype=jnp.float32)
        Wqkv = jax.random.normal(ks[1], (C, 3 * C), dtype=jnp.float32) * C ** (-0.5)
        Wproj = jax.random.normal(ks[2], (C, C), dtype=jnp.float32) * C ** (-0.5)
        bproj = jnp.zeros((C,), dtype=jnp.float32)
        q_scale = jnp.ones((hd,), dtype=jnp.float32)
        k_scale = jnp.ones((hd,), dtype=jnp.float32)
        return {'x': x, 'Wqkv': Wqkv, 'Wproj': Wproj, 'bproj': bproj, 'q_scale': q_scale, 'k_scale': k_scale}
    _L0_attn_in = _L0_attn_setup()

    def _L0_ffn_setup():
        import jax, jax.numpy as jnp
        import numpy as np
        import math
        D_MODEL = 128
        N_EXPERTS = 16
        D_FF = 512
        CAP_FACTOR = 1.25
        MIN_CAPACITY = 4

        def _capacity(num_tokens, num_experts):
            cap = math.floor(CAP_FACTOR * num_tokens / num_experts)
            cap += cap % 2
            return max(cap, MIN_CAPACITY)

        def _top1_router(gate_logits, capacity):
            s, e = gate_logits.shape
            probs = jax.nn.softmax(gate_logits, axis=-1)
            top1 = jnp.argmax(gate_logits, axis=-1)
            mask = jax.nn.one_hot(top1, e, dtype=jnp.int32)
            ranks = jnp.cumsum(mask, axis=0) - 1
            mask = mask * (ranks < capacity).astype(jnp.int32)
            rank1 = jnp.sum(mask * ranks, axis=-1)
            ranks_oh = jax.nn.one_hot(rank1, capacity, dtype=probs.dtype)
            weight = mask.astype(probs.dtype) * probs
            combine_weights = weight[:, :, None] * ranks_oh[:, None, :]
            sec_mask = combine_weights > 0
            return (combine_weights, sec_mask)
        key = jax.random.key(seed)
        k1, k2, k3, k4 = jax.random.split(key, 4)
        x = jax.random.normal(k1, (4, 256, D_MODEL), dtype=jnp.float32)
        gate_w = jax.random.normal(k2, (N_EXPERTS, D_MODEL), dtype=jnp.float32) * math.sqrt(0.1 / D_MODEL)
        w1 = jax.random.normal(k3, (N_EXPERTS, D_MODEL, D_FF), dtype=jnp.float32) * (1.0 / math.sqrt(D_MODEL))
        w2 = jax.random.normal(k4, (N_EXPERTS, D_FF, D_MODEL), dtype=jnp.float32) * (1.0 / math.sqrt(D_FF))
        return {'x': x, 'gate_w': gate_w, 'w1': w1, 'w2': w2}
    _L0_ffn_in = _L0_ffn_setup()

    def _L1_attn_setup():
        import jax, jax.numpy as jnp
        import numpy as np
        HEADS, D_MODEL, D_V = (16, 128, 64)
        D_K = D_MODEL // HEADS
        key = jax.random.key(seed)
        k1, k2, k3, k4, k5 = jax.random.split(key, 5)
        B, T = (2, 256)
        s = 1.0 / np.sqrt(D_MODEL)
        return {'x': jax.random.normal(k1, (B, T, D_MODEL), dtype=jnp.float32), 'Wq': jax.random.normal(k2, (D_MODEL, HEADS * D_K), dtype=jnp.float32) * s, 'Wk': jax.random.normal(k3, (D_MODEL, HEADS * D_K), dtype=jnp.float32) * s, 'Wv': jax.random.normal(k4, (D_MODEL, HEADS * D_V), dtype=jnp.float32) * s, 'Wo': jax.random.normal(k5, (HEADS * D_V, D_MODEL), dtype=jnp.float32) * (1.0 / np.sqrt(HEADS * D_V))}
    _L1_attn_in = _L1_attn_setup()

    def _L1_ffn_setup():
        import jax, jax.numpy as jnp
        import numpy as np
        B, S, DIM = (4, 512, 128)
        BASE_COUPLING = 0.1
        NUM_CYCLES = 3

        def _gelu(x):
            return jax.nn.gelu(x, approximate=False)

        def _coupling_net(h, w1, b1, w2, b2, w3, b3, w4, b4):
            h = _gelu(h @ w1 + b1)
            h = _gelu(h @ w2 + b2)
            h = _gelu(h @ w3 + b3)
            return jax.nn.sigmoid(h @ w4 + b4)

        def _global_net(h, w1, b1, w2, b2, w3, b3):
            h = _gelu(h @ w1 + b1)
            h = _gelu(h @ w2 + b2)
            return jax.nn.sigmoid(h @ w3 + b3)

        def _twist(x):
            o_r, o_i, p_r, p_i = jnp.split(x, 4, axis=-1)
            return jnp.concatenate([p_r, -p_i, -o_r, o_i], axis=-1)
        key = jax.random.key(seed)
        ks = jax.random.split(key, 9)
        d = DIM

        def w(k, fan_in, fan_out):
            return jax.random.normal(k, (fan_in, fan_out), dtype=jnp.float32) / np.sqrt(fan_in).astype(np.float32)
        inp = {'x': jax.random.normal(ks[0], (B, S, d), dtype=jnp.float32)}
        cn_dims = [(d, d), (d, d // 2), (d // 2, d // 4), (d // 4, 1)]
        for i, (a, b) in enumerate(cn_dims):
            inp[f'cn_w{i + 1}'] = w(ks[1 + i], a, b)
            inp[f'cn_b{i + 1}'] = jnp.zeros((b,), dtype=jnp.float32)
        gc_dims = [(d, d // 2), (d // 2, d // 4), (d // 4, 1)]
        for i, (a, b) in enumerate(gc_dims):
            inp[f'gc_w{i + 1}'] = w(ks[5 + i], a, b)
            inp[f'gc_b{i + 1}'] = jnp.zeros((b,), dtype=jnp.float32)
        inp['adaptive_range'] = jnp.full((1,), 0.2, dtype=jnp.float32)
        return inp
    _L1_ffn_in = _L1_ffn_setup()
    _d = {'L0_attn_x': _L0_attn_in['x'], 'L0_attn_Wqkv': _L0_attn_in['Wqkv'], 'L0_attn_Wproj': _L0_attn_in['Wproj'], 'L0_attn_bproj': _L0_attn_in['bproj'], 'L0_attn_q_scale': _L0_attn_in['q_scale'], 'L0_attn_k_scale': _L0_attn_in['k_scale'], 'L0_ffn_gate_w': _L0_ffn_in['gate_w'], 'L0_ffn_w1': _L0_ffn_in['w1'], 'L0_ffn_w2': _L0_ffn_in['w2'], 'L1_attn_Wq': _L1_attn_in['Wq'], 'L1_attn_Wk': _L1_attn_in['Wk'], 'L1_attn_Wv': _L1_attn_in['Wv'], 'L1_attn_Wo': _L1_attn_in['Wo'], 'L1_ffn_cn_w1': _L1_ffn_in['cn_w1'], 'L1_ffn_cn_b1': _L1_ffn_in['cn_b1'], 'L1_ffn_cn_w2': _L1_ffn_in['cn_w2'], 'L1_ffn_cn_b2': _L1_ffn_in['cn_b2'], 'L1_ffn_cn_w3': _L1_ffn_in['cn_w3'], 'L1_ffn_cn_b3': _L1_ffn_in['cn_b3'], 'L1_ffn_cn_w4': _L1_ffn_in['cn_w4'], 'L1_ffn_cn_b4': _L1_ffn_in['cn_b4'], 'L1_ffn_gc_w1': _L1_ffn_in['gc_w1'], 'L1_ffn_gc_b1': _L1_ffn_in['gc_b1'], 'L1_ffn_gc_w2': _L1_ffn_in['gc_w2'], 'L1_ffn_gc_b2': _L1_ffn_in['gc_b2'], 'L1_ffn_gc_w3': _L1_ffn_in['gc_w3'], 'L1_ffn_gc_b3': _L1_ffn_in['gc_b3'], 'L1_ffn_adaptive_range': _L1_ffn_in['adaptive_range']}
    _x0 = _d['L0_attn_x']
    _d['L0_attn_x'] = jax.random.normal(jax.random.fold_in(jax.random.key(seed), 1), (16, 256, 128), dtype=_x0.dtype)
    del _x0
    return _d

def reference(L0_attn_x, L0_attn_Wqkv, L0_attn_Wproj, L0_attn_bproj, L0_attn_q_scale, L0_attn_k_scale, L0_ffn_gate_w, L0_ffn_w1, L0_ffn_w2, L1_attn_Wq, L1_attn_Wk, L1_attn_Wv, L1_attn_Wo, L1_ffn_cn_w1, L1_ffn_cn_b1, L1_ffn_cn_w2, L1_ffn_cn_b2, L1_ffn_cn_w3, L1_ffn_cn_b3, L1_ffn_cn_w4, L1_ffn_cn_b4, L1_ffn_gc_w1, L1_ffn_gc_b1, L1_ffn_gc_w2, L1_ffn_gc_b2, L1_ffn_gc_w3, L1_ffn_gc_b3, L1_ffn_adaptive_range):

    def _L0_attn_ref(x, Wqkv, Wproj, bproj, q_scale, k_scale):
        import jax, jax.numpy as jnp
        import numpy as np
        EPS = 1e-08

        def rms_norm(x, scale):
            d = x.shape[-1]
            norm = jnp.linalg.norm(x, ord=2, axis=-1, keepdims=True)
            rms = norm * d ** (-0.5)
            return scale * (x / (rms + EPS))
        B, N, C = x.shape
        H = 16
        hd = C // H
        scale = hd ** (-0.5)
        qkv = (x @ Wqkv).reshape(B, N, 3, H, hd)
        qkv = jnp.transpose(qkv, (2, 0, 3, 1, 4))
        q, k, v = (qkv[0], qkv[1], qkv[2])
        q = rms_norm(q, q_scale)
        k = rms_norm(k, k_scale)
        attn = jnp.einsum('bhnc,bhmc->bhnm', q, k) * scale
        attn = jax.nn.softmax(attn, axis=-1)
        out = jnp.einsum('bhnm,bhmc->bhnc', attn, v)
        out = jnp.transpose(out, (0, 2, 1, 3)).reshape(B, N, C)
        return out @ Wproj + bproj

    def _L0_ffn_ref(x, gate_w, w1, w2):
        import jax, jax.numpy as jnp
        import numpy as np
        import math
        D_MODEL = 128
        N_EXPERTS = 16
        D_FF = 512
        CAP_FACTOR = 1.25
        MIN_CAPACITY = 4

        def _capacity(num_tokens, num_experts):
            cap = math.floor(CAP_FACTOR * num_tokens / num_experts)
            cap += cap % 2
            return max(cap, MIN_CAPACITY)

        def _top1_router(gate_logits, capacity):
            s, e = gate_logits.shape
            probs = jax.nn.softmax(gate_logits, axis=-1)
            top1 = jnp.argmax(gate_logits, axis=-1)
            mask = jax.nn.one_hot(top1, e, dtype=jnp.int32)
            ranks = jnp.cumsum(mask, axis=0) - 1
            mask = mask * (ranks < capacity).astype(jnp.int32)
            rank1 = jnp.sum(mask * ranks, axis=-1)
            ranks_oh = jax.nn.one_hot(rank1, capacity, dtype=probs.dtype)
            weight = mask.astype(probs.dtype) * probs
            combine_weights = weight[:, :, None] * ranks_oh[:, None, :]
            sec_mask = combine_weights > 0
            return (combine_weights, sec_mask)
        tokens = x.reshape(-1, D_MODEL)
        s = tokens.shape[0]
        capacity = _capacity(s, N_EXPERTS)
        gate_logits = tokens.astype(jnp.float32) @ gate_w.T
        combine_weights, sec_mask = _top1_router(gate_logits, capacity)
        dispatch = jnp.einsum('sec,sd->ecd', sec_mask.astype(tokens.dtype), tokens)
        h = jax.nn.gelu(jnp.einsum('ecd,edf->ecf', dispatch, w1))
        expert_out = jnp.einsum('ecf,efd->ecd', h, w2)
        out = jnp.einsum('sec,ecd->sd', combine_weights.astype(tokens.dtype), expert_out)
        return out.reshape(x.shape)

    def _L1_attn_ref(x, Wq, Wk, Wv, Wo):
        import jax, jax.numpy as jnp
        import numpy as np
        HEADS, D_MODEL, D_V = (16, 128, 64)
        D_K = D_MODEL // HEADS
        B, T, _ = x.shape
        scale = jnp.asarray(np.sqrt(D_K), x.dtype)
        q = (x @ Wq).reshape(B, T, HEADS, D_K).transpose(0, 2, 1, 3)
        k = (x @ Wk).reshape(B, T, HEADS, D_K).transpose(0, 2, 1, 3)
        v = (x @ Wv).reshape(B, T, HEADS, D_V).transpose(0, 2, 1, 3)
        scores = jnp.einsum('bhqd,bhkd->bhqk', q, k) / scale
        causal = jnp.triu(jnp.ones((T, T), dtype=bool), k=1)
        scores = jnp.where(causal, jnp.asarray(-jnp.inf, scores.dtype), scores)
        attn = jax.nn.softmax(scores, axis=-1)
        ctx = jnp.einsum('bhqk,bhkd->bhqd', attn, v)
        out = ctx.transpose(0, 2, 1, 3).reshape(B, T, HEADS * D_V)
        return out @ Wo

    def _L1_ffn_ref(x, cn_w1, cn_b1, cn_w2, cn_b2, cn_w3, cn_b3, cn_w4, cn_b4, gc_w1, gc_b1, gc_w2, gc_b2, gc_w3, gc_b3, adaptive_range):
        import jax, jax.numpy as jnp
        import numpy as np
        B, S, DIM = (4, 512, 128)
        BASE_COUPLING = 0.1
        NUM_CYCLES = 3

        def _gelu(x):
            return jax.nn.gelu(x, approximate=False)

        def _coupling_net(h, w1, b1, w2, b2, w3, b3, w4, b4):
            h = _gelu(h @ w1 + b1)
            h = _gelu(h @ w2 + b2)
            h = _gelu(h @ w3 + b3)
            return jax.nn.sigmoid(h @ w4 + b4)

        def _global_net(h, w1, b1, w2, b2, w3, b3):
            h = _gelu(h @ w1 + b1)
            h = _gelu(h @ w2 + b2)
            return jax.nn.sigmoid(h @ w3 + b3)

        def _twist(x):
            o_r, o_i, p_r, p_i = jnp.split(x, 4, axis=-1)
            return jnp.concatenate([p_r, -p_i, -o_r, o_i], axis=-1)
        global_context = x.mean(axis=1, keepdims=True)
        gf = _global_net(global_context, gc_w1, gc_b1, gc_w2, gc_b2, gc_w3, gc_b3)
        out = x
        for _ in range(NUM_CYCLES):
            tf = _coupling_net(out, cn_w1, cn_b1, cn_w2, cn_b2, cn_w3, cn_b3, cn_w4, cn_b4)
            combined = 0.7 * gf + 0.3 * tf
            coupling = BASE_COUPLING + adaptive_range * (combined - 0.5) * 2.0
            out = out + coupling * _twist(out)
        return out
    x = L0_attn_x
    x = _layernorm(x + _L0_attn_ref(x, L0_attn_Wqkv, L0_attn_Wproj, L0_attn_bproj, L0_attn_q_scale, L0_attn_k_scale), axis=-1)
    x = _layernorm(x + _L0_ffn_ref(x, L0_ffn_gate_w, L0_ffn_w1, L0_ffn_w2), axis=-1)
    x = _layernorm(x + _L1_attn_ref(x, L1_attn_Wq, L1_attn_Wk, L1_attn_Wv, L1_attn_Wo), axis=-1)
    x = _layernorm(x + _L1_ffn_ref(x, L1_ffn_cn_w1, L1_ffn_cn_b1, L1_ffn_cn_w2, L1_ffn_cn_b2, L1_ffn_cn_w3, L1_ffn_cn_b3, L1_ffn_cn_w4, L1_ffn_cn_b4, L1_ffn_gc_w1, L1_ffn_gc_b1, L1_ffn_gc_w2, L1_ffn_gc_b2, L1_ffn_gc_w3, L1_ffn_gc_b3, L1_ffn_adaptive_range), axis=-1)
    return x

_drawn_inputs = setup_inputs


def setup_inputs(seed=0):
    import zlib

    import numpy as np

    out = dict(_drawn_inputs(seed))
    spreads = {'L0_attn_bproj': (0.0, 0.1),
     'L0_attn_q_scale': (1.0, 0.2),
     'L0_attn_k_scale': (1.0, 0.6),
     'L1_ffn_cn_b1': (0.0, 0.8),
     'L1_ffn_cn_b2': (0.0, 2.0),
     'L1_ffn_cn_b3': (0.0, 2.0),
     'L1_ffn_gc_b1': (0.0, 0.8),
     'L1_ffn_gc_b2': (0.0, 2.0)}
    factors = {'L1_ffn_cn_w1': 7.434,
     'L1_ffn_cn_w2': 5.984,
     'L1_ffn_cn_w3': 5.672,
     'L1_ffn_cn_w4': 5.42,
     'L1_ffn_gc_w1': 8.0,
     'L1_ffn_gc_w2': 6.848,
     'L1_ffn_gc_w3': 8.0}
    for name, (base, spread) in spreads.items():
        noise = np.random.default_rng([zlib.crc32(name.encode()), seed]).standard_normal(out[name].shape)
        drawn = base * np.exp(spread * noise) if base else spread * noise
        out[name] = jnp.asarray(drawn.astype(out[name].dtype))
    for name, factor in factors.items():
        out[name] = (out[name] * factor).astype(out[name].dtype)
    return out
```

```python
from contextlib import ExitStack

import concourse.bass as bass
from concourse import mybir

FP32 = mybir.dt.float32
BF16 = mybir.dt.bfloat16
I32 = mybir.dt.int32
U32 = mybir.dt.uint32
ALU = mybir.AluOpType
ACT = mybir.ActivationFunctionType
AX = mybir.AxisListType

P = 128
B, N, C = 16, 256, 128
NB = N // P
T = B * N
H, HD = 16, 8
QUADS = H // 4
EPS_LN = 1e-5
EPS_RMS = 1e-8
SCALE = HD ** -0.5

E, FF = 16, 512
CAP = int(1.25 * T / E)
CAP += CAP % 2
SLOTS = E * CAP
FC = FF // P

MEETS = ((0, 3), (1, 2), (2, 1))
TERMS = sum(n for _, n in MEETS)
SHIFT_ROW = 64


def load_stacks(eng, parts_d, q_st, k_st, loaded):
    src = parts_d.rearrange("t (c h) n -> t c h n", h=H)
    queries = src.rearrange("t c h n -> (t c) h n")
    first = 0
    for part, n in MEETS:
        eng.dma_start(q_st[first:first + n * HD, :, :], queries[0:n * HD, :, 0:N]).then_inc(loaded, 16)
        keys = src[part, :, :, N:2 * N].unsqueeze(0).broadcast_to([n, HD, H, N])
        eng.dma_start(k_st[first:first + n * HD, :, :], keys).then_inc(loaded, 16)
        first += n * HD


STACK_LOADS = 2 * len(MEETS)


class Steps:

    def __init__(self, eng, sem, per_batch):
        self.eng, self.sem, self.per_batch = eng, sem, per_batch

    def batch(self, b):
        self.base, self.n = b * self.per_batch, 0
        return self

    def did(self, ins):
        ins.then_inc(self.sem, 1)
        self.n += 1

    def wait(self):
        self.eng.wait_ge(self.sem, self.base + self.n)

    def end(self):
        assert self.n == self.per_batch, (self.n, self.per_batch)


def at_least(eng, sem, value):
    if not isinstance(value, int) or value > 0:
        eng.wait_ge(sem, value)


def wait_apart(eng, k, *waits):
    waits = [(sem, value if isinstance(value, int) else eng.compute_val(value)) for sem, value in waits]
    eng.wait_ge(k["constants_set"], 1)
    for sem, value in waits:
        at_least(eng, sem, value)


def pipelined(eng, step, ahead, behind, total=B, unroll=2, first=0):
    lo, hi = max(behind, first), total - ahead
    hi -= (hi - lo) % unroll
    for b in range(-ahead, lo):
        step(b, b // unroll, b % unroll)
    with eng.Fori(0, (hi - lo) // unroll) as turn:
        for b in range(lo, lo + unroll):
            step(turn * unroll + b, turn + b // unroll, b % unroll)
    for b in range(hi, total + behind):
        step(b, b // unroll, b % unroll)


def real(b):
    return not isinstance(b, int) or 0 <= b < B


def newton_rsqrt(eng, steps, v, y, t):
    steps.did(eng.tensor_scalar(t.bitcast(I32), v.bitcast(I32), 1, None, ALU.logical_shift_right))
    steps.wait()
    steps.did(eng.tensor_scalar(y.bitcast(I32), t.bitcast(I32), -1.0, float(0x5F3759DF), ALU.mult, ALU.add))
    for _ in range(3):
        steps.wait()
        steps.did(eng.tensor_tensor(t, y, y, ALU.mult))
        steps.wait()
        steps.did(eng.scalar_tensor_tensor(t, t, -0.5, v, ALU.mult, ALU.mult))
        steps.wait()
        steps.did(eng.scalar_tensor_tensor(y, t, 1.5, y, ALU.add, ALU.mult))


NEWTON = 11


def constants(nc, k, gate_w, q_scale, k_scale):
    with ExitStack() as ctx:
        sb = lambda name, shape, dt: ctx.enter_context(nc.sbuf_tensor(name, shape, dt))
        sem = lambda name: ctx.enter_context(nc.semaphore(name))
        iota_base = sb("iota_base", [P, E], I32)
        iota_back = sb("iota_back", [P, E], I32)
        iota_dump = sb("iota_dump", [P, NB], I32)
        gate_rows = sb("gate_rows", [E, C], FP32)
        ks = sb("ks_rep", [P, HD], FP32)
        small = sb("bound_parts", [P, 4], FP32)
        gps = ctx.enter_context(nc.psum_tensor("gate_ps", [P, E], FP32))
        filled, cut, loaded = sem("filled"), sem("cut"), sem("loaded")
        gate_turned, step = sem("gate_turned"), sem("const_step")
        block = ctx.enter_context(nc.Block())

        @block.sync
        def _(sp):
            sp.dma_start(gate_rows[:, :], gate_w).then_inc(loaded, 16)
            sp.dma_start(k["qks"][:, :], q_scale[None, :].broadcast_to([P, HD])).then_inc(loaded, 16)
            sp.dma_start(ks[:, :], k_scale[None, :].broadcast_to([P, HD])).then_inc(loaded, 16)

        @block.gpsimd
        def _(pool):
            pool.memset(k["ident"][:, :], 0.0).then_inc(filled, 1)
            pool.memset(k["tri_bf"][:, :], 1.0).then_inc(filled, 1)
            pool.memset(k["causal"][:, :], 0.0).then_inc(filled, 1)
            pool.iota(iota_base[:, :], pattern=[[CAP, E]], base=0, channel_multiplier=0).then_inc(filled, 1)
            pool.iota(iota_back[:, :], pattern=[[-1, E]], base=E, channel_multiplier=0).then_inc(filled, 1)
            pool.iota(iota_dump[:, :], pattern=[[P, NB]], base=SLOTS, channel_multiplier=1).then_inc(filled, 1)
            pool.wait_ge(filled, 6)
            pool.affine_select(out=k["ident"][:, :], in_=k["ident"][:, :], compare_op=ALU.not_equal, fill=1.0,
                               base=0, pattern=[[-1, P]], channel_multiplier=1).then_inc(cut, 1)
            pool.affine_select(out=k["tri_bf"][:, :], in_=k["tri_bf"][:, :], compare_op=ALU.is_ge, fill=0.0,
                               base=0, pattern=[[1, P]], channel_multiplier=-1).then_inc(cut, 1)
            pool.affine_select(out=k["causal"][:, :].rearrange("p (a b) -> p a b", b=P),
                               in_=k["causal"][:, :].rearrange("p (a b) -> p a b", b=P),
                               compare_op=ALU.is_ge, fill=-1e30,
                               base=0, pattern=[[0, 4], [-1, P]], channel_multiplier=1).then_inc(cut, 1)

        @block.tensor
        def _(pe):
            pe.wait_ge(loaded, 48)
            pe.wait_ge(cut, 1)
            pe.transpose(gps[:, :], gate_rows[:, :], k["ident"][0:E, 0:E]).then_inc(gate_turned, 1)

        @block.vector
        def _(dve):
            s = Steps(dve, step, 99).batch(0)
            s.did(dve.memset(k["ones"][:, :], 1.0))
            s.did(dve.memset(k["ones_bf"][:, :].bitcast(I32), 0x3F803F80))
            s.did(dve.memset(k["minus_half"][:, :], -0.5))
            s.did(dve.memset(k["zeros"][:, :], 0.0))
            dve.wait_ge(gate_turned, 1)
            s.did(dve.tensor_copy(k["gate_T"][:, :], gps[:, :]))
            dve.wait_ge(cut, 3)
            s.did(dve.tensor_copy(k["ident_bf"][:, :], k["ident"][:, :]))
            s.did(dve.tensor_copy(k["backwards"][:, :], iota_back[:, :]))
            s.did(dve.tensor_copy(k["slots_before"][:, :], iota_base[:, :]))
            s.did(dve.tensor_copy(k["dump"][:, :], iota_dump[:, :]))
            s.wait()
            s.did(dve.tensor_scalar(k["slots_end"][:, :], k["slots_before"][:, :], float(CAP), None, ALU.add))
            s.wait()
            s.did(dve.tensor_scalar(k["slots_before"][:, :], k["slots_before"][:, :], -1.0, None, ALU.add))
            dve.wait_ge(loaded, 48)
            s.did(dve.tensor_tensor(k["qks"][:, :], k["qks"][:, :], ks[:, :], ALU.mult))
            s.wait()
            s.did(dve.tensor_reduce(small[:, 0:1], k["qks"][:, :], AX.X, ALU.max, apply_absolute_value=True))
            s.wait()
            s.did(dve.tensor_scalar(k["minus_bound"][:, :], small[:, 0:1], -HD * SCALE, None, ALU.mult))
            s.wait()
            dve.nop().then_inc(k["constants_set"], 1)



def l0_layer(nc, k, x, Wqkv, Wproj, bproj, w1, w2, parts_d, x1_d, disp_d):
    SC = 4 * N
    CHUNKS = QUADS * NB
    RING = 4
    VW = 2 * HD
    VQ = 8 * VW + VW
    G2 = NB * H * 2

    def v_first(j):
        return VQ * j - VW * (j % 2)

    with ExitStack() as ctx:
        sb = lambda name, shape, dt: ctx.enter_context(nc.sbuf_tensor("l0_" + name, shape, dt))
        pb = lambda name, shape, dt: ctx.enter_context(nc.psum_tensor("l0_" + name, shape, dt))
        sem = lambda name: ctx.enter_context(nc.semaphore("l0_" + name))
        two = range(2)
        w_qkv = sb("w_qkv", [P, 3 * C], FP32)
        w_proj = sb("w_proj", [P, C], FP32)
        b_proj = sb("b_proj", [P, C], FP32)
        xin = [sb(f"xin{i}", [P, NB, C], FP32) for i in two]
        xr = [sb(f"xr{i}", [P, NB, C], FP32) for i in two]
        xT = [sb(f"xT{i}", [P, N], FP32) for i in two]
        sq = sb("sq", [P, NB, 2 * C], FP32)
        ms = sb("ms", [P, G2], FP32)
        nr_y = sb("nr_y", [P, G2], FP32)
        nr_t = sb("nr_t", [P, G2], FP32)
        rms = sb("rms", [P, G2], FP32)
        qkn = [sb(f"qkn{i}", [P, NB, 2 * C], FP32) for i in two]
        parts = [sb(f"parts{i}", [P, 3, 2 * N], BF16) for i in two]
        rest = sb("rest", [P, 2 * N], FP32)
        q_st = [sb(f"q_st{i}", [P, H, N], BF16) for i in two]
        k_st = [sb(f"k_st{i}", [P, H, N], BF16) for i in two]
        vpad = [sb(f"vpad{i}", [P, NB, QUADS * VQ], FP32) for i in two]
        probs = [sb(f"probs{i}", [P, SC], FP32) for i in range(RING)]
        o_sb = sb("o_sb", [P, 2 * N], FP32)
        rden = sb("rden", [P, NB * H], FP32)
        att = sb("att", [P, NB * C], FP32)
        attT = sb("attT", [P, N], FP32)
        y = sb("y", [P, NB, C], FP32)
        stats = sb("stats", [P, NB, 6], FP32)
        mv = sb("mv", [P, NB, 2], FP32)
        veps = sb("veps", [P, NB], FP32)
        rstd = sb("rstd", [P, NB], FP32)
        x1 = [sb(f"x1_{i}", [P, NB, C], FP32) for i in two]
        x1T = sb("x1T", [P, N], FP32)
        lg = sb("lg", [P, NB, E], FP32)
        top = sb("top", [P, NB], FP32)
        below = sb("below", [P, NB, E], FP32)
        ex = sb("ex", [P, NB, E], FP32)
        cand = sb("cand", [P, NB, E], FP32)
        first = sb("first", [P, NB], FP32)
        hot = sb("hot", [P, NB, E], FP32)
        hot_bf = sb("hot_bf", [P, NB, E], BF16)
        rank = sb("rank", [P, NB, E], FP32)
        picked = sb("picked", [P, NB, E], FP32)
        slot = sb("slot", [P, NB], FP32)
        limit = sb("limit", [P, NB], FP32)
        keep = sb("keep", [P, NB], FP32)
        kept_slot = sb("kept_slot", [P, NB], FP32)
        spare = sb("spare", [P, NB], FP32)
        esum = sb("esum", [P, NB], FP32)
        prob = sb("prob", [P, NB], FP32)
        sidx = [sb(f"sidx{i}", [P, NB], U32) for i in two]
        ps_s = [pb(f"ps_s{i}", [P, SC], FP32) for i in two]
        ps_o = pb("ps_o", [P, 2 * N], FP32)
        ps_a = [pb(f"ps_a{i}", [P, 512], FP32) for i in two]
        ps_b = pb("ps_b", [P, 512], FP32)

        w_in, cleared, v_ones = sem("w_in"), sem("cleared"), sem("v_ones")
        x_in, xr_in = [sem(f"x_in{i}") for i in two], [sem(f"xr_in{i}") for i in two]
        xT_ps, xT_sb, qk_ps, sq_sb, v_ps, v_sb = (sem(n) for n in ("xT_ps", "xT_sb", "qk_ps", "sq_sb", "v_ps", "v_sb"))
        norm_step, kn_done, qkT_ps, hi_sb = (sem(n) for n in ("norm_step", "kn_done", "qkT_ps", "hi_sb"))
        split_step, lo_sb, parts_out, stacks_in = (sem(n) for n in ("split_step", "lo_sb", "parts_out", "stacks_in"))
        scores_ps, probs_sb, pv_done, o_out = (sem(n) for n in ("scores_ps", "probs_sb", "pv_done", "o_out"))
        oT_ps, att_step, attT_ps, attT_sb, proj_ps = (sem(n) for n in ("oT_ps", "att_step", "attT_ps", "attT_sb", "proj_ps"))
        xr_step, ln_step, pow_step, x1T_ps, x1T_sb = (sem(n) for n in ("xr_step", "ln_step", "pow_step", "x1T_ps", "x1T_sb"))
        logit_ps, gate_step, exp_sb, rank_ps, rank_step = (sem(n) for n in ("logit_ps", "gate_step", "exp_sb", "rank_ps", "rank_step"))
        disp_zero = sem("disp_zero")
        x1_out, sent = [sem(f"x1_out{i}") for i in two], [sem(f"sent{i}") for i in two]
        block = ctx.enter_context(nc.Block())

        NORM, SPLIT, ATT, LN, POW, GATE, RANK = 2 + NEWTON + 3 + NB, 2, 2, 1 + 2 * NB + NB, 2, 7, 16
        STATS = 1 + 2 * NB
        V_OUT = NB
        STACKS = STACK_LOADS
        W_IN = 16 * (2 + H)

        def rows(dram, b):
            r = dram[b * N:(b + 1) * N, :] if isinstance(b, int) else dram[bass.ds(b * N, N), :]
            return r.rearrange("(j p) c -> p j c", p=P)

        @block.sync
        def _(sp):
            sp.dma_start(w_qkv[:, :], Wqkv).then_inc(w_in, 16)
            for n in range(SLOTS // (5 * P)):
                part = disp_d[n * 5 * P:(n + 1) * 5 * P, :].rearrange("(p a) c -> p (a c)", a=5)
                sp.dma_start(part, k["zeros"][:, :]).then_inc(disp_zero, 16)
            for h in range(H):
                t, u, g = h // 8, h // 4 % 2, h % 4
                r = HD * (8 * t + 2 * g + u)
                sp.dma_start(w_proj[r:r + HD, :], Wproj[h * HD:(h + 1) * HD, :]).then_inc(w_in, 16)
            sp.dma_start(b_proj[:, :], bproj[None, :].broadcast_to([P, C])).then_inc(w_in, 16)
            for e, (w1_e, w2_e) in enumerate(zip(k["w1"], k["w2"])):
                sp.dma_start(w1_e[:, :], w1[e]).then_inc(k["w_in"][e], 16)
                sp.dma_start(w2_e[:, :, :], w2[e].rearrange("(f p) c -> p f c", p=P)).then_inc(k["w_in"][e], 16)
            sp.wait_ge(cleared, 4)

            def step(b, hb, p):
                o = 1 - p
                if real(b + 3):
                    wait_apart(sp, k, (xT_ps, b + 2))
                    sp.dma_start(xin[o][:, :, :], rows(x, b + 3)).then_inc(x_in[o], 16)
                if real(b):
                    if real(b - 2):
                        wait_apart(sp, k, (ln_step, (b - 2) * LN + 1))
                    sp.dma_start(xr[p][:, :, :], rows(x, b)).then_inc(xr_in[p], 16)
                if real(b + 1):
                    sp.wait_ge(lo_sb, b + 2)
                    sp.dma_start(parts_d.rearrange("t p n -> p t n"), parts[o][:, :, :]).then_inc(parts_out, 16)
                    wait_apart(sp, k, (parts_out, (b + 2) * 16),
                                      (scores_ps, b * CHUNKS))
                    load_stacks(sp, parts_d, q_st[o], k_st[o], stacks_in)
                    wait_apart(sp, k, (stacks_in, (b + 2) * 16 * STACKS))
                if real(b - 1):
                    wait_apart(sp, k, (ln_step, b * LN))
                    sp.dma_start(rows(x1_d, b - 1), x1[o][:, :, :]).then_inc(x1_out[o], 16)

            pipelined(sp, step, 3, 2)
            for i in two:
                sp.wait_ge(x1_out[i], 16 * B // 2)

        @block.tensor
        def _(pe):
            ident, ident_bf = k["ident"], k["ident_bf"]
            pe.wait_ge(w_in, W_IN)
            pe.wait_ge(v_ones, 4)

            def scores(b, p, c):
                j, kb = divmod(c, NB)
                if c == 0:
                    pe.wait_ge(stacks_in, (b + 1) * 16 * STACKS)
                at_least(pe, probs_sb, b * CHUNKS + c - 1)
                for g in range(4):
                    last = pe.matmul(ps_s[c % 2][:, g * N:(g + 1) * N], k_st[p][:, 4 * j + g, kb * P:(kb + 1) * P],
                                     q_st[p][:, 4 * j + g, :], start=True, stop=True)
                last.then_inc(scores_ps, 1)

            def context(b, p, c):
                j, kb = divmod(c, NB)
                t, u = divmod(j, 2)
                if c == 0:
                    at_least(pe, o_out, b)
                    pe.wait_ge(v_sb, (b + 1) * V_OUT)
                pe.wait_ge(probs_sb, b * CHUNKS + c + 1)
                for g in range(4):
                    f = v_first(j) + 32 * g
                    last = pe.matmul(ps_o[32 * g:32 * g + 32, t * N:(t + 1) * N], vpad[p][:, kb, f:f + 32],
                                     probs[c % RING][:, g * N:(g + 1) * N],
                                     start=u == 0 and kb == 0, stop=u == 1 and kb == NB - 1)
                last.then_inc(pv_done, 1)

            def step(b, hb, p):
                o = 1 - p
                for c in range(CHUNKS):
                    if real(b):
                        scores(b, p, c)
                    if c == 0 and real(b + 2):
                        pe.wait_ge(x_in[p], (hb + 2) * 16)
                        at_least(pe, split_step, (b + 2) * SPLIT)
                        for j in range(NB):
                            last = pe.transpose(ps_a[0][:, j * P:(j + 1) * P], xin[p][:, j, :], ident[:, :])
                        last.then_inc(xT_ps, 1)
                    if c == 0 and real(b - 2):
                        pe.wait_ge(x1T_sb, b - 1)
                        for j in range(NB):
                            last = pe.matmul(ps_b[:, j * E:(j + 1) * E], x1T[:, j * P:(j + 1) * P], k["gate_T"][:, :],
                                             start=True, stop=True)
                        last.then_inc(logit_ps, 1)
                    if c == 1 and real(b + 2):
                        pe.wait_ge(xT_sb, b + 3)
                        at_least(pe, v_sb, (b + 1) * V_OUT)
                        for j in range(NB):
                            last = pe.matmul(ps_a[j][:, 0:2 * C], xT[p][:, j * P:(j + 1) * P], w_qkv[:, 0:2 * C],
                                             start=True, stop=True)
                        last.then_inc(qk_ps, 1)
                    if c == 1 and real(b - 2):
                        pe.wait_ge(gate_step, (b - 1) * GATE)
                        at = lambda n: ps_b[:, (2 + n) * E:(3 + n) * E]
                        pe.matmul(at(0), k["tri_bf"][:, :], hot_bf[:, 0, :], start=True, stop=True)
                        pe.matmul(at(1), k["ones_bf"][:, :], hot_bf[:, 0, :], start=True, stop=False)
                        pe.matmul(at(1), k["tri_bf"][:, :], hot_bf[:, 1, :], start=False, stop=True)
                        pe.matmul(at(2), k["ones_bf"][:, :], hot_bf[:, 0, :], start=True, stop=False)
                        pe.matmul(at(2), k["ones_bf"][:, :], hot_bf[:, 1, :], start=False, stop=True)\
                          .then_inc(rank_ps, 1)
                    if c == 2 and real(b - 1):
                        pe.wait_ge(o_out, b)
                        at_least(pe, rank_step, (b - 2) * RANK + 2)
                        for q in range(NB):
                            for t in range(2):
                                last = pe.transpose(ps_b[:, (2 * q + t) * P:(2 * q + t + 1) * P],
                                                    o_sb[:, t * N + q * P:t * N + (q + 1) * P], ident[:, :])
                        last.then_inc(oT_ps, 1)
                    if c == 3 and real(b - 1):
                        pe.wait_ge(att_step, b * ATT)
                        for j in range(NB):
                            last = pe.transpose(ps_b[:, j * P:(j + 1) * P], att[:, j * C:(j + 1) * C], ident[:, :])
                        last.then_inc(attT_ps, 1)
                    if c == 4 and real(b - 1):
                        pe.wait_ge(attT_sb, b)
                        for j in range(NB):
                            last = pe.matmul(ps_b[:, j * C:(j + 1) * C], attT[:, j * P:(j + 1) * P], w_proj[:, :],
                                             start=True, stop=True)
                        last.then_inc(proj_ps, 1)
                    if c == 6 and real(b + 2):
                        pe.wait_ge(norm_step, (b + 3) * NORM)
                        pe.wait_ge(kn_done, b + 3)
                        for n in range(2 * NB):
                            s, j = divmod(n, NB)
                            last = pe.transpose(ps_a[0][:, n * P:(n + 1) * P], qkn[p][:, j, s * C:(s + 1) * C], ident[:, :])
                        last.then_inc(qkT_ps, 1)
                    if c == 7 and real(b - 1):
                        pe.wait_ge(ln_step, b * LN)
                        for j in range(NB):
                            last = pe.transpose(ps_b[:, j * P:(j + 1) * P], x1[o][:, j, :], ident[:, :])
                        last.then_inc(x1T_ps, 1)
                    if c == 7 and real(b + 1):
                        at_least(pe, norm_step, (b + 3 if real(b + 2) else B) * NORM)
                        for j in range(NB):
                            last = pe.matmul(ps_a[1][:, j * C:(j + 1) * C], xT[o][:, j * P:(j + 1) * P],
                                             w_qkv[:, 2 * C:3 * C], start=True, stop=True)
                        last.then_inc(v_ps, 1)
                    if c == 0 and real(b - 1):
                        context(b - 1, o, CHUNKS - 1)
                    if c > 0 and real(b):
                        context(b, p, c - 1)

            pipelined(pe, step, 2, 2)

        @block.scalar
        def _(act):
            act.wait_ge(v_ones, 4)

            def step(b, hb, p):
                o = 1 - p
                for c in range(CHUNKS):
                    if real(b):
                        act.wait_ge(scores_ps, b * CHUNKS + c + 1)
                        at_least(act, pv_done, b * CHUNKS + c + 1 - RING)
                        act.activation(probs[c % RING][:, :], ps_s[c % 2][:, :], ACT.Exp, bias=k["minus_bound"][:, :],
                                       scale=SCALE).then_inc(probs_sb, 1)
                    if c == 0 and real(b + 2):
                        act.wait_ge(xT_ps, b + 3)
                        at_least(act, v_ps, b + 1)
                        act.activation(xT[p][:, :], ps_a[0][:, 0:N], ACT.Copy).then_inc(xT_sb, 1)
                    if c == 0 and real(b - 1):
                        act.wait_ge(pv_done, b * CHUNKS)
                        at_least(act, oT_ps, b - 1)
                        act.activation(o_sb[:, :], ps_o[:, :], ACT.Copy).then_inc(o_out, 1)
                    if c == 1 and real(b + 2):
                        act.wait_ge(qk_ps, b + 3)
                        if real(b + 1):
                            act.wait_ge(norm_step, (b + 1) * NORM + 1)
                        for j in range(NB):
                            act.activation(sq[:, j, :], ps_a[j][:, 0:2 * C], ACT.Square).then_inc(sq_sb, 1)
                    if c == 2 and real(b - 2):
                        act.wait_ge(gate_step, (b - 2) * GATE + 3)
                        if real(b - 3):
                            act.wait_ge(rank_step, (b - 2) * RANK)
                        act.activation(ex[:, :, :], below[:, :, :], ACT.Exp).then_inc(exp_sb, 1)
                    if c == 3 and real(b - 1):
                        act.wait_ge(attT_ps, b)
                        at_least(act, proj_ps, b - 1)
                        act.activation(attT[:, :], ps_b[:, 0:N], ACT.Copy).then_inc(attT_sb, 1)
                    if c == 6 and real(b + 2):
                        act.wait_ge(qkT_ps, b + 3)
                        at_least(act, parts_out, (b + 1) * 16)
                        act.activation(parts[p][:, 0, :], ps_a[0][:, :], ACT.Copy).then_inc(hi_sb, 1)
                    if c == 7 and real(b - 1):
                        act.wait_ge(x1T_ps, b)
                        at_least(act, logit_ps, b - 1)
                        act.activation(x1T[:, :], ps_b[:, 0:N], ACT.Copy).then_inc(x1T_sb, 1)
                    if c == 7 and real(b + 1):
                        act.wait_ge(v_ps, b + 2)
                        at_least(act, pv_done, b * CHUNKS)
                        for j in range(NB):
                            dst = vpad[o][:, j, :].rearrange("p (q g w) -> p q g w", q=QUADS, w=VW)
                            act.activation(dst[:, :, 0:8:2, 0:HD],
                                           ps_a[1][:, j * C:(j + 1) * C].rearrange("p (q g w) -> p q g w", q=QUADS, w=HD),
                                           ACT.Copy).then_inc(v_sb, 1)

            pipelined(act, step, 2, 2, first=3)

        @block.vector
        def _(dve):
            for i in two:
                dve.memset(q_st[i][:, :, :].bitcast(FP32), 0.0).then_inc(cleared, 1)
            dve.memset(k_st[0][:, :, :].bitcast(FP32), 0.0).then_inc(cleared, 1)
            norm, split, attn = Steps(dve, norm_step, NORM), Steps(dve, split_step, SPLIT), Steps(dve, att_step, ATT)
            ln, gate, route = Steps(dve, ln_step, LN), Steps(dve, gate_step, GATE), Steps(dve, rank_step, RANK)
            over = lambda a, n: a.unsqueeze(2).broadcast_to([P, a.shape[1], n])
            each = lambda a: a.unsqueeze(1).broadcast_to([P, NB, a.shape[1]])

            def gates(b):
                s = gate.batch(b)
                dve.wait_ge(logit_ps, b + 1)
                s.did(dve.tensor_copy(lg[:, :, :], ps_b[:, 0:NB * E].rearrange("p (j e) -> p j e", j=NB)))
                s.wait()
                s.did(dve.tensor_reduce(top[:, :], lg[:, :, :], AX.X, ALU.max))
                s.wait()
                at_least(dve, exp_sb, b)
                s.did(dve.tensor_tensor(below[:, :, :], lg[:, :, :], over(top[:, :], E), ALU.subtract))
                s.wait()
                s.did(dve.scalar_tensor_tensor(cand[:, :, :], below[:, :, :], 0.0, each(k["backwards"][:, :]),
                                               ALU.is_ge, ALU.mult))
                s.wait()
                s.did(dve.tensor_reduce(first[:, :], cand[:, :, :], AX.X, ALU.max))
                s.wait()
                s.did(dve.tensor_tensor(hot[:, :, :], cand[:, :, :], over(first[:, :], E), ALU.is_equal))
                s.wait()
                at_least(dve, rank_ps, b)
                s.did(dve.tensor_copy(hot_bf[:, :, :], hot[:, :, :]))
                s.end()

            def routes(b, hb, p):
                s = route.batch(b)
                before, dump = k["slots_before"], k["dump"]
                dve.wait_ge(rank_ps, b + 1)
                s.did(dve.tensor_tensor(rank[:, :, :], ps_b[:, 2 * E:4 * E].rearrange("p (j e) -> p j e", j=NB),
                                        each(before[:, :]), ALU.add))
                s.wait()
                s.did(dve.tensor_tensor(before[:, :], ps_b[:, 4 * E:5 * E], before[:, :], ALU.add))
                s.wait()
                s.did(dve.tensor_tensor(picked[:, :, :], hot[:, :, :], rank[:, :, :], ALU.mult))
                s.wait()
                s.did(dve.tensor_reduce(slot[:, :], picked[:, :, :], AX.X, ALU.add))
                s.wait()
                s.did(dve.tensor_tensor(picked[:, :, :], hot[:, :, :], each(k["slots_end"][:, :]), ALU.mult))
                s.wait()
                s.did(dve.tensor_reduce(limit[:, :], picked[:, :, :], AX.X, ALU.add))
                s.wait()
                s.did(dve.tensor_tensor(keep[:, :], limit[:, :], slot[:, :], ALU.is_gt))
                s.wait()
                s.did(dve.tensor_tensor(kept_slot[:, :], slot[:, :], keep[:, :], ALU.mult))
                s.did(dve.tensor_scalar(spare[:, :], keep[:, :], -1.0, 1.0, ALU.mult, ALU.add))
                s.wait()
                cols = slice(b * NB, (b + 1) * NB) if isinstance(b, int) else bass.ds(b * NB, NB)
                s.did(dve.tensor_copy(k["fetch"][:, cols], kept_slot[:, :]))
                s.did(dve.tensor_tensor(spare[:, :], spare[:, :], dump[:, :], ALU.mult))
                s.wait()
                at_least(dve, sent[p], 16 * NB * hb)
                s.did(dve.tensor_tensor(sidx[p][:, :], kept_slot[:, :], spare[:, :], ALU.add))
                s.did(dve.tensor_scalar(dump[:, :], dump[:, :], float(N), None, ALU.add))
                dve.wait_ge(exp_sb, b + 1)
                s.did(dve.tensor_reduce(esum[:, :], ex[:, :, :], AX.X, ALU.add))
                s.wait()
                s.did(dve.reciprocal(prob[:, :], esum[:, :]))
                s.wait()
                s.did(dve.tensor_tensor(k["weight"][:, cols], prob[:, :], keep[:, :], ALU.mult))
                s.end()

            def step(b, hb, p):
                o = 1 - p
                if real(b - 2):
                    gates(b - 2)
                    routes(b - 2, hb - 1, p)
                if real(b - 1):
                    s = attn.batch(b - 1)
                    dve.wait_ge(oT_ps, b)
                    ctxs = ps_b[:, :].rearrange("p (n w) -> p n w", w=VW)
                    s.did(dve.reciprocal(rden[:, :], ctxs[:, :, HD]))
                    s.wait()
                    at_least(dve, attT_ps, b - 1)
                    s.did(dve.tensor_tensor(att[:, :].rearrange("p (n w) -> p n w", w=HD), ctxs[:, :, 0:HD],
                                            over(rden[:, :], HD), ALU.mult))
                    s.end()
                if real(b + 2):
                    s = norm.batch(b + 2)
                    dve.wait_ge(sq_sb, (b + 3) * NB)
                    s.did(dve.tensor_reduce(ms[:, :], sq[:, :, :].rearrange("p j (n w) -> p (j n) w", w=HD), AX.X, ALU.add))
                    s.wait()
                    s.did(dve.tensor_scalar(ms[:, :], ms[:, :], 1.0 / HD, 1e-30, ALU.mult, ALU.max))
                    s.wait()
                    newton_rsqrt(dve, s, ms[:, :], nr_y[:, :], nr_t[:, :])
                    s.wait()
                    s.did(dve.tensor_tensor(rms[:, :], ms[:, :], nr_y[:, :], ALU.mult))
                    s.wait()
                    s.did(dve.tensor_scalar(rms[:, :], rms[:, :], EPS_RMS, None, ALU.add))
                    s.wait()
                    s.did(dve.reciprocal(nr_t[:, :], rms[:, :]))
                    s.wait()
                    at_least(dve, qkT_ps, b + 1)
                    for j in range(NB):
                        scale = nr_t[:, 2 * H * j:2 * H * (j + 1)].rearrange("p (s h) -> p s h", h=H)
                        s.did(dve.tensor_tensor(qkn[p][:, j, :].rearrange("p (s w h) -> p s h w", s=2, h=H),
                                                ps_a[j][:, 0:2 * C].rearrange("p (s h w) -> p s h w", s=2, w=HD),
                                                scale.unsqueeze(3).broadcast_to([P, 2, H, HD]), ALU.mult))
                    s.end()
                if real(b - 1):
                    s = ln.batch(b - 1)
                    dve.wait_ge(proj_ps, b)
                    dve.wait_ge(xr_step, b)
                    s.did(dve.tensor_tensor(y[:, :, :], ps_b[:, 0:NB * C].rearrange("p (j c) -> p j c", j=NB),
                                            xr[o][:, :, :], ALU.add))
                    s.wait()
                    for j in range(NB):
                        s.did(dve.bn_stats(stats[:, j, :], y[:, j, :]))
                    wait_apart(dve, k, (s.sem, s.base + s.n),
                                       (pow_step, (b - 1) * POW))
                    for j in range(NB):
                        s.did(dve.bn_aggr(mv[:, j, :], stats[:, j, :]))
                    s.wait()
                    dve.wait_ge(pow_step, b * POW)
                    at_least(dve, x1_out[o], 16 * (hb - 1 + p))
                    at_least(dve, sent[o], 16 * NB * (hb - 1 + p))
                    at_least(dve, x1T_ps, b - 2)
                    for j in range(NB):
                        s.did(dve.tensor_scalar(x1[o][:, j, :], y[:, j, :], mv[:, j, 0:1], rstd[:, j:j + 1],
                                                ALU.subtract, ALU.mult))
                    s.end()
                if real(b + 2):
                    s = split.batch(b + 2)
                    dve.wait_ge(hi_sb, b + 3)
                    at_least(dve, lo_sb, b + 2)
                    s.did(dve.tensor_tensor(rest[:, :], ps_a[0][:, :], parts[p][:, 0, :], ALU.subtract))
                    s.wait()
                    s.did(dve.tensor_copy(parts[p][:, 1, :], rest[:, :]))
                    s.end()

            pipelined(dve, step, 2, 2, first=3)

        @block.gpsimd
        def _(pool):
            pool.memset(k_st[1][:, :, :].bitcast(FP32), 0.0).then_inc(cleared, 1)
            for i in two:
                pool.memset(vpad[i][:, :, :], 0.0).then_inc(v_ones, 1)
            pool.wait_ge(v_ones, 2)
            for i in two:
                ones = vpad[i][:, :, :].rearrange("p j (q g w) -> p (j q) g w", q=QUADS, w=VW)[:, :, 0:8:2, HD]
                pool.memset(ones, 1.0).then_inc(v_ones, 1)
            pool.wait_ge(w_in, W_IN)

            def step(b, hb, p):
                o = 1 - p
                if real(b):
                    pool.wait_ge(xr_in[p], (hb + 1) * 16)
                    pool.tensor_tensor(xr[p][:, :, :], xr[p][:, :, :],
                                       b_proj[:, :].unsqueeze(1).broadcast_to([P, NB, C]), ALU.add).then_inc(xr_step, 1)
                if real(b - 2):
                    if isinstance(b, int) and b == 2:
                        pool.wait_ge(disp_zero, 16 * (SLOTS // (5 * P)))
                    wait_apart(pool, k, (rank_step, (b - 1) * RANK))
                    for j in range(NB):
                        pool.indirect_dma_start(out=disp_d, out_offset=bass.IndirectOffsetOnAxis(ap=sidx[p][:, j:j + 1], axis=0),
                                                in_=x1[p][:, j, :], in_offset=None).then_inc(sent[p], 16)
                if real(b + 2):
                    pool.wait_ge(norm_step, (b + 3) * NORM)
                    kn = qkn[p][:, :, C:2 * C].rearrange("p j (w h) -> p j w h", h=H)
                    for j in range(NB):
                        ins = pool.tensor_tensor(kn[:, j], kn[:, j], k["qks"][:, :].unsqueeze(2).broadcast_to([P, HD, H]), ALU.mult)
                    ins.then_inc(kn_done, 1)
                if real(b - 1):
                    wait_apart(pool, k, (ln_step, (b - 1) * LN + STATS))
                    pool.tensor_scalar(veps[:, :], mv[:, :, 1], EPS_LN, None, ALU.add).then_inc(pow_step, 1)
                    pool.wait_ge(pow_step, (b - 1) * POW + 1)
                    pool.tensor_tensor(rstd[:, :], veps[:, :], k["minus_half"][:, 0:NB], ALU.pow).then_inc(pow_step, 1)
                if real(b + 2):
                    pool.wait_ge(split_step, (b + 3) * SPLIT)
                    pool.tensor_tensor(parts[p][:, 2, :], rest[:, :], parts[p][:, 1, :], ALU.subtract).then_inc(lo_sb, 1)

            pipelined(pool, step, 2, 2)
            for i in two:
                pool.wait_ge(sent[i], 16 * NB * B // 2)


def experts(nc, k, w1, w2, disp_d, eout_d):
    TILES = [(t, min(P, CAP - t)) for t in range(0, CAP, P)]
    FULL = CAP // P
    with ExitStack() as ctx:
        sb = lambda name, shape, dt: ctx.enter_context(nc.sbuf_tensor("ex_" + name, shape, dt))
        pb = lambda name, shape, dt: ctx.enter_context(nc.psum_tensor("ex_" + name, shape, dt))
        sem = lambda name: ctx.enter_context(nc.semaphore("ex_" + name))
        two = range(2)
        xe = [sb(f"xe{i}", [P, len(TILES), C], FP32) for i in two]
        xeT = [sb(f"xeT{i}", [P, CAP], FP32) for i in two]
        hT = [sb(f"hT{i}", [P, FC, CAP], FP32) for i in two]
        ye = [sb(f"ye{i}", [P, len(TILES), C], FP32) for i in two]
        ps_x = pb("ps_x", [P, 512], FP32)
        ps_h = [pb(f"ps_h{i}", [P, FC // 2, 512], FP32) for i in two]
        ps_y = [pb(f"ps_y{i}", [P, 512], FP32) for i in two]
        xe_in, ye_out = [sem(f"xe_in{i}") for i in two], [sem(f"ye_out{i}") for i in two]
        xeT_ps, xeT_sb, h_ps, h_sb, y_ps, y_sb = (sem(n) for n in ("xeT_ps", "xeT_sb", "h_ps", "h_sb", "y_ps", "y_sb"))
        block = ctx.enter_context(nc.Block())
        w1_sb, w2_sb, w_in = k["w1"], k["w2"], k["w_in"]
        W = len(w1_sb)
        real = lambda e: not isinstance(e, int) or 0 <= e < E

        def expert(dram, e):
            return dram[e] if isinstance(e, int) else dram[bass.ds(e, 1)].rearrange("a b c -> (a b) c")

        def tiles(dram, e, sbuf):
            r = dram[e * CAP:(e + 1) * CAP, :] if isinstance(e, int) else dram[bass.ds(e * CAP, CAP), :]
            yield r[0:FULL * P, :].rearrange("(t p) c -> p t c", p=P), sbuf[:, 0:FULL, :]
            if CAP % P:
                yield r[FULL * P:CAP, :], sbuf[0:CAP % P, FULL, :]

        LOADS = 16 * len(list(tiles(disp_d, 0, xe[0])))
        ye_parts = [(slice(0, P), slice(0, FULL))] + ([(slice(0, CAP % P), slice(FULL, FULL + 1))] if CAP % P else [])

        @block.sync
        def _(sp):
            def step(e, he, q):
                p = q % 2
                if real(e + 3):
                    wait_apart(sp, k, (xeT_ps, e + 2))
                    for dram, sbuf in tiles(disp_d, e + 3, xe[1 - p]):
                        sp.dma_start(sbuf, dram).then_inc(xe_in[1 - p], 16)
                if real(e):
                    wait_apart(sp, k, (y_sb, (e + 1) * len(ye_parts)))
                    for dram, sbuf in tiles(eout_d, e, ye[p]):
                        sp.dma_start(dram, sbuf).then_inc(ye_out[p], 16)
                if real(e) and real(e + W):
                    wait_apart(sp, k, (y_ps, e + 1))
                    sp.dma_start(w1_sb[q][:, :], expert(w1, e + W)).then_inc(w_in[q], 16)
                    sp.dma_start(w2_sb[q][:, :, :], expert(w2, e + W).rearrange("(f p) c -> p f c", p=P)).then_inc(w_in[q], 16)

            pipelined(sp, step, 3, 0, E, W)
            for i in two:
                sp.wait_ge(ye_out[i], LOADS * E // 2)

        @block.tensor
        def _(pe):
            def step(e, he, q):
                p, o = q % 2, 1 - q % 2
                half = lambda d: (he * W + q + d) // 2 if isinstance(he, int) else he * (W // 2) + (q + d) // 2
                if real(e + 1):
                    qn = (q + 1) % W
                    pe.wait_ge(w_in[qn], ((he + (q + 1) // W) + 1) * 32)
                    pe.wait_ge(xeT_sb, e + 2)
                    for f in range(FC):
                        if f % 2 == 0:
                            at_least(pe, h_sb, (e + 1) * 2 - 1 + f // 2)
                        last = pe.matmul(ps_h[f // 2][:, f % 2, 0:CAP], w1_sb[qn][:, f * P:(f + 1) * P], xeT[o][:, :],
                                         start=True, stop=True)
                        if f % 2:
                            last.then_inc(h_ps, 1)
                if real(e + 2):
                    pe.wait_ge(xe_in[p], (half(2) + 1) * LOADS)
                    at_least(pe, xeT_sb, e + 2)
                    for t, n in TILES:
                        last = pe.transpose(ps_x[:, t:t + n], xe[p][0:n, t // P, :], k["ident"][0:n, 0:n])
                    last.then_inc(xeT_ps, 1)
                if real(e):
                    pe.wait_ge(h_sb, (e + 1) * 2)
                    at_least(pe, y_sb, (e - 1) * len(ye_parts))
                    for t, n in TILES:
                        for f in range(FC):
                            last = pe.matmul(ps_y[p][0:n, t // P * C:(t // P + 1) * C], hT[p][:, f, t:t + n],
                                             w2_sb[q][:, f, :], start=f == 0, stop=f == FC - 1)
                    last.then_inc(y_ps, 1)

            pipelined(pe, step, 2, 0, E, W, first=2)

        @block.scalar
        def _(act):
            def step(e, he, q):
                o = 1 - q % 2
                if real(e + 1):
                    for i in two:
                        act.wait_ge(h_ps, (e + 1) * 2 + i + 1)
                        at_least(act, y_ps, e)
                        act.activation(hT[o][:, 2 * i:2 * i + 2, :], ps_h[i][:, :, 0:CAP], ACT.Gelu_apprx_tanh).then_inc(h_sb, 1)

            pipelined(act, step, 2, 0, E, W, first=1)

        @block.vector
        def _(dve):
            def step(e, he, q):
                p = q % 2
                half = lambda d: (he * W + q + d) // 2 if isinstance(he, int) else he * (W // 2) + (q + d) // 2
                if real(e + 2):
                    dve.wait_ge(xeT_ps, e + 3)
                    at_least(dve, h_ps, (e + 1) * 2)
                    dve.tensor_copy(xeT[p][:, :], ps_x[:, 0:CAP]).then_inc(xeT_sb, 1)
                if real(e):
                    dve.wait_ge(y_ps, e + 1)
                    at_least(dve, ye_out[p], LOADS * half(0))
                    for r, c in ye_parts:
                        dve.tensor_copy(ye[p][r, c, :], ps_y[p][r, c.start * C:c.stop * C].rearrange("p (t c) -> p t c", c=C))\
                           .then_inc(y_sb, 1)

            pipelined(dve, step, 2, 0, E, W, first=2)


def l1_layer(nc, k, Wq, Wk, Wv, Wo, parts_d, rden_d, x1_d, eout_d, x2_d):
    DV = 64
    PAIRS = H // 2
    STACKS = STACK_LOADS + 1

    with ExitStack() as ctx:
        sb = lambda name, shape, dt: ctx.enter_context(nc.sbuf_tensor("l1_" + name, shape, dt))
        pb = lambda name, shape, dt: ctx.enter_context(nc.psum_tensor("l1_" + name, shape, dt))
        sem = lambda name: ctx.enter_context(nc.semaphore("l1_" + name))
        two = range(2)
        w_qk_in = sb("w_qk_in", [P, 2 * C], FP32)
        w_qk = sb("w_qk", [P, 2 * C], FP32)
        w_v = sb("w_v", [P, H * DV], FP32)
        w_o = sb("w_o", [P, PAIRS, C], FP32)
        sums = sb("sums", [P, QUADS, 32], FP32)
        index = sb("index", [P, NB], U32)
        eg = [sb(f"eg{i}", [P, NB, C], FP32) for i in two]
        xa = [sb(f"xa{i}", [P, NB, C], FP32) for i in two]
        y2 = sb("y2", [P, NB, C], FP32)
        x2 = [sb(f"x2_{i}", [P, NB, C], FP32) for i in two]
        xT = [sb(f"xT{i}", [P, N], FP32) for i in two]
        stats2, stats3 = sb("stats2", [P, NB, 6], FP32), sb("stats3", [P, NB, 6], FP32)
        mv2, mv3 = sb("mv2", [P, NB, 2], FP32), sb("mv3", [P, NB, 2], FP32)
        veps2, veps3 = sb("veps2", [P, NB], FP32), sb("veps3", [P, NB], FP32)
        rstd2, rstd3 = sb("rstd2", [P, NB], FP32), sb("rstd3", [P, NB], FP32)
        parts = [sb(f"parts{i}", [P, 3, 2 * N], BF16) for i in two]
        rest = sb("rest", [P, 2 * N], FP32)
        q_st = [sb(f"q_st{i}", [P, H, N], BF16) for i in two]
        k_st = [sb(f"k_st{i}", [P, H, N], BF16) for i in two]
        values = [sb(f"values{i}", [P, NB, H * DV], FP32) for i in two]
        neg_max = sb("neg_max", [P, NB, H], BF16)
        max_rows = [sb(f"max_rows{i}", [H // 2, N], BF16) for i in two]
        p0 = [sb(f"p0_{i}", [P, 4, N], FP32) for i in two]
        p1 = [sb(f"p1_{i}", [P, 4, P], FP32) for i in two]
        ctxs = [sb(f"ctx{i}", [P, PAIRS, N], FP32) for i in two]
        rden = sb("rden", [P, N], FP32)
        rrep = sb("rrep", [P, PAIRS, N], FP32)
        xr = [sb(f"xr{i}", [P, NB, C], FP32) for i in two]
        y3 = sb("y3", [P, NB, C], FP32)
        st0 = pb("st0", [P, 4, N], FP32)
        st1 = pb("st1", [P, 4, P], FP32)
        sm1 = pb("sm1", [P, 4, N], FP32)
        sm0 = pb("sm0", [P, 4, P], FP32)
        ps_c = pb("ps_c", [P, 2, N], FP32)
        ps_d = pb("ps_d", [P, 512], FP32)

        w_in, w_turned, ready, sums_set = sem("w_in"), sem("w_turned"), sem("ready"), sem("sums_set")
        index_set, fetched, xa_in = sem("index_set"), [sem(f"fetched{i}") for i in two], [sem(f"xa_in{i}") for i in two]
        x2_step, pow2, pow3, x3_step = (sem(n) for n in ("x2_step", "pow2", "pow3", "x3_step"))
        x2_out = [sem(f"x2_out{i}") for i in two]
        xr_in = [sem(f"xr_in{i}") for i in two]
        xT_ps, xT_sb, qk_ps, hi_sb, split_step, lo_sb = (sem(n) for n in ("xT_ps", "xT_sb", "qk_ps", "hi_sb", "split_step", "lo_sb"))
        parts_out, stacks_in, v_ps, v_sb = (sem(n) for n in ("parts_out", "stacks_in", "v_ps", "v_sb"))
        sm_ps, max_done, rows_ps, rows_sb = (sem(n) for n in ("sm_ps", "max_done", "rows_ps", "rows_sb"))
        rows_in = [sem(f"rows_in{i}") for i in two]
        st_ps, p_sb, masked, ctx_ps, ctx_sb = (sem(n) for n in ("st_ps", "p_sb", "masked", "ctx_ps", "ctx_sb"))
        rden_sb, rden_out, rrep_in, divided, wo_ps = (sem(n) for n in ("rden_sb", "rden_out", "rrep_in", "divided", "wo_ps"))
        block = ctx.enter_context(nc.Block())
        turned = lambda bank: bank[0:H // 2, :, :].rearrange("p a b -> p (a b)").bitcast(BF16)[:, 0:N]
        X2, X3, SPLIT, POW, V_OUT = 4 * NB, 1 + 3 * NB, 2, 2, 2 * NB
        W_IN = 16 * 4

        def rows(dram, b):
            r = dram[b * N:(b + 1) * N, :] if isinstance(b, int) else dram[bass.ds(b * N, N), :]
            return r.rearrange("(j p) c -> p j c", p=P)

        @block.sync
        def _(sp):
            sp.dma_start(w_qk_in[:, 0:C], Wq).then_inc(w_in, 16)
            sp.dma_start(w_qk_in[:, C:2 * C], Wk).then_inc(w_in, 16)
            sp.dma_start(w_v[:, :], Wv).then_inc(w_in, 16)
            sp.dma_start(w_o[:, :, :], Wo.rearrange("(i p) c -> p i c", p=P)).then_inc(w_in, 16)
            sp.wait_ge(ready, 4)

            def step(b, hb, p):
                o = 1 - p
                if real(b + 1):
                    sp.wait_ge(lo_sb, b + 2)
                    sp.dma_start(parts_d.rearrange("t p n -> p t n"), parts[o][:, :, :]).then_inc(parts_out, 16)
                    wait_apart(sp, k, (parts_out, (b + 2) * 16),
                                      (st_ps, b * 2 * QUADS))
                    sp.dma_start(q_st[o][SHIFT_ROW:SHIFT_ROW + 1, :, :],
                                 k["zeros"][0:H, 0:N // 2].bitcast(BF16)).then_inc(stacks_in, 16)
                    load_stacks(sp, parts_d, q_st[o], k_st[o], stacks_in)
                    wait_apart(sp, k, (stacks_in, (b + 2) * 16 * STACKS))
                if real(b + 2):
                    wait_apart(sp, k, (x2_step, (b + 3) * X2))
                    sp.dma_start(rows(x2_d, b + 2), x2[p][:, :, :]).then_inc(x2_out[p], 16)
                if real(b):
                    wait_apart(sp, k, (x2_out[p], (hb + 1) * 16),
                                      (x3_step, (b - 2) * X3 + 1))
                    sp.dma_start(xr[p][:, :, :], rows(x2_d, b)).then_inc(xr_in[p], 16)
                if real(b + 3):
                    wait_apart(sp, k, (x2_step, (b + 1) * X2 + NB))
                    sp.dma_start(xa[o][:, :, :], rows(x1_d, b + 3)).then_inc(xa_in[o], 16)
                if real(b):
                    sp.wait_ge(rden_sb, b + 1)
                    sp.dma_start(rden_d, rden[:, :]).then_inc(rden_out, 16)
                    wait_apart(sp, k, (rden_out, (b + 1) * 16),
                                      (divided, b * QUADS))
                    src = rden_d.rearrange("(i u r) n -> u r i n", i=2, u=2)
                    for u in two:
                        for i in two:
                            sp.dma_start(rrep[u * DV:(u + 1) * DV, i:PAIRS:2, :],
                                         src[u, 0:QUADS, i, :].unsqueeze(0).broadcast_to([DV, QUADS, N])).then_inc(rrep_in, 16)

            pipelined(sp, step, 3, 1, first=2)
            for i in two:
                sp.wait_ge(x2_out[i], 16 * B // 2)

        @block.tensor
        def _(pe):
            ident, ident_bf = k["ident"], k["ident_bf"]
            pe.wait_ge(w_in, W_IN)
            pe.wait_ge(ready, 4)
            pe.wait_ge(sums_set, 1 + QUADS)
            pe.wait_ge(w_turned, 1)

            def values_of(b, p, n0):
                pe.wait_ge(max_done, (b + 1) * 2 * QUADS - 1)
                for n in (n0, n0 + 1):
                    j, half = divmod(n, 2)
                    if n >= 2:
                        pe.wait_ge(v_sb, b * V_OUT + n - 1)
                    pe.matmul(sm1[:, 2 * half:2 * half + 2, :], xT[p][:, j * P:(j + 1) * P],
                              w_v[:, half * 512:(half + 1) * 512], start=True, stop=True).then_inc(v_ps, 1)

            def scores_by_key(b, p, j):
                if j % 2 == 0:
                    pe.wait_ge(rows_in[j // 2], (b + 1) * 16)
                if j == 0:
                    at_least(pe, xT_sb, b + 2 if real(b + 1) else B)
                    at_least(pe, split_step, (b + 1) * SPLIT + 1 if real(b + 1) else B * SPLIT)
                else:
                    pe.wait_ge(p_sb, (b * QUADS + j) * 2)
                for g in range(4):
                    h = 4 * j + g
                    last = pe.matmul(st0[:, g, :], k_st[p][:, h, 0:P], q_st[p][:, h, :], start=True, stop=True)
                last.then_inc(st_ps, 1)
                for g in range(4):
                    h = 4 * j + g
                    last = pe.matmul(st1[:, g, :], k_st[p][:, h, P:N], q_st[p][:, h, P:N], start=True, stop=True)
                last.then_inc(st_ps, 1)

            def scores_by_query(b, p, j):
                if j == 0:
                    pe.wait_ge(stacks_in, (b + 1) * 16 * STACKS)
                    at_least(pe, v_sb, b * V_OUT)
                    at_least(pe, rows_sb, b * 2)
                    at_least(pe, x3_step, (b - 2) * X3 + 1)
                else:
                    pe.wait_ge(max_done, (b * QUADS + j) * 2)
                for half in two:
                    pe.matmul(sm1[:, 2 * half:2 * half + 2, P:N], ident_bf[:, :],
                              k["causal"][:, 0:2 * P].rearrange("p (a b) -> p a b", b=P),
                              start=True, stop=False, skip_group_check=True)
                    for g in (2 * half, 2 * half + 1):
                        last = pe.matmul(sm1[:, g, :], q_st[p][:, 4 * j + g, P:N], k_st[p][:, 4 * j + g, :],
                                         start=False, stop=g % 2 == 1, skip_group_check=True)
                last.then_inc(sm_ps, 1)
                pe.matmul(sm0[:, :, :], ident_bf[:, :], k["causal"][:, :].rearrange("p (a b) -> p a b", b=P),
                          start=True, stop=False, skip_group_check=True)
                for g in range(4):
                    last = pe.matmul(sm0[:, g, :], q_st[p][:, 4 * j + g, 0:P], k_st[p][:, 4 * j + g, 0:P],
                                     start=False, stop=g == 3, skip_group_check=True)
                last.then_inc(sm_ps, 1)

            def maxima_by_head(b, half, bank):
                pe.wait_ge(max_done, (b * 2 + half + 1) * QUADS)
                for j in range(NB):
                    last = pe.transpose(turned(bank)[:, j * P:(j + 1) * P], neg_max[:, j, half * H // 2:(half + 1) * H // 2],
                                        ident_bf[:, :])
                last.then_inc(rows_ps, 1)

            def project(b, o, j):
                if j == 0:
                    pe.wait_ge(divided, b * QUADS)
                    if real(b):
                        pe.wait_ge(rows_sb, (b + 1) * 2)
                for i in range(PAIRS):
                    last = pe.matmul(sm0[:, j, :], ctxs[o][:, i, j * P:(j + 1) * P], w_o[:, i, :],
                                     start=i == 0, stop=i == PAIRS - 1)
                if j == NB - 1:
                    last.then_inc(wo_ps, 1)

            def context(b, p, j):
                pe.wait_ge(masked, (b * QUADS + j + 1) * 2)
                if j == 0:
                    pe.wait_ge(v_sb, (b + 1) * V_OUT)
                at_least(pe, ctx_sb, b * QUADS + j)
                for i in two:
                    for kb, pr, q0 in ((0, p0[j % 2], 0), (1, p1[j % 2], P)):
                        for u in two:
                            h = 4 * j + 2 * i + u
                            last = pe.matmul(ps_c[u * DV:(u + 1) * DV, i, q0:N], values[p][:, kb, h * DV:(h + 1) * DV],
                                             pr[:, 2 * i + u, :], start=kb == 0, stop=kb == 1)
                if j == 0:
                    at_least(pe, rden_sb, b)
                for kb, pr, q0 in ((0, p0[j % 2], 0), (1, p1[j % 2], P)):
                    for g in range(4):
                        last = pe.matmul(ps_d[32 * g:32 * g + 32, q0:N], sums[:, j, :], pr[:, g, :],
                                         start=j == 0 and kb == 0, stop=j == QUADS - 1 and kb == 1)
                last.then_inc(ctx_ps, 1)

            def step(b, hb, p):
                o = 1 - p
                if real(b):
                    scores_by_key(b, p, 1)
                if real(b - 1):
                    project(b, o, 0)
                if real(b):
                    context(b, p, 0)
                    scores_by_key(b, p, 2)
                if real(b - 1):
                    project(b, o, 1)
                if real(b):
                    context(b, p, 1)
                    scores_by_key(b, p, 3)
                if real(b + 1):
                    scores_by_query(b + 1, o, 0)
                if real(b):
                    context(b, p, 2)
                if real(b + 1):
                    scores_by_query(b + 1, o, 1)
                if real(b):
                    context(b, p, 3)
                if real(b + 1):
                    at_least(pe, p_sb, (b + 1) * 2 * QUADS)
                    maxima_by_head(b + 1, 0, st1)
                    scores_by_query(b + 1, o, 2)
                if real(b + 2):
                    pe.wait_ge(x2_step, (b + 3) * X2)
                    at_least(pe, p_sb, (b + 1) * 2 * QUADS)
                    if real(b + 1):
                        pe.wait_ge(rows_sb, b * 2 + 3)
                    for j in range(NB):
                        last = pe.transpose(st1[:, j, :], x2[p][:, j, :], ident[:, :])
                    last.then_inc(xT_ps, 1)
                    pe.wait_ge(xT_sb, b + 3)
                    at_least(pe, split_step, (b + 2) * SPLIT)
                    for s in two:
                        last = pe.matmul(st0[:, 2 + s, :], w_qk[:, s * C:(s + 1) * C], xT[p][:, :], start=True, stop=True)
                    last.then_inc(qk_ps, 1)
                if real(b + 1):
                    scores_by_query(b + 1, o, 3)
                    values_of(b + 1, o, 0)
                    maxima_by_head(b + 1, 1, sm0)
                    scores_by_key(b + 1, o, 0)
                    values_of(b + 1, o, 2)

            pipelined(pe, step, 3, 1, first=2)

        @block.scalar
        def _(act):
            def exponentials(b, j):
                at_least(act, ctx_ps, b * QUADS + j - 1)
                act.wait_ge(st_ps, (b * QUADS + j) * 2 + 1)
                act.activation(p0[j % 2][:, :, :], st0[:, :, :], ACT.Exp, scale=SCALE).then_inc(p_sb, 1)
                act.wait_ge(st_ps, (b * QUADS + j) * 2 + 2)
                act.activation(p1[j % 2][:, :, :], st1[:, :, :], ACT.Exp, scale=SCALE).then_inc(p_sb, 1)

            def maxima_out(b, p, half, bank):
                act.wait_ge(rows_ps, b * 2 + half + 1)
                at_least(act, rows_in[half], b * 16)
                act.activation(max_rows[half][:, :], turned(bank), ACT.Copy).then_inc(rows_sb, 1)
                act.wait_ge(rows_sb, b * 2 + half + 1)
                heads = slice(half * H // 2, (half + 1) * H // 2)
                act.dma_start(q_st[p][SHIFT_ROW:SHIFT_ROW + 1, heads, :], max_rows[half][:, :]).then_inc(rows_in[half], 16)

            def values_out(b, p, n0):
                for n in (n0, n0 + 1):
                    j, half = divmod(n, 2)
                    act.wait_ge(v_ps, b * V_OUT + n + 1)
                    act.activation(values[p][:, j, half * 512:(half + 1) * 512],
                                   sm1[:, 2 * half:2 * half + 2, :].rearrange("p a b -> p (a b)"), ACT.Copy).then_inc(v_sb, 1)

            def context_out(b, p, j):
                act.wait_ge(ctx_ps, b * QUADS + j + 1)
                at_least(act, wo_ps, b - 1)
                act.activation(ctxs[p][:, 2 * j:2 * j + 2, :], ps_c[:, :, :], ACT.Copy).then_inc(ctx_sb, 1)

            def step(b, hb, p):
                o = 1 - p
                if real(b):
                    exponentials(b, 1)
                    context_out(b, p, 0)
                    exponentials(b, 2)
                    context_out(b, p, 1)
                    exponentials(b, 3)
                    context_out(b, p, 2)
                    context_out(b, p, 3)
                if real(b + 1):
                    maxima_out(b + 1, o, 0, st1)
                if real(b + 2):
                    act.wait_ge(xT_ps, b + 3)
                    at_least(act, v_ps, (b + 1) * V_OUT)
                    act.activation(xT[p][:, :], st1[:, 0:NB, :].rearrange("p a b -> p (a b)"), ACT.Copy).then_inc(xT_sb, 1)
                    act.wait_ge(qk_ps, b + 3)
                    at_least(act, parts_out, (b + 1) * 16)
                    act.activation(parts[p][:, 0, :], st0[:, 2:4, :].rearrange("p a b -> p (a b)"), ACT.Copy).then_inc(hi_sb, 1)
                if real(b + 1):
                    at_least(act, ctx_ps, b * QUADS)
                    values_out(b + 1, o, 0)
                    maxima_out(b + 1, o, 1, sm0)
                    exponentials(b + 1, 0)
                    values_out(b + 1, o, 2)

            pipelined(act, step, 3, 1, first=2)

        @block.vector
        def _(dve):
            for i in two:
                dve.memset(q_st[i][:, :, :].bitcast(FP32), 0.0).then_inc(ready, 1)
            dve.wait_ge(w_in, W_IN)
            dve.tensor_copy(w_qk[:, :].rearrange("p (s c h) -> p s c h", s=2, h=H),
                            w_qk_in[:, :].rearrange("p (s h c) -> p s c h", s=2, c=HD)).then_inc(w_turned, 1)
            added, layer3, split = Steps(dve, x2_step, X2), Steps(dve, x3_step, X3), Steps(dve, split_step, SPLIT)

            def normalise(s, y, stats, mv, rstd, pow_sem, b, out, free):
                s.wait()
                for j in range(NB):
                    s.did(dve.bn_stats(stats[:, j, :], y[:, j, :]))
                wait_apart(dve, k, (s.sem, s.base + s.n),
                                   (pow_sem, b * POW))
                for j in range(NB):
                    s.did(dve.bn_aggr(mv[:, j, :], stats[:, j, :]))
                s.wait()
                dve.wait_ge(pow_sem, (b + 1) * POW)
                free()
                for j in range(NB):
                    s.did(dve.tensor_scalar(out[:, j, :], y[:, j, :], mv[:, j, 0:1], rstd[:, j:j + 1], ALU.subtract, ALU.mult))
                s.end()

            def maxima(b, j):
                for n, (ps, q) in enumerate(((sm1, 1), (sm0, 0))):
                    dve.wait_ge(sm_ps, (b * QUADS + j) * 2 + n + 1)
                    if j == 0 and n == 0:
                        at_least(dve, rows_ps, b * 2)
                    dve.tensor_reduce(neg_max[:, q, 4 * j:4 * j + 4], ps[:, :, :], AX.X, ALU.max, negate=True)\
                       .then_inc(max_done, 1)

            def divide(b, p, j):
                dve.wait_ge(ctx_sb, b * QUADS + j + 1)
                dve.wait_ge(rrep_in, (b + 1) * 64)
                dve.tensor_tensor(ctxs[p][:, 2 * j:2 * j + 2, :], ctxs[p][:, 2 * j:2 * j + 2, :],
                                  rrep[:, 2 * j:2 * j + 2, :], ALU.mult).then_inc(divided, 1)

            def step(b, hb, p):
                o = 1 - p
                if real(b - 1):
                    for j in range(QUADS):
                        divide(b - 1, o, j)
                if real(b + 2):
                    s = added.batch(b + 2)
                    dve.wait_ge(xa_in[p], (hb + 2) * 16)
                    dve.wait_ge(fetched[p], (hb + 2) * 16 * NB)
                    for j in range(NB):
                        col = (b + 2) * NB + j
                        w = k["weight"][:, col:col + 1] if isinstance(b, int) else k["weight"][:, bass.ds(col, 1)]
                        s.did(dve.scalar_tensor_tensor(y2[:, j, :], eg[p][:, j, :], w, xa[p][:, j, :], ALU.mult, ALU.add))

                    def free():
                        at_least(dve, x2_out[p], (hb + 1) * 16)
                        at_least(dve, xT_ps, b + 1)
                    normalise(s, y2, stats2, mv2, rstd2, pow2, b + 2, x2[p], free)
                if real(b - 1):
                    s = layer3.batch(b - 1)
                    dve.wait_ge(wo_ps, b)
                    dve.wait_ge(xr_in[o], 16 * (hb + p))
                    s.did(dve.tensor_tensor(y3[:, :, :], sm0[:, 0:NB, :], xr[o][:, :, :], ALU.add))
                    cols = slice((b - 1) * NB, b * NB) if isinstance(b, int) else bass.ds((b - 1) * NB, NB)
                    normalise(s, y3, stats3, mv3, rstd3, pow3, b - 1, k["x3"][:, cols, :], lambda: None)
                if real(b + 1):
                    maxima(b + 1, 0)
                    maxima(b + 1, 1)
                if real(b):
                    dve.wait_ge(ctx_ps, (b + 1) * QUADS)
                    at_least(dve, rden_out, b * 16)
                    dve.reciprocal(rden[:, :], ps_d[:, 0:N]).then_inc(rden_sb, 1)
                if real(b + 1):
                    maxima(b + 1, 2)
                    maxima(b + 1, 3)
                if real(b + 2):
                    s = split.batch(b + 2)
                    dve.wait_ge(hi_sb, b + 3)
                    at_least(dve, lo_sb, b + 2)
                    s.did(dve.tensor_tensor(rest[:, :], st0[:, 2:4, :].rearrange("p a b -> p (a b)"), parts[p][:, 0, :], ALU.subtract))
                    s.wait()
                    s.did(dve.tensor_copy(parts[p][:, 1, :], rest[:, :]))
                    s.end()

            pipelined(dve, step, 3, 1, first=2)

        @block.gpsimd
        def _(pool):
            for i in two:
                pool.memset(k_st[i][:, :, :].bitcast(FP32), 0.0).then_inc(index_set, 1)
            pool.memset(sums[:, :, :], 0.0).then_inc(sums_set, 1)
            pool.wait_ge(index_set, 2)
            pool.wait_ge(sums_set, 1)
            for i in two:
                pool.memset(k_st[i][SHIFT_ROW:SHIFT_ROW + 1, :, :], 1.0).then_inc(ready, 1)
            pool.wait_ge(ready, 4)
            for j in range(QUADS):
                pool.memset(sums[:, j, j:32:QUADS], 1.0).then_inc(sums_set, 1)

            def root(pow_sem, step_sem, done, mv, veps, rstd, b):
                wait_apart(pool, k, (step_sem, done))
                pool.tensor_scalar(veps[:, :], mv[:, :, 1], EPS_LN, None, ALU.add).then_inc(pow_sem, 1)
                pool.wait_ge(pow_sem, b * POW + 1)
                pool.tensor_tensor(rstd[:, :], veps[:, :], k["minus_half"][:, 0:NB], ALU.pow).then_inc(pow_sem, 1)

            def mask(b, j):
                for n, pr in enumerate((p0[j % 2], p1[j % 2])):
                    wait_apart(pool, k, (p_sb, (b * QUADS + j) * 2 + n + 1))
                    pool.affine_select(out=pr[:, :, 0:P], in_=pr[:, :, 0:P], compare_op=ALU.is_ge, fill=0.0, base=0,
                                       pattern=[[0, 4], [1, P]], channel_multiplier=-1).then_inc(masked, 1)

            def step(b, hb, p):
                o = 1 - p
                if real(b + 3):
                    at_least(pool, x2_step, (b + 1) * X2 + NB)
                    at_least(pool, fetched[p], 16 * NB * (hb + 2))
                    cols = slice((b + 3) * NB, (b + 4) * NB) if isinstance(b, int) else bass.ds((b + 3) * NB, NB)
                    pool.tensor_copy(index[:, :], k["fetch"][:, cols]).then_inc(index_set, 1)
                    wait_apart(pool, k, (index_set, b + 6))
                    for j in range(NB):
                        pool.indirect_dma_start(out=eg[o][:, j, :], out_offset=None, in_=eout_d,
                                                in_offset=bass.IndirectOffsetOnAxis(ap=index[:, j:j + 1], axis=0))\
                            .then_inc(fetched[o], 16)
                if real(b + 2):
                    root(pow2, x2_step, (b + 2) * X2 + 3 * NB, mv2, veps2, rstd2, b + 2)
                if real(b):
                    mask(b, 1)
                    mask(b, 2)
                if real(b - 1):
                    root(pow3, x3_step, (b - 1) * X3 + 1 + 2 * NB, mv3, veps3, rstd3, b - 1)
                if real(b):
                    mask(b, 3)
                if real(b + 2):
                    pool.wait_ge(split_step, (b + 3) * SPLIT)
                    pool.tensor_tensor(parts[p][:, 2, :], rest[:, :], parts[p][:, 1, :], ALU.subtract).then_inc(lo_sb, 1)
                if real(b + 1):
                    mask(b + 1, 0)

            pipelined(pool, step, 3, 1)


def coupling_layer(nc, k, a, out, debug=None):
    CYCLES, HALVES, GROUPS, GB = 3, 2, 4, 4
    W = GB * P
    HB = GROUPS * GB
    BATCHES = HB // NB
    F2, F3 = C // 2, C // 4
    Q = C // 4

    with ExitStack() as ctx:
        sb = lambda name, shape, dt: ctx.enter_context(nc.sbuf_tensor("cn_" + name, shape, dt))
        pb = lambda name, shape, dt: ctx.enter_context(nc.psum_tensor("cn_" + name, shape, dt))
        sem = lambda name: ctx.enter_context(nc.semaphore("cn_" + name))
        two = range(2)
        x3 = k["x3"]
        cur = sb("cur", [P, HALVES * HB, C], FP32)
        w1, w2 = sb("w1", [P, C], FP32), sb("w2", [P, F2], FP32)
        w3 = sb("w3", [P, 2 * F3], FP32)
        w4 = sb("w4", [P, GROUPS], FP32)
        b1, b2, b3, b4 = (sb(f"b{i}", [P, 1], FP32) for i in (1, 2, 3, 4))
        g1, g2, g3 = sb("g1", [P, F2], FP32), sb("g2", [F2, F3], FP32), sb("g3", [F3, 1], FP32)
        g3_rep = sb("g3_rep", [F3, P], FP32)
        gb1, gb2, gb3 = sb("gb1", [F2, 1], FP32), sb("gb2", [F3, 1], FP32), sb("gb3", [P, 1], FP32)
        spread = sb("spread", [P, 1], FP32)
        spread_g, spread_t = sb("spread_g", [P, 1], FP32), sb("spread_t", [P, 1], FP32)
        xT = [sb(f"xT{i}", [P, W], FP32) for i in two]
        h1 = [sb(f"h1_{i}", [P, W], FP32) for i in range(GROUPS)]
        h2 = [sb(f"h2_{i}", [P, W], FP32) for i in two]
        h3 = sb("h3", [P, W], FP32)
        tanh_t = sb("tanh_t", [P, HB], FP32)
        coupling, minus_coupling = sb("coupling", [P, HB], FP32), sb("minus_coupling", [P, HB], FP32)
        context = sb("context", [P, HALVES, BATCHES], FP32)
        gh1, gh2 = sb("gh1", [F2, BATCHES], FP32), sb("gh2", [F3, BATCHES], FP32)
        tanh_g = sb("tanh_g", [P, BATCHES], FP32)
        base = sb("base", [P, HALVES, BATCHES], FP32)
        turned = sb("turned", [P, GB, 2, Q], FP32)
        y = sb("y", [P, HB, C], FP32)
        stats, mv = sb("stats", [P, HB, 6], FP32), sb("mv", [P, HB, 2], FP32)
        veps, rstd, nr_t = sb("veps", [P, HB], FP32), sb("rstd", [P, HB], FP32), sb("nr_t", [P, HB], FP32)
        result = sb("result", [P, HALVES * HB, C], FP32)
        ps_t = [pb(f"ps_t{i}", [P, W], FP32) for i in two]
        ps_1 = [pb(f"ps_1{i}", [P, W], FP32) for i in two]
        ps_2 = [pb(f"ps_2{i}", [P, W], FP32) for i in two]
        ps_3 = pb("ps_3", [P, W], FP32)
        ps_z = pb("ps_z", [P, W], FP32)
        w_in, cleared, t_ps, xT_sb, h1_ps, h1_sb = (sem(n) for n in ("w_in", "cleared", "t_ps", "xT_sb", "h1_ps", "h1_sb"))
        h2_ps, h2_sb, h3_ps, h3_sb, z_ps, tanh_sb = (sem(n) for n in ("h2_ps", "h2_sb", "h3_ps", "h3_sb", "z_ps", "tanh_sb"))
        setup, summed, g_ps, g_sb, base_set = (sem(n) for n in ("setup", "summed", "g_ps", "g_sb", "base_set"))
        coupled, turn_step, moved, norm_step, normed, stored = (sem(n) for n in ("coupled", "turn_step", "moved", "norm_step", "normed", "stored"))
        block = ctx.enter_context(nc.Block())
        LOADS = 3 + 2 * 2 + 2 * GROUPS + 8
        NORM = 4 + NEWTON
        ZERO = 2
        SETUP = 5
        G = 3

        @block.sync
        def _(sp):
            column = lambda v: v.unsqueeze(1)
            col_rep = lambda v: v[None, :].broadcast_to([P, 1])
            sp.dma_start(w1[:, :], a["L1_ffn_cn_w1"]).then_inc(w_in, 16)
            sp.dma_start(b1[:, :], column(a["L1_ffn_cn_b1"])).then_inc(w_in, 16)
            sp.dma_start(w2[:, :], a["L1_ffn_cn_w2"]).then_inc(w_in, 16)
            sp.wait_ge(cleared, ZERO)
            for u in two:
                sp.dma_start(b2[u * F2:(u + 1) * F2, :], column(a["L1_ffn_cn_b2"])).then_inc(w_in, 16)
                sp.dma_start(w3[u * F2:(u + 1) * F2, u * F3:(u + 1) * F3], a["L1_ffn_cn_w3"]).then_inc(w_in, 16)
            for g in range(GROUPS):
                sp.dma_start(b3[g * F3:(g + 1) * F3, :], column(a["L1_ffn_cn_b3"])).then_inc(w_in, 16)
                sp.dma_start(w4[g * F3:(g + 1) * F3, g:g + 1], a["L1_ffn_cn_w4"]).then_inc(w_in, 16)
            sp.dma_start(b4[:, :], col_rep(a["L1_ffn_cn_b4"])).then_inc(w_in, 16)
            sp.dma_start(g1[:, :], a["L1_ffn_gc_w1"]).then_inc(w_in, 16)
            sp.dma_start(gb1[:, :], column(a["L1_ffn_gc_b1"])).then_inc(w_in, 16)
            sp.dma_start(g2[:, :], a["L1_ffn_gc_w2"]).then_inc(w_in, 16)
            sp.dma_start(gb2[:, :], column(a["L1_ffn_gc_b2"])).then_inc(w_in, 16)
            sp.dma_start(g3[:, :], a["L1_ffn_gc_w3"]).then_inc(w_in, 16)
            sp.dma_start(gb3[:, :], col_rep(a["L1_ffn_gc_b3"])).then_inc(w_in, 16)
            sp.dma_start(spread[:, :], col_rep(a["L1_ffn_adaptive_range"])).then_inc(w_in, 16)
            if debug:
                sp.dma_start(debug["x3"].rearrange("(b p) c -> p b c", p=P), x3[:, :, :]).then_inc(stored, 16)
                sp.wait_ge(stored, 16)
            for g in range(HALVES * GROUPS):
                sp.wait_ge(normed, g + 1)
                sp.dma_start(out[g * W:(g + 1) * W, :].rearrange("(j p) c -> p j c", p=P),
                             result[:, g * GB:(g + 1) * GB, :]).then_inc(stored, 16)
            sp.wait_ge(stored, 16 * (HALVES * GROUPS + (1 if debug else 0)))

        @block.gpsimd
        def _(pool):
            pool.memset(w3[:, :], 0.0).then_inc(cleared, 1)
            pool.memset(w4[:, :], 0.0).then_inc(cleared, 1)


        @block.tensor
        def _(pe):
            pe.wait_ge(w_in, 16 * LOADS)

            def turn(n, s, src, g):
                at_least(pe, moved, (n - 2) * GROUPS + g + 1)
                at_least(pe, xT_sb, n * GROUPS + g - 1)
                for j in range(GB):
                    last = pe.transpose(ps_t[g % 2][:, j * P:(j + 1) * P], src[:, s * HB + g * GB + j, :], k["ident"][:, :])
                last.then_inc(t_ps, 1)

            def layer1(n, g):
                pe.wait_ge(xT_sb, n * GROUPS + g + 1)
                at_least(pe, h1_sb, n * GROUPS + g - 1)
                pe.matmul(ps_1[g % 2][:, :], w1[:, :], xT[g % 2][:, :], start=True, stop=True).then_inc(h1_ps, 1)

            def layer2(n, i):
                pe.wait_ge(h1_sb, n * GROUPS + 2 * i + 2)
                at_least(pe, h2_sb, (n - 1) * 2 + i + 1)
                for u in two:
                    last = pe.matmul(ps_2[i][u * F2:(u + 1) * F2, :], w2[:, :], h1[2 * i + u][:, :], start=True, stop=True)
                last.then_inc(h2_ps, 1)

            def layer3(n):
                pe.wait_ge(h2_sb, n * 2 + 2)
                at_least(pe, h3_sb, n)
                for i in two:
                    last = pe.matmul(ps_3[i * F2:(i + 1) * F2, :], w3[:, :], h2[i][:, :], start=True, stop=True)
                last.then_inc(h3_ps, 1)

            def layer4(n):
                pe.wait_ge(h3_sb, n + 1)
                at_least(pe, tanh_sb, n)
                if isinstance(n, int) and n == 1:
                    pe.wait_ge(g_sb, 2 * G)
                elif isinstance(n, int) and n == 0:
                    pe.wait_ge(g_sb, G)
                for j in range(GB):
                    last = pe.matmul(ps_z[:, j:HB:GB], h3[:, j * P:(j + 1) * P], w4[:, :], start=True, stop=True)
                last.then_inc(z_ps, 1)

            def global_net(s):
                pe.wait_ge(summed, (s + 1) * GROUPS)
                at_least(pe, tanh_sb, s)
                n = s * G
                pe.matmul(ps_z[0:F2, 0:BATCHES], g1[:, :], context[:, s, :], start=True, stop=True).then_inc(g_ps, 1)
                pe.wait_ge(g_sb, n + 1)
                pe.matmul(ps_z[0:F3, 0:BATCHES], g2[:, :], gh1[:, :], start=True, stop=True).then_inc(g_ps, 1)
                pe.wait_ge(g_sb, n + 2)
                pe.matmul(ps_z[:, 0:BATCHES], g3_rep[:, :], gh2[:, :], start=True, stop=True).then_inc(g_ps, 1)

            def run(n, s, src, before=True):
                turn(n, s, src, 0)
                turn(n, s, src, 1)
                if before:
                    layer2(n - 1, 1)
                layer1(n, 0)
                turn(n, s, src, 2)
                if before:
                    layer3(n - 1)
                layer1(n, 1)
                turn(n, s, src, 3)
                if before:
                    layer4(n - 1)
                layer1(n, 2)
                layer2(n, 0)
                layer1(n, 3)

            pe.wait_ge(setup, SETUP)
            run(0, 0, x3, before=False)
            global_net(0)
            run(1, 1, x3)
            global_net(1)
            with pe.Fori(1, CYCLES) as cycle:
                for s in two:
                    run(cycle * 2 + s, s, cur)
            layer2(2 * CYCLES - 1, 1)
            layer3(2 * CYCLES - 1)
            layer4(2 * CYCLES - 1)

        @block.scalar
        def _(act):
            def gelu1(n, g):
                act.wait_ge(h1_ps, n * GROUPS + g + 1)
                at_least(act, h2_ps, (n - 1) * 2 + g // 2 + 1)
                act.activation(h1[g][:, :], ps_1[g % 2][:, :], ACT.Gelu, bias=b1[:, :]).then_inc(h1_sb, 1)

            def gelu2(n, i):
                act.wait_ge(h2_ps, n * 2 + i + 1)
                at_least(act, h3_ps, n)
                act.activation(h2[i][:, :], ps_2[i][:, :], ACT.Gelu, bias=b2[:, :]).then_inc(h2_sb, 1)

            def gelu3(n):
                act.wait_ge(h3_ps, n + 1)
                at_least(act, z_ps, n)
                act.activation(h3[:, :], ps_3[:, :], ACT.Gelu, bias=b3[:, :]).then_inc(h3_sb, 1)

            def tanh4(n):
                act.wait_ge(z_ps, n + 1)
                at_least(act, coupled, 2 * n)
                act.activation(tanh_t[:, :], ps_z[:, 0:HB], ACT.Tanh, bias=b4[:, :], scale=0.5).then_inc(tanh_sb, 1)

            def global_net(s):
                n = s * G
                act.wait_ge(g_ps, n + 1)
                act.activation(gh1[:, :], ps_z[0:F2, 0:BATCHES], ACT.Gelu, bias=gb1[:, :], scale=1.0 / N).then_inc(g_sb, 1)
                act.wait_ge(g_ps, n + 2)
                act.activation(gh2[:, :], ps_z[0:F3, 0:BATCHES], ACT.Gelu, bias=gb2[:, :]).then_inc(g_sb, 1)
                act.wait_ge(g_ps, n + 3)
                at_least(act, base_set, s)
                act.activation(tanh_g[:, :], ps_z[:, 0:BATCHES], ACT.Tanh, bias=gb3[:, :], scale=0.5).then_inc(g_sb, 1)

            def run(n, s, before=True):
                if before:
                    gelu2(n - 1, 1)
                gelu1(n, 0)
                if before:
                    gelu3(n - 1)
                gelu1(n, 1)
                if before:
                    tanh4(n - 1)
                gelu1(n, 2)
                gelu2(n, 0)
                gelu1(n, 3)

            act.wait_ge(w_in, 16 * LOADS)
            act.wait_ge(setup, SETUP)
            run(0, 0, before=False)
            global_net(0)
            run(1, 1)
            global_net(1)
            with act.Fori(1, CYCLES) as cycle:
                for s in two:
                    run(cycle * 2 + s, s)
            gelu2(2 * CYCLES - 1, 1)
            gelu3(2 * CYCLES - 1)
            tanh4(2 * CYCLES - 1)

        @block.vector
        def _(dve):
            dve.wait_ge(w_in, 16 * LOADS)
            dve.tensor_copy(g3_rep[:, :], g3[:, :].broadcast_to([F3, P])).then_inc(setup, 1)
            dve.tensor_scalar(b4[:, :], b4[:, :], 0.5, None, ALU.mult).then_inc(setup, 1)
            dve.tensor_scalar(gb3[:, :], gb3[:, :], 0.5, None, ALU.mult).then_inc(setup, 1)
            dve.tensor_scalar(spread_g[:, :], spread[:, :], 0.7, None, ALU.mult).then_inc(setup, 1)
            dve.tensor_scalar(spread_t[:, :], spread[:, :], 0.3, None, ALU.mult).then_inc(setup, 1)
            dve.wait_ge(setup, SETUP)

            def copy_out(n, g):
                dve.wait_ge(t_ps, n * GROUPS + g + 1)
                at_least(dve, h1_ps, n * GROUPS + g - 1)
                dve.tensor_copy(xT[g % 2][:, :], ps_t[g % 2][:, :]).then_inc(xT_sb, 1)

            def sums(s, g):
                dve.wait_ge(xT_sb, s * GROUPS + g + 1)
                dve.tensor_reduce(context[:, s, 2 * g:2 * g + 2], xT[g % 2][:, :].rearrange("p (b n) -> p b n", n=N),
                                  AX.X, ALU.add).then_inc(summed, 1)

            def global_part(s):
                dve.wait_ge(g_sb, (s + 1) * G)
                dve.tensor_scalar(base[:, s, :], tanh_g[:, :], spread_g[:, :], 0.1, ALU.mult, ALU.add).then_inc(base_set, 1)

            def couple(n, s):
                dve.wait_ge(tanh_sb, n + 1)
                at_least(dve, moved, n * GROUPS)
                dve.scalar_tensor_tensor(coupling[:, :].rearrange("p (b j) -> p b j", j=NB),
                                         tanh_t[:, :].rearrange("p (b j) -> p b j", j=NB), spread_t[:, :],
                                         base[:, s, :].unsqueeze(2).broadcast_to([P, BATCHES, NB]),
                                         ALU.mult, ALU.add).then_inc(coupled, 1)
                dve.wait_ge(coupled, 2 * n + 1)
                dve.tensor_scalar(minus_coupling[:, :], coupling[:, :], -1.0, None, ALU.mult).then_inc(coupled, 1)
                dve.wait_ge(coupled, 2 * n + 2)

            def quarters(t, b):
                return t[:, b, :].rearrange("p (q w) -> p q w", w=Q)

            def move(n, s, src, g):
                in_place = src is cur
                base_step = (n - 2) * GROUPS * 2 + g * 2
                for j in range(GB):
                    t = s * HB + g * GB + j
                    b = g * GB + j
                    x = quarters(src, t)
                    aside = turned[:, j, :, :] if in_place else quarters(cur, t)[:, 0:4:3, :]
                    last = dve.scalar_tensor_tensor(aside, x[:, 2:0:-1, :], coupling[:, b:b + 1], x[:, 0:4:3, :], ALU.mult, ALU.add)
                if in_place:
                    last.then_inc(turn_step, 1)
                    dve.wait_ge(turn_step, base_step + 1)
                for j in range(GB):
                    t = s * HB + g * GB + j
                    b = g * GB + j
                    x = quarters(src, t)
                    last = dve.scalar_tensor_tensor(quarters(cur, t)[:, 1:3, :], x[:, 3::-3, :], minus_coupling[:, b:b + 1],
                                                    x[:, 1:3, :], ALU.mult, ALU.add)
                if in_place:
                    last.then_inc(turn_step, 1)
                    dve.wait_ge(turn_step, base_step + 2)
                    blocks = slice(s * HB + g * GB, s * HB + (g + 1) * GB)
                    last = dve.tensor_copy(cur[:, blocks, :].rearrange("p b (q w) -> p b q w", w=Q)[:, :, 0:4:3, :], turned[:, :, :, :])
                last.then_inc(moved, 1)
                if in_place:
                    dve.wait_ge(moved, n * GROUPS + g + 1)

            def norm(s):
                steps = Steps(dve, norm_step, 1000).batch(0)
                steps.n = s * NORM
                dve.wait_ge(moved, (2 * CYCLES - 2 + s + 1) * GROUPS)
                blocks = slice(s * HB, (s + 1) * HB)
                steps.did(dve.tensor_tensor(y[:, :, :], x3[:, blocks, :], cur[:, blocks, :], ALU.add))
                steps.wait()
                for j in range(HB):
                    last = dve.bn_stats(stats[:, j, :], y[:, j, :])
                steps.did(last)
                steps.wait()
                for j in range(HB):
                    last = dve.bn_aggr(mv[:, j, :], stats[:, j, :])
                steps.did(last)
                steps.wait()
                steps.did(dve.tensor_scalar(veps[:, :], mv[:, :, 1], EPS_LN, None, ALU.add))
                steps.wait()
                newton_rsqrt(dve, steps, veps[:, :], rstd[:, :], nr_t[:, :])
                steps.wait()
                assert steps.n == (s + 1) * NORM
                for g in range(GROUPS):
                    for j in range(g * GB, (g + 1) * GB):
                        last = dve.tensor_scalar(result[:, s * HB + j, :], y[:, j, :], mv[:, j, 0:1], rstd[:, j:j + 1],
                                                 ALU.subtract, ALU.mult)
                    last.then_inc(normed, 1)

            def run(n, s, src, before_s=None, before_src=None):
                for g in range(GROUPS):
                    copy_out(n, g)
                    if src is x3:
                        sums(s, g)
                if before_src is not None:
                    couple(n - 1, before_s)
                    for g in range(GROUPS):
                        move(n - 1, before_s, before_src, g)

            run(0, 0, x3)
            global_part(0)
            run(1, 1, x3, 0, x3)
            global_part(1)
            for g in range(GROUPS):
                copy_out(2, g)
            couple(1, 1)
            for g in range(GROUPS):
                move(1, 1, x3, g)
            run(3, 1, cur, 0, cur)
            with dve.Fori(2, CYCLES) as cycle:
                for s in two:
                    run(cycle * 2 + s, s, cur, 1 - s, cur)
            norm(0)
            couple(2 * CYCLES - 1, 1)
            for g in range(GROUPS):
                move(2 * CYCLES - 1, 1, cur, g)
            dve.wait_ge(normed, GROUPS)
            norm(1)


def program(nc, a, out, debug=None):
    x = a["L0_attn_x"].rearrange("b n c -> (b n) c")
    scratch = lambda name, shape, dt: nc.dram_tensor(name, shape, dt, kind="Internal").ap()
    parts_d = scratch("parts_d", [3, P, 2 * N], BF16)
    x1_d = scratch("x1_d", [T, C], FP32) if not debug else debug["x1"]
    disp_d = scratch("disp_d", [SLOTS + T, C], FP32)
    eout_d = scratch("eout_d", [SLOTS, C], FP32) if not debug else debug["eout"]
    x2_d = scratch("x2_d", [T, C], FP32) if not debug else debug["x2"]
    rden_d = scratch("rden_d", [P, N], FP32)
    with ExitStack() as ctx:
        sb = lambda name, shape, dt: ctx.enter_context(nc.sbuf_tensor(name, shape, dt))
        k = {
            "ident": sb("ident", [P, P], FP32), "ident_bf": sb("ident_bf", [P, P], BF16),
            "tri_bf": sb("tri_bf", [P, P], BF16), "ones_bf": sb("ones_bf", [P, P], BF16),
            "ones": sb("ones", [P, P], FP32), "causal": sb("causal", [P, 4 * P], BF16),
            "zeros": sb("zeros", [P, 5 * C], FP32), "minus_half": sb("minus_half", [P, 4], FP32),
            "backwards": sb("backwards", [P, E], FP32), "gate_T": sb("gate_T", [P, E], FP32),
            "slots_before": sb("slots_before", [P, E], FP32), "slots_end": sb("slots_end", [P, E], FP32),
            "dump": sb("dump", [P, NB], FP32), "qks": sb("qks", [P, HD], FP32),
            "minus_bound": sb("minus_bound", [P, 1], FP32),
            "w1": [sb(f"w1_{i}", [P, FF], FP32) for i in range(4)],
            "w2": [sb(f"w2_{i}", [P, FC, C], FP32) for i in range(4)],
            "w_in": [ctx.enter_context(nc.semaphore(f"expert_in{i}")) for i in range(4)],
            "constants_set": ctx.enter_context(nc.semaphore("constants_set")),
            "fetch": sb("fetch", [P, T // P], U32), "weight": sb("weight", [P, T // P], FP32),
            "x3": sb("x3", [P, T // P, C], FP32),
        }
        constants(nc, k, a["L0_ffn_gate_w"], a["L0_attn_q_scale"], a["L0_attn_k_scale"])
        l0_layer(nc, k, x, a["L0_attn_Wqkv"], a["L0_attn_Wproj"], a["L0_attn_bproj"],
                 a["L0_ffn_w1"], a["L0_ffn_w2"], parts_d, x1_d, disp_d)
        experts(nc, k, a["L0_ffn_w1"], a["L0_ffn_w2"], disp_d, eout_d)
        l1_layer(nc, k, a["L1_attn_Wq"], a["L1_attn_Wk"], a["L1_attn_Wv"], a["L1_attn_Wo"], parts_d, rden_d,
                 x1_d, eout_d, x2_d)
        coupling_layer(nc, k, a, out, debug)


_INS = ['L0_attn_x', 'L0_attn_Wqkv', 'L0_attn_Wproj', 'L0_attn_bproj',
        'L0_attn_q_scale', 'L0_attn_k_scale', 'L0_ffn_gate_w', 'L0_ffn_w1',
        'L0_ffn_w2', 'L1_attn_Wq', 'L1_attn_Wk', 'L1_attn_Wv',
        'L1_attn_Wo', 'L1_ffn_cn_w1', 'L1_ffn_cn_b1', 'L1_ffn_cn_w2',
        'L1_ffn_cn_b2', 'L1_ffn_cn_w3', 'L1_ffn_cn_b3', 'L1_ffn_cn_w4',
        'L1_ffn_cn_b4', 'L1_ffn_gc_w1', 'L1_ffn_gc_b1', 'L1_ffn_gc_w2',
        'L1_ffn_gc_b2', 'L1_ffn_gc_w3', 'L1_ffn_gc_b3', 'L1_ffn_adaptive_range']


def kernel(**inputs):
    import numpy as np
    import concourse.bacc as bacc
    from concourse.bass_utils import run_bass_kernel_spmd

    nc = bacc.Bacc("TRN2", target_bir_lowering=False, num_devices=1)
    arrays, tensors = {}, {}
    for name in _INS:
        array = np.ascontiguousarray(inputs[name])
        arrays[f"in_{name}_dram"] = array
        tensors[name] = nc.dram_tensor(f"in_{name}_dram", array.shape, mybir.dt.from_np(array.dtype), kind="ExternalInput").ap()
    out = nc.dram_tensor("out_0_dram", (B, N, C), FP32, kind="ExternalOutput").ap()
    program(nc, tensors, out.rearrange("b n c -> (b n) c"))
    result = run_bass_kernel_spmd(nc, [arrays], core_ids=[0])
    return result.results[0]["out_0_dram"]
```

```python
from contextlib import ExitStack

import concourse.bass as bass
from concourse import mybir

FP32 = mybir.dt.float32
BF16 = mybir.dt.bfloat16
I32 = mybir.dt.int32
U32 = mybir.dt.uint32
ALU = mybir.AluOpType
ACT = mybir.ActivationFunctionType
AX = mybir.AxisListType

P = 128
B, N, C = 16, 256, 128
NB = N // P
T = B * N
H, HD = 16, 8
DV = 64
PAIRS = H // 2
QUADS = H // 4
EPS_LN = 1e-5
EPS_RMS = 1e-8
SCALE = HD ** -0.5

E, FF = 16, 512
CAP = int(1.25 * T / E)
CAP += CAP % 2
SLOTS = E * CAP
FC = FF // P

MEETS = ((0, 3), (1, 2), (2, 1))
TERMS = sum(n for _, n in MEETS)
SHIFT_ROW = 64


def load_stacks(eng, parts_d, q_st, k_st, loaded):
    src = parts_d.rearrange("t (c h) n -> t c h n", h=H)
    queries = src.rearrange("t c h n -> (t c) h n")
    first = 0
    for part, n in MEETS:
        eng.dma_start(q_st[first:first + n * HD, :, :], queries[0:n * HD, :, 0:N]).then_inc(loaded, 16)
        keys = src[part, :, :, N:2 * N].unsqueeze(0).broadcast_to([n, HD, H, N])
        eng.dma_start(k_st[first:first + n * HD, :, :], keys).then_inc(loaded, 16)
        first += n * HD


STACK_LOADS = 2 * len(MEETS)


class Steps:

    def __init__(self, eng, sem, per_batch):
        self.eng, self.sem, self.per_batch = eng, sem, per_batch

    def batch(self, b):
        self.base, self.n = b * self.per_batch, 0
        return self

    def did(self, ins):
        ins.then_inc(self.sem, 1)
        self.n += 1

    def wait(self):
        self.eng.wait_ge(self.sem, self.base + self.n)

    def end(self):
        assert self.n == self.per_batch, (self.n, self.per_batch)


def at_least(eng, sem, value):
    if not isinstance(value, int) or value > 0:
        eng.wait_ge(sem, value)


def wait_apart(eng, k, *waits):
    waits = [(sem, value if isinstance(value, int) else eng.compute_val(value)) for sem, value in waits]
    eng.wait_ge(k["constants_set"], 1)
    for sem, value in waits:
        at_least(eng, sem, value)


def pipelined(eng, step, ahead, behind, total=B, unroll=2, first=0):
    lo, hi = max(behind, first), total - ahead
    hi -= (hi - lo) % unroll
    for b in range(-ahead, lo):
        step(b, b // unroll, b % unroll)
    with eng.Fori(0, (hi - lo) // unroll) as turn:
        for b in range(lo, lo + unroll):
            step(turn * unroll + b, turn + b // unroll, b % unroll)
    for b in range(hi, total + behind):
        step(b, b // unroll, b % unroll)


def real(b):
    return not isinstance(b, int) or 0 <= b < B


GUESS = float(0x5F3759DF)


def constants(nc, k, gate_w, q_scale, k_scale):
    with ExitStack() as ctx:
        sb = lambda name, shape, dt: ctx.enter_context(nc.sbuf_tensor(name, shape, dt))
        sem = lambda name: ctx.enter_context(nc.semaphore(name))
        iota_base = sb("iota_base", [P, E], I32)
        iota_back = sb("iota_back", [P, E], I32)
        iota_dump = sb("iota_dump", [P, NB], I32)
        gate_rows = sb("gate_rows", [E, C], FP32)
        ks = sb("ks_rep", [P, HD], FP32)
        small = sb("bound_parts", [P, 4], FP32)
        gps = ctx.enter_context(nc.psum_tensor("gate_ps", [P, E], FP32))
        filled, cut, loaded = sem("filled"), sem("cut"), sem("loaded")
        gate_turned, step = sem("gate_turned"), sem("const_step")
        block = ctx.enter_context(nc.Block())

        @block.sync
        def _(sp):
            sp.dma_start(gate_rows[:, :], gate_w).then_inc(loaded, 16)
            sp.dma_start(k["qks"][:, :], q_scale[None, :].broadcast_to([P, HD])).then_inc(loaded, 16)
            sp.dma_start(ks[:, :], k_scale[None, :].broadcast_to([P, HD])).then_inc(loaded, 16)

        @block.gpsimd
        def _(pool):
            pool.memset(k["ident"][:, :], 0.0).then_inc(filled, 1)
            pool.memset(k["tri_bf"][:, :], 1.0).then_inc(filled, 1)
            pool.memset(k["causal"][:, :], 0.0).then_inc(filled, 1)
            pool.iota(iota_base[:, :], pattern=[[CAP, E]], base=0, channel_multiplier=0).then_inc(filled, 1)
            pool.iota(iota_back[:, :], pattern=[[-1, E]], base=E, channel_multiplier=0).then_inc(filled, 1)
            pool.iota(iota_dump[:, :], pattern=[[P, NB]], base=SLOTS, channel_multiplier=1).then_inc(filled, 1)
            pool.wait_ge(filled, 6)
            pool.affine_select(out=k["ident"][:, :], in_=k["ident"][:, :], compare_op=ALU.not_equal, fill=1.0,
                               base=0, pattern=[[-1, P]], channel_multiplier=1).then_inc(cut, 1)
            pool.affine_select(out=k["tri_bf"][:, :], in_=k["tri_bf"][:, :], compare_op=ALU.is_ge, fill=0.0,
                               base=0, pattern=[[1, P]], channel_multiplier=-1).then_inc(cut, 1)
            pool.affine_select(out=k["causal"][:, :].rearrange("p (a b) -> p a b", b=P),
                               in_=k["causal"][:, :].rearrange("p (a b) -> p a b", b=P),
                               compare_op=ALU.is_ge, fill=-1e30,
                               base=0, pattern=[[0, 4], [-1, P]], channel_multiplier=1).then_inc(cut, 1)

        @block.tensor
        def _(pe):
            pe.wait_ge(loaded, 48)
            pe.wait_ge(cut, 1)
            pe.transpose(gps[:, :], gate_rows[:, :], k["ident"][0:E, 0:E]).then_inc(gate_turned, 1)

        @block.vector
        def _(dve):
            s = Steps(dve, step, 99).batch(0)
            s.did(dve.memset(k["ones"][:, :], 1.0))
            s.did(dve.memset(k["ones_bf"][:, :].bitcast(I32), 0x3F803F80))
            s.did(dve.memset(k["minus_half"][:, :], -0.5))
            s.did(dve.memset(k["three_halves"][:, :], 1.5))
            s.did(dve.memset(k["eps_rms"][:, :], EPS_RMS))
            s.did(dve.memset(k["zeros"][:, :], 0.0))
            dve.wait_ge(gate_turned, 1)
            s.did(dve.tensor_copy(k["gate_T"][:, :], gps[:, :]))
            dve.wait_ge(cut, 3)
            s.did(dve.tensor_copy(k["ident_bf"][:, :], k["ident"][:, :]))
            s.did(dve.tensor_copy(k["backwards"][:, :], iota_back[:, :]))
            s.did(dve.tensor_copy(k["slots_before"][:, :], iota_base[:, :]))
            s.did(dve.tensor_copy(k["dump"][:, :], iota_dump[:, :]))
            s.wait()
            s.did(dve.tensor_scalar(k["slots_end"][:, :], k["slots_before"][:, :], float(CAP), None, ALU.add))
            s.wait()
            s.did(dve.tensor_scalar(k["slots_before"][:, :], k["slots_before"][:, :], -1.0, None, ALU.add))
            dve.wait_ge(loaded, 48)
            s.did(dve.tensor_tensor(k["qks"][:, :], k["qks"][:, :], ks[:, :], ALU.mult))
            s.wait()
            s.did(dve.tensor_reduce(small[:, 0:1], k["qks"][:, :], AX.X, ALU.max, apply_absolute_value=True))
            s.wait()
            s.did(dve.tensor_scalar(k["minus_bound"][:, :], small[:, 0:1], -HD * SCALE, None, ALU.mult))
            s.wait()
            dve.nop().then_inc(k["constants_set"], 1)



def l0_layer(nc, k, x, Wqkv, Wproj, bproj, w1, w2, parts_d, x1_d, disp_d):
    SC = 4 * N
    CHUNKS = QUADS * NB
    RING = 4
    VW = 2 * HD
    VQ = 8 * VW + VW
    G2 = NB * H * 2

    def v_first(j):
        return VQ * j - VW * (j % 2)

    with ExitStack() as ctx:
        sb = lambda name, shape, dt: ctx.enter_context(nc.sbuf_tensor("l0_" + name, shape, dt))
        pb = lambda name, shape, dt: ctx.enter_context(nc.psum_tensor("l0_" + name, shape, dt))
        sem = lambda name: ctx.enter_context(nc.semaphore("l0_" + name))
        two = range(2)
        w_qkv = sb("w_qkv", [P, 3 * C], FP32)
        w_proj = sb("w_proj", [P, C], FP32)
        b_proj = sb("b_proj", [P, C], FP32)
        xin = [sb(f"xin{i}", [P, NB, C], FP32) for i in two]
        xr = [sb(f"xr{i}", [P, NB, C], FP32) for i in two]
        xT = [sb(f"xT{i}", [P, N], FP32) for i in two]
        sq = sb("sq", [P, NB, 2 * C], FP32)
        ms = sb("ms", [P, G2], FP32)
        half_ms = sb("half_ms", [P, G2], FP32)
        nr_y = sb("nr_y", [P, G2], FP32)
        nr_t = sb("nr_t", [P, G2], FP32)
        rms = sb("rms", [P, G2], FP32)
        qkn = [sb(f"qkn{i}", [P, NB, 2 * C], FP32) for i in two]
        parts = [sb(f"parts{i}", [P, 3, 2 * N], BF16) for i in two]
        rest = sb("rest", [P, 2 * N], FP32)
        q_st, k_st = k["q_st"], k["k_st"]
        vpad = [sb(f"vpad{i}", [P, NB, QUADS * VQ], FP32) for i in two]
        probs = [sb(f"probs{i}", [P, SC], FP32) for i in range(RING)]
        o_sb = sb("o_sb", [P, 2 * N], FP32)
        rden = sb("rden", [P, NB * H], FP32)
        att = sb("att", [P, NB * C], FP32)
        attT = sb("attT", [P, N], FP32)
        y = sb("y", [P, NB, C], FP32)
        stats = sb("stats", [P, NB, 6], FP32)
        mv = sb("mv", [P, NB, 2], FP32)
        veps = sb("veps", [P, NB], FP32)
        rstd = sb("rstd", [P, NB], FP32)
        x1 = [sb(f"x1_{i}", [P, NB, C], FP32) for i in two]
        x1T = sb("x1T", [P, N], FP32)
        top = sb("top", [P, NB], FP32)
        below = sb("below", [P, NB, E], FP32)
        ex = sb("ex", [P, NB, E], FP32)
        cand = sb("cand", [P, NB, E], FP32)
        first = sb("first", [P, NB], FP32)
        hot = sb("hot", [P, NB, E], FP32)
        hot_bf = sb("hot_bf", [P, NB, E], BF16)
        slots = sb("slots", [P, NB, 2, E], FP32)
        choices = sb("choices", [P, NB, 2, E], FP32)
        picked = sb("picked", [P, NB, 2], FP32)
        keep = sb("keep", [P, NB], FP32)
        kept_slot = sb("kept_slot", [P, NB], FP32)
        spare = sb("spare", [P, NB], FP32)
        esum = sb("esum", [P, NB], FP32)
        prob = sb("prob", [P, NB], FP32)
        sidx = [sb(f"sidx{i}", [P, NB], U32) for i in two]
        ps_s = [pb(f"ps_s{i}", [P, SC], FP32) for i in two]
        ps_o = pb("ps_o", [P, 2 * N], FP32)
        ps_a = [pb(f"ps_a{i}", [P, 512], FP32) for i in two]
        ps_b = pb("ps_b", [P, 512], FP32)

        w_qkv_in, w_in, cleared, rows_set = (sem(n) for n in ("w_qkv_in", "w_in", "cleared", "rows_set"))
        v_ones, ends_set = sem("v_ones"), sem("ends_set")
        x_in, xr_in = [sem(f"x_in{i}") for i in two], [sem(f"xr_in{i}") for i in two]
        xT_ps, xT_sb, qk_ps, sq_sb, v_ps, v_sb = (sem(n) for n in ("xT_ps", "xT_sb", "qk_ps", "sq_sb", "v_ps", "v_sb"))
        norm_step, newton_step, qkT_ps, hi_sb = (sem(n) for n in ("norm_step", "newton_step", "qkT_ps", "hi_sb"))
        split_step, lo_sb, parts_out, stacks_in = (sem(n) for n in ("split_step", "lo_sb", "parts_out", "stacks_in"))
        scores_ps, probs_sb, pv_done, o_out = (sem(n) for n in ("scores_ps", "probs_sb", "pv_done", "o_out"))
        oT_ps, att_step, attT_ps, attT_sb, proj_ps = (sem(n) for n in ("oT_ps", "att_step", "attT_ps", "attT_sb", "proj_ps"))
        xr_step, ln_step, pow_step, x1T_ps, x1T_sb = (sem(n) for n in ("xr_step", "ln_step", "pow_step", "x1T_ps", "x1T_sb"))
        logit_ps, gate_step, exp_sb, rank_ps, rank_step = (sem(n) for n in ("logit_ps", "gate_step", "exp_sb", "rank_ps", "rank_step"))
        disp_zero = sem("disp_zero")
        x1_out, sent = [sem(f"x1_out{i}") for i in two], [sem(f"sent{i}") for i in two]
        block = ctx.enter_context(nc.Block())

        NORM, SPLIT, ATT, LN, POW, GATE, RANK = 9 + 2 * NB, 2, 2, 1 + 2 * NB + NB, 2, 6, 14
        GUESSED = 8
        NEWTON = 2 * 4 + 2
        STATS = 1 + 2 * NB
        V_OUT = NB
        STACKS = STACK_LOADS
        W_IN = 16 * (1 + 2 * 4)

        def rows(dram, b):
            r = dram[b * N:(b + 1) * N, :] if isinstance(b, int) else dram[bass.ds(b * N, N), :]
            return r.rearrange("(j p) c -> p j c", p=P)

        @block.sync
        def _(sp):
            sp.dma_start(w_qkv[:, :], Wqkv).then_inc(w_qkv_in, 16)

            def early_loads(b):
                if b == -2:
                    sp.dma_start(b_proj[:, :], bproj[None, :].broadcast_to([P, C])).then_inc(w_in, 16)
                    rows_of = Wproj.rearrange("(t u g c) n -> t g u c n", t=2, u=2, c=HD)
                    for t in two:
                        for g in range(4):
                            r = 64 * t + 16 * g
                            sp.dma_start(w_proj[r:r + 16, :], rows_of[t, g]).then_inc(w_in, 16)
                    sp.wait_ge(cleared, 4)
                    for i in two:
                        sp.dma_start(k_st[i][SHIFT_ROW:SHIFT_ROW + 1, :, :], k["ones_bf"][0:H * N // P, :]).then_inc(rows_set, 16)
                if b == 0:
                    for n in range(SLOTS // (5 * P)):
                        part = disp_d[n * 5 * P:(n + 1) * 5 * P, :].rearrange("(p a) c -> p (a c)", a=5)
                        sp.dma_start(part, k["zeros"][:, :]).then_inc(disp_zero, 16)
                if b == 1:
                    for e, (w1_e, w2_e) in enumerate(zip(k["w1"], k["w2"])):
                        sp.dma_start(w1_e[:, :], w1[e]).then_inc(k["w_in"][e], 16)
                        sp.dma_start(w2_e[:, :, :], w2[e].rearrange("(f p) c -> p f c", p=P)).then_inc(k["w_in"][e], 16)

            def step(b, hb, p):
                o = 1 - p
                if real(b + 3):
                    wait_apart(sp, k, (xT_ps, b + 2))
                    sp.dma_start(xin[o][:, :, :], rows(x, b + 3)).then_inc(x_in[o], 16)
                if real(b):
                    if real(b - 2):
                        wait_apart(sp, k, (ln_step, (b - 2) * LN + 1))
                    sp.dma_start(xr[p][:, :, :], rows(x, b)).then_inc(xr_in[p], 16)
                if real(b + 1):
                    sp.wait_ge(lo_sb, b + 2)
                    sp.dma_start(parts_d.rearrange("t p n -> p t n"), parts[o][:, :, :]).then_inc(parts_out, 16)
                    wait_apart(sp, k, (parts_out, (b + 2) * 16),
                                      (scores_ps, b * CHUNKS))
                    load_stacks(sp, parts_d, q_st[o], k_st[o], stacks_in)
                    wait_apart(sp, k, (stacks_in, (b + 2) * 16 * STACKS))
                if isinstance(b, int):
                    early_loads(b)
                if real(b - 1):
                    wait_apart(sp, k, (ln_step, b * LN))
                    sp.dma_start(rows(x1_d, b - 1), x1[o][:, :, :]).then_inc(x1_out[o], 16)

            pipelined(sp, step, 3, 2)
            for i in two:
                sp.wait_ge(x1_out[i], 16 * B // 2)

        @block.tensor
        def _(pe):
            ident, ident_bf = k["ident"], k["ident_bf"]
            pe.wait_ge(w_qkv_in, 16)

            def scores(b, p, c):
                j, kb = divmod(c, NB)
                if c == 0:
                    if isinstance(b, int) and b == 0:
                        pe.wait_ge(rows_set, 32)
                    pe.wait_ge(stacks_in, (b + 1) * 16 * STACKS)
                at_least(pe, probs_sb, b * CHUNKS + c - 1)
                for g in range(4):
                    last = pe.matmul(ps_s[c % 2][:, g * N:(g + 1) * N], k_st[p][:, 4 * j + g, kb * P:(kb + 1) * P],
                                     q_st[p][:, 4 * j + g, :], start=True, stop=True)
                last.then_inc(scores_ps, 1)

            def context(b, p, c):
                j, kb = divmod(c, NB)
                t, u = divmod(j, 2)
                if c == 0:
                    if isinstance(b, int) and b == 0:
                        pe.wait_ge(v_ones, 4)
                    at_least(pe, o_out, b)
                    pe.wait_ge(v_sb, (b + 1) * V_OUT)
                pe.wait_ge(probs_sb, b * CHUNKS + c + 1)
                for g in range(4):
                    f = v_first(j) + 32 * g
                    last = pe.matmul(ps_o[32 * g:32 * g + 32, t * N:(t + 1) * N], vpad[p][:, kb, f:f + 32],
                                     probs[c % RING][:, g * N:(g + 1) * N],
                                     start=u == 0 and kb == 0, stop=u == 1 and kb == NB - 1)
                last.then_inc(pv_done, 1)

            def step(b, hb, p):
                o = 1 - p
                for c in range(CHUNKS):
                    if c < CHUNKS - 1 and real(b):
                        scores(b, p, c + 1)
                    if c == 0 and real(b - 2):
                        pe.wait_ge(ln_step, (b - 1) * LN)
                        for j in range(NB):
                            last = pe.transpose(ps_b[:, j * P:(j + 1) * P], x1[p][:, j, :], ident[:, :])
                        last.then_inc(x1T_ps, 1)
                    if c == 1 and real(b + 2):
                        pe.wait_ge(x_in[p], (hb + 2) * 16)
                        if real(b + 1):
                            pe.wait_ge(split_step, (b + 1) * SPLIT + 1)
                        for j in range(NB):
                            last = pe.transpose(ps_a[0][:, j * P:(j + 1) * P], xin[p][:, j, :], ident[:, :])
                        last.then_inc(xT_ps, 1)
                    if c == 1 and real(b - 2):
                        pe.wait_ge(x1T_sb, b - 1)
                        for j in range(NB):
                            last = pe.matmul(ps_b[:, j * E:(j + 1) * E], x1T[:, j * P:(j + 1) * P], k["gate_T"][:, :],
                                             start=True, stop=True)
                        last.then_inc(logit_ps, 1)
                    if c == 2 and real(b - 2):
                        pe.wait_ge(gate_step, (b - 1) * GATE)
                        at = lambda n: ps_b[:, (2 + n) * E:(3 + n) * E]
                        pe.matmul(at(0), k["tri_bf"][:, :], hot_bf[:, 0, :], start=True, stop=True)
                        pe.matmul(at(1), k["ones_bf"][:, :], hot_bf[:, 0, :], start=True, stop=False)
                        pe.matmul(at(1), k["tri_bf"][:, :], hot_bf[:, 1, :], start=False, stop=True)
                        pe.matmul(at(2), k["ones_bf"][:, :], hot_bf[:, 0, :], start=True, stop=False)
                        pe.matmul(at(2), k["ones_bf"][:, :], hot_bf[:, 1, :], start=False, stop=True)\
                          .then_inc(rank_ps, 1)
                    if c == 3 and real(b - 1):
                        pe.wait_ge(o_out, b)
                        at_least(pe, rank_step, (b - 2) * RANK + 2)
                        for q in range(NB):
                            for t in range(2):
                                last = pe.transpose(ps_b[:, (2 * q + t) * P:(2 * q + t + 1) * P],
                                                    o_sb[:, t * N + q * P:t * N + (q + 1) * P], ident[:, :])
                        last.then_inc(oT_ps, 1)
                    if c == 5 and real(b - 1):
                        pe.wait_ge(att_step, b * ATT)
                        for j in range(NB):
                            last = pe.transpose(ps_b[:, j * P:(j + 1) * P], att[:, j * C:(j + 1) * C], ident[:, :])
                        last.then_inc(attT_ps, 1)
                    if c == 6 and real(b - 1):
                        if isinstance(b, int) and b == 1:
                            pe.wait_ge(w_in, W_IN)
                        pe.wait_ge(attT_sb, b)
                        for j in range(NB):
                            last = pe.matmul(ps_b[:, j * C:(j + 1) * C], attT[:, j * P:(j + 1) * P], w_proj[:, :],
                                             start=True, stop=True)
                        last.then_inc(proj_ps, 1)
                    if c == 0 and real(b - 1):
                        context(b - 1, o, CHUNKS - 1)
                    if c > 0 and real(b):
                        context(b, p, c - 1)
                    if c == 1 and real(b + 2):
                        pe.wait_ge(xT_sb, b + 3)
                        at_least(pe, v_sb, (b + 1) * V_OUT)
                        for j in range(NB):
                            last = pe.matmul(ps_a[j][:, 0:2 * C], xT[p][:, j * P:(j + 1) * P], w_qkv[:, 0:2 * C],
                                             start=True, stop=True)
                        last.then_inc(qk_ps, 1)
                    if c == CHUNKS - 1 and real(b + 1):
                        scores(b + 1, o, 0)
                    if c == 7 and real(b + 2):
                        pe.wait_ge(norm_step, (b + 3) * NORM)
                        for n in range(2 * NB):
                            s, j = divmod(n, NB)
                            last = pe.transpose(ps_a[0][:, n * P:(n + 1) * P], qkn[p][:, j, s * C:(s + 1) * C], ident[:, :])
                        last.then_inc(qkT_ps, 1)
                    if c == 7 and real(b + 1):
                        at_least(pe, norm_step, (b + 3 if real(b + 2) else B) * NORM)
                        for j in range(NB):
                            last = pe.matmul(ps_a[1][:, j * C:(j + 1) * C], xT[o][:, j * P:(j + 1) * P],
                                             w_qkv[:, 2 * C:3 * C], start=True, stop=True)
                        last.then_inc(v_ps, 1)

            pipelined(pe, step, 2, 2)

        @block.scalar
        def _(act):
            def exponentials(b, c):
                act.wait_ge(scores_ps, b * CHUNKS + c + 1)
                at_least(act, pv_done, b * CHUNKS + c + 1 - RING)
                act.activation(probs[c % RING][:, :], ps_s[c % 2][:, :], ACT.Exp, bias=k["minus_bound"][:, :],
                               scale=SCALE).then_inc(probs_sb, 1)

            def step(b, hb, p):
                o = 1 - p
                for c in range(CHUNKS):
                    if c == 1 and real(b + 2):
                        act.wait_ge(xT_ps, b + 3)
                        at_least(act, v_ps, b + 1)
                        act.activation(xT[p][:, :], ps_a[0][:, 0:N], ACT.Copy).then_inc(xT_sb, 1)
                    if c == 2 and real(b + 2):
                        act.wait_ge(qk_ps, b + 3)
                        if real(b + 1):
                            act.wait_ge(norm_step, (b + 1) * NORM + 1)
                        for j in range(NB):
                            act.activation(sq[:, j, :], ps_a[j][:, 0:2 * C], ACT.Square).then_inc(sq_sb, 1)
                    if c < CHUNKS - 1 and real(b):
                        exponentials(b, c + 1)
                    if c == CHUNKS - 1 and real(b + 1):
                        exponentials(b + 1, 0)
                    if c == 0 and real(b - 2):
                        act.wait_ge(x1T_ps, b - 1)
                        at_least(act, logit_ps, b - 2)
                        act.activation(x1T[:, :], ps_b[:, 0:N], ACT.Copy).then_inc(x1T_sb, 1)
                    if c == 0 and real(b - 1):
                        act.wait_ge(pv_done, b * CHUNKS)
                        at_least(act, oT_ps, b - 1)
                        act.activation(o_sb[:, :], ps_o[:, :], ACT.Copy).then_inc(o_out, 1)
                    if c == 3 and real(b - 2):
                        act.wait_ge(gate_step, (b - 2) * GATE + 2)
                        if real(b - 3):
                            act.wait_ge(rank_step, (b - 2) * RANK)
                        act.activation(ex[:, :, :], below[:, :, :], ACT.Exp).then_inc(exp_sb, 1)
                    if c == 5 and real(b - 1):
                        act.wait_ge(attT_ps, b)
                        at_least(act, proj_ps, b - 1)
                        act.activation(attT[:, :], ps_b[:, 0:N], ACT.Copy).then_inc(attT_sb, 1)
                    if c == 7 and real(b + 2):
                        act.wait_ge(qkT_ps, b + 3)
                        at_least(act, parts_out, (b + 1) * 16)
                        act.activation(parts[p][:, 0, :], ps_a[0][:, :], ACT.Copy).then_inc(hi_sb, 1)
                    if c == 7 and real(b + 1):
                        if isinstance(b, int) and b == -1:
                            act.wait_ge(v_ones, 4)
                        act.wait_ge(v_ps, b + 2)
                        at_least(act, pv_done, b * CHUNKS)
                        for j in range(NB):
                            dst = vpad[o][:, j, :].rearrange("p (q g w) -> p q g w", q=QUADS, w=VW)
                            act.activation(dst[:, :, 0:8:2, 0:HD],
                                           ps_a[1][:, j * C:(j + 1) * C].rearrange("p (q g w) -> p q g w", q=QUADS, w=HD),
                                           ACT.Copy).then_inc(v_sb, 1)

            pipelined(act, step, 2, 2, first=3)

        @block.vector
        def _(dve):
            for i in two:
                dve.memset(q_st[i][:, :, :].bitcast(FP32), 0.0).then_inc(cleared, 1)
            before, dump = k["slots_before"], k["dump"]
            for j in range(NB):
                dve.tensor_copy(slots[:, j, 1, :], k["slots_end"][:, :]).then_inc(ends_set, 1)
            dve.wait_ge(ends_set, NB)
            norm, split, attn = Steps(dve, norm_step, NORM), Steps(dve, split_step, SPLIT), Steps(dve, att_step, ATT)
            ln, gate, route = Steps(dve, ln_step, LN), Steps(dve, gate_step, GATE), Steps(dve, rank_step, RANK)
            over = lambda a, n: a.unsqueeze(2).broadcast_to([P, a.shape[1], n])
            each = lambda a: a.unsqueeze(1).broadcast_to([P, NB, a.shape[1]])

            def gates(b):
                s = gate.batch(b)
                dve.wait_ge(logit_ps, b + 1)
                lg = ps_b[:, 0:NB * E].rearrange("p (j e) -> p j e", j=NB)
                s.did(dve.tensor_reduce(top[:, :], lg, AX.X, ALU.max))
                s.wait()
                at_least(dve, exp_sb, b)
                s.did(dve.tensor_tensor(below[:, :, :], lg, over(top[:, :], E), ALU.subtract))
                s.wait()
                s.did(dve.scalar_tensor_tensor(cand[:, :, :], below[:, :, :], 0.0, each(k["backwards"][:, :]),
                                               ALU.is_ge, ALU.mult))
                s.wait()
                s.did(dve.tensor_reduce(first[:, :], cand[:, :, :], AX.X, ALU.max))
                s.wait()
                s.did(dve.tensor_tensor(hot[:, :, :], cand[:, :, :], over(first[:, :], E), ALU.is_equal))
                s.wait()
                at_least(dve, rank_ps, b)
                s.did(dve.tensor_copy(hot_bf[:, :, :], hot[:, :, :]))
                s.end()

            def ranks(b):
                s = route.batch(b)
                dve.wait_ge(rank_ps, b + 1)
                s.did(dve.tensor_tensor(slots[:, :, 0, :], ps_b[:, 2 * E:4 * E].rearrange("p (j e) -> p j e", j=NB),
                                        each(before[:, :]), ALU.add))
                s.wait()
                s.did(dve.tensor_tensor(before[:, :], ps_b[:, 4 * E:5 * E], before[:, :], ALU.add))

            def routes(b, hb, p):
                s = route
                slot, limit = picked[:, :, 0], picked[:, :, 1]
                s.did(dve.tensor_tensor(choices[:, :, :, :], slots[:, :, :, :],
                                        hot[:, :, :].unsqueeze(2).broadcast_to([P, NB, 2, E]), ALU.mult))
                s.wait()
                s.did(dve.tensor_reduce(picked[:, :, :], choices[:, :, :, :], AX.X, ALU.add))
                s.wait()
                s.did(dve.tensor_tensor(keep[:, :], limit, slot, ALU.is_gt))
                s.wait()
                s.did(dve.tensor_tensor(kept_slot[:, :], slot, keep[:, :], ALU.mult))
                s.did(dve.tensor_scalar(spare[:, :], keep[:, :], -1.0, 1.0, ALU.mult, ALU.add))
                s.wait()
                cols = slice(b * NB, (b + 1) * NB) if isinstance(b, int) else bass.ds(b * NB, NB)
                s.did(dve.tensor_copy(k["fetch"][:, cols], kept_slot[:, :]))
                s.did(dve.tensor_tensor(spare[:, :], spare[:, :], dump[:, :], ALU.mult))
                s.wait()
                at_least(dve, sent[p], 16 * NB * hb)
                s.did(dve.tensor_tensor(sidx[p][:, :], kept_slot[:, :], spare[:, :], ALU.add))
                s.did(dve.tensor_scalar(dump[:, :], dump[:, :], float(N), None, ALU.add))
                dve.wait_ge(exp_sb, b + 1)
                s.did(dve.tensor_reduce(esum[:, :], ex[:, :, :], AX.X, ALU.add))
                s.wait()
                s.did(dve.reciprocal(prob[:, :], esum[:, :]))
                s.wait()
                s.did(dve.tensor_tensor(k["weight"][:, cols], prob[:, :], keep[:, :], ALU.mult))
                s.end()

            def step(b, hb, p):
                o = 1 - p
                if real(b + 1):
                    s = split.batch(b + 1)
                    dve.wait_ge(hi_sb, b + 2)
                    at_least(dve, lo_sb, b + 1)
                    s.did(dve.tensor_tensor(rest[:, :], ps_a[0][:, :], parts[o][:, 0, :], ALU.subtract))
                    s.wait()
                    s.did(dve.tensor_copy(parts[o][:, 1, :], rest[:, :]))
                    s.end()
                if real(b - 2):
                    gates(b - 2)
                    ranks(b - 2)
                if real(b + 2):
                    s = norm.batch(b + 2)
                    dve.wait_ge(sq_sb, (b + 3) * NB)
                    s.did(dve.tensor_reduce(ms[:, :], sq[:, :, :].rearrange("p j (n w) -> p (j n) w", w=HD), AX.X, ALU.add))
                    s.wait()
                    s.did(dve.tensor_scalar(ms[:, :], ms[:, :], 1.0 / HD, 1e-30, ALU.mult, ALU.max))
                    s.wait()
                    s.did(dve.tensor_scalar(nr_t[:, :].bitcast(I32), ms[:, :].bitcast(I32), 1, None, ALU.logical_shift_right))
                    s.did(dve.tensor_scalar(half_ms[:, :], ms[:, :], -0.5, None, ALU.mult))
                    s.wait()
                    s.did(dve.tensor_scalar(nr_y[:, :].bitcast(I32), nr_t[:, :].bitcast(I32), -1.0, GUESS, ALU.mult, ALU.add))
                    s.wait()
                    s.did(dve.tensor_tensor(nr_t[:, :], nr_y[:, :], nr_y[:, :], ALU.mult))
                    s.wait()
                    s.did(dve.tensor_tensor(nr_t[:, :], nr_t[:, :], half_ms[:, :], ALU.mult))
                    s.wait()
                    s.did(dve.scalar_tensor_tensor(nr_y[:, :], nr_t[:, :], 1.5, nr_y[:, :], ALU.add, ALU.mult))
                if real(b - 1):
                    s = attn.batch(b - 1)
                    dve.wait_ge(oT_ps, b)
                    ctxs = ps_b[:, :].rearrange("p (n w) -> p n w", w=VW)
                    s.did(dve.reciprocal(rden[:, :], ctxs[:, :, HD]))
                    s.wait()
                    at_least(dve, attT_ps, b - 1)
                    s.did(dve.tensor_tensor(att[:, :].rearrange("p (n w) -> p n w", w=HD), ctxs[:, :, 0:HD],
                                            over(rden[:, :], HD), ALU.mult))
                    s.end()
                if real(b - 2):
                    routes(b - 2, hb - 1, p)
                if real(b - 1):
                    s = ln.batch(b - 1)
                    dve.wait_ge(proj_ps, b)
                    dve.wait_ge(xr_step, b)
                    s.did(dve.tensor_tensor(y[:, :, :], ps_b[:, 0:NB * C].rearrange("p (j c) -> p j c", j=NB),
                                            xr[o][:, :, :], ALU.add))
                    s.wait()
                    for j in range(NB):
                        s.did(dve.bn_stats(stats[:, j, :], y[:, j, :]))
                    wait_apart(dve, k, (s.sem, s.base + s.n),
                                       (pow_step, (b - 1) * POW))
                    for j in range(NB):
                        s.did(dve.bn_aggr(mv[:, j, :], stats[:, j, :]))
                if real(b + 2):
                    s = norm
                    dve.wait_ge(newton_step, (b + 3) * NEWTON)
                    s.did(dve.reciprocal(nr_t[:, :], rms[:, :]))
                    s.wait()
                    at_least(dve, qkT_ps, b + 1)
                    for j in range(NB):
                        scale = nr_t[:, 2 * H * j:2 * H * (j + 1)].rearrange("p (s h) -> p s h", h=H)
                        s.did(dve.tensor_tensor(qkn[p][:, j, :].rearrange("p (s w h) -> p s h w", s=2, h=H),
                                                ps_a[j][:, 0:2 * C].rearrange("p (s h w) -> p s h w", s=2, w=HD),
                                                scale.unsqueeze(3).broadcast_to([P, 2, H, HD]), ALU.mult))
                    s.wait()
                    for j in range(NB):
                        kn = qkn[p][:, j, C:2 * C].rearrange("p (w h) -> p w h", h=H)
                        s.did(dve.tensor_tensor(kn, kn, k["qks"][:, :].unsqueeze(2).broadcast_to([P, HD, H]), ALU.mult))
                    s.end()
                if real(b - 1):
                    s = ln
                    dve.wait_ge(pow_step, b * POW)
                    at_least(dve, x1_out[o], 16 * (hb - 1 + p))
                    at_least(dve, sent[o], 16 * NB * (hb - 1 + p))
                    at_least(dve, x1T_ps, b - 2)
                    for j in range(NB):
                        s.did(dve.tensor_scalar(x1[o][:, j, :], y[:, j, :], mv[:, j, 0:1], rstd[:, j:j + 1],
                                                ALU.subtract, ALU.mult))
                    s.end()

            pipelined(dve, step, 2, 2, first=3)

        @block.gpsimd
        def _(pool):
            for i in two:
                pool.memset(k_st[i][:, :, :].bitcast(FP32), 0.0).then_inc(cleared, 1)
            for i in two:
                pool.memset(vpad[i][:, :, :], 0.0).then_inc(v_ones, 1)
            pool.wait_ge(v_ones, 2)
            for i in two:
                ones = vpad[i][:, :, :].rearrange("p j (q g w) -> p (j q) g w", q=QUADS, w=VW)[:, :, 0:8:2, HD]
                pool.memset(ones, 1.0).then_inc(v_ones, 1)

            newton, half, eps = Steps(pool, newton_step, NEWTON), k["three_halves"][:, 0:G2], k["eps_rms"][:, 0:G2]

            def step(b, hb, p):
                o = 1 - p
                if real(b + 1):
                    pool.wait_ge(split_step, (b + 2) * SPLIT)
                    pool.tensor_tensor(parts[o][:, 2, :], rest[:, :], parts[o][:, 1, :], ALU.subtract).then_inc(lo_sb, 1)
                if real(b):
                    if isinstance(b, int) and b == 0:
                        pool.wait_ge(w_in, W_IN)
                    pool.wait_ge(xr_in[p], (hb + 1) * 16)
                    pool.tensor_tensor(xr[p][:, :, :], xr[p][:, :, :],
                                       b_proj[:, :].unsqueeze(1).broadcast_to([P, NB, C]), ALU.add).then_inc(xr_step, 1)
                if real(b + 2):
                    s = newton.batch(b + 2)
                    pool.wait_ge(norm_step, (b + 2) * NORM + GUESSED)
                    for _ in range(2):
                        s.did(pool.tensor_tensor(nr_t[:, :], nr_y[:, :], nr_y[:, :], ALU.mult))
                        s.wait()
                        s.did(pool.tensor_tensor(nr_t[:, :], nr_t[:, :], half_ms[:, :], ALU.mult))
                        s.wait()
                        s.did(pool.tensor_tensor(nr_t[:, :], nr_t[:, :], half, ALU.add))
                        s.wait()
                        s.did(pool.tensor_tensor(nr_y[:, :], nr_y[:, :], nr_t[:, :], ALU.mult))
                        s.wait()
                    s.did(pool.tensor_tensor(rms[:, :], ms[:, :], nr_y[:, :], ALU.mult))
                    s.wait()
                    s.did(pool.tensor_tensor(rms[:, :], rms[:, :], eps, ALU.add))
                    s.end()
                if real(b - 1):
                    wait_apart(pool, k, (ln_step, (b - 1) * LN + STATS))
                    pool.tensor_scalar(veps[:, :], mv[:, :, 1], EPS_LN, None, ALU.add).then_inc(pow_step, 1)
                    pool.wait_ge(pow_step, (b - 1) * POW + 1)
                    pool.tensor_tensor(rstd[:, :], veps[:, :], k["minus_half"][:, 0:NB], ALU.pow).then_inc(pow_step, 1)
                if real(b - 2):
                    if isinstance(b, int) and b == 2:
                        pool.wait_ge(disp_zero, 16 * (SLOTS // (5 * P)))
                    wait_apart(pool, k, (rank_step, (b - 1) * RANK))
                    for j in range(NB):
                        pool.indirect_dma_start(out=disp_d, out_offset=bass.IndirectOffsetOnAxis(ap=sidx[p][:, j:j + 1], axis=0),
                                                in_=x1[p][:, j, :], in_offset=None).then_inc(sent[p], 16)

            pipelined(pool, step, 2, 2)
            for i in two:
                pool.wait_ge(sent[i], 16 * NB * B // 2)


def second_layer_weights(sb):
    C2, C4 = C // 2, C // 4
    return {
        "w_qk_in": sb("w_qk_in", [P, 2 * C], FP32), "w_v": sb("w_v", [P, H * DV], FP32),
        "w_o": sb("w_o", [P, PAIRS, C], FP32),
        "sums": sb("sums", [P, QUADS, 32], FP32),
        "cn_w": [sb("cn_w1", [P, C], FP32), sb("cn_w2", [P, C2], FP32),
                 sb("cn_w3", [P, 2 * C4], FP32),
                 sb("cn_w4", [P, 4], FP32)],
        "cn_b": [sb(f"cn_b{i}", [P, 1], FP32) for i in (1, 2, 3, 4)],
        "gc_w": [sb("gc_w1", [P, C2], FP32), sb("gc_w2", [C2, C4], FP32), sb("gc_w3", [C4, 1], FP32)],
        "gc_b": [sb("gc_b1", [C2, 1], FP32), sb("gc_b2", [C4, 1], FP32), sb("gc_b3", [P, 1], FP32)],
        "spread": sb("spread", [P, 1], FP32),
    }


def load_second_layer(pool, k, a, cleared, loaded):
    load = lambda dst, src: pool.dma_start(dst, src).then_inc(loaded, 16)
    column, repeated = (lambda v: v.unsqueeze(1)), (lambda v: v[None, :].broadcast_to([P, 1]))
    (w1, w2, w3, w4), (b1, b2, b3, b4) = k["cn_w"], k["cn_b"]
    (g1, g2, g3), (gb1, gb2, gb3) = k["gc_w"], k["gc_b"]
    pool.memset(k["sums"][:, :, :], 0.0).then_inc(cleared, 1)
    pool.memset(w3[:, :], 0.0).then_inc(cleared, 1)
    pool.memset(w4[:, :], 0.0).then_inc(cleared, 1)
    pool.wait_ge(cleared, 3)
    for j in range(QUADS):
        pool.memset(k["sums"][:, j, j:32:QUADS], 1.0).then_inc(cleared, 1)
    load(k["w_qk_in"][:, 0:C], a["L1_attn_Wq"])
    load(k["w_qk_in"][:, C:2 * C], a["L1_attn_Wk"])
    load(k["w_v"][:, :], a["L1_attn_Wv"])
    load(k["w_o"][:, :, :], a["L1_attn_Wo"].rearrange("(i p) c -> p i c", p=P))
    load(w1[:, :], a["L1_ffn_cn_w1"])
    load(w2[:, :], a["L1_ffn_cn_w2"])
    load(b1[:, :], column(a["L1_ffn_cn_b1"]))
    for u in range(2):
        load(b2[u * C // 2:(u + 1) * C // 2, :], column(a["L1_ffn_cn_b2"]))
        load(w3[u * C // 2:(u + 1) * C // 2, u * C // 4:(u + 1) * C // 4], a["L1_ffn_cn_w3"])
    for g in range(4):
        load(b3[g * C // 4:(g + 1) * C // 4, :], column(a["L1_ffn_cn_b3"]))
        load(w4[g * C // 4:(g + 1) * C // 4, g:g + 1], a["L1_ffn_cn_w4"])
    load(b4[:, :], repeated(a["L1_ffn_cn_b4"]))
    load(g1[:, :], a["L1_ffn_gc_w1"])
    load(g2[:, :], a["L1_ffn_gc_w2"])
    load(g3[:, :], a["L1_ffn_gc_w3"])
    load(gb1[:, :], column(a["L1_ffn_gc_b1"]))
    load(gb2[:, :], column(a["L1_ffn_gc_b2"]))
    load(gb3[:, :], repeated(a["L1_ffn_gc_b3"]))
    load(k["spread"][:, :], repeated(a["L1_ffn_adaptive_range"]))
    pool.wait_ge(loaded, 16 * (7 + 2 * 2 + 2 * 4 + 8))
    pool.wait_ge(cleared, 3 + QUADS)


def experts(nc, k, a, disp_d, eout_d):
    TILES = [(t, min(P, CAP - t)) for t in range(0, CAP, P)]
    FULL = CAP // P
    with ExitStack() as ctx:
        sb = lambda name, shape, dt: ctx.enter_context(nc.sbuf_tensor("ex_" + name, shape, dt))
        pb = lambda name, shape, dt: ctx.enter_context(nc.psum_tensor("ex_" + name, shape, dt))
        sem = lambda name: ctx.enter_context(nc.semaphore("ex_" + name))
        two = range(2)
        xe = [sb(f"xe{i}", [P, len(TILES), C], FP32) for i in two]
        xeT = [sb(f"xeT{i}", [P, CAP], FP32) for i in two]
        hT = [sb(f"hT{i}", [P, FC, CAP], FP32) for i in two]
        ye = [sb(f"ye{i}", [P, len(TILES), C], FP32) for i in two]
        ps_x = pb("ps_x", [P, 512], FP32)
        ps_h = [pb(f"ps_h{i}", [P, FC // 2, 512], FP32) for i in two]
        ps_y = [pb(f"ps_y{i}", [P, 512], FP32) for i in two]
        xe_in, ye_out = [sem(f"xe_in{i}") for i in two], [sem(f"ye_out{i}") for i in two]
        cleared, later_in = sem("cleared"), sem("later_in")
        xeT_ps, xeT_sb, h_ps, h_sb, y_ps, y_sb = (sem(n) for n in ("xeT_ps", "xeT_sb", "h_ps", "h_sb", "y_ps", "y_sb"))
        block = ctx.enter_context(nc.Block())
        w1_sb, w2_sb, w_in = k["w1"], k["w2"], k["w_in"]
        W = len(w1_sb)
        w1, w2 = a["L0_ffn_w1"], a["L0_ffn_w2"]
        real = lambda e: not isinstance(e, int) or 0 <= e < E

        def expert(dram, e):
            return dram[e] if isinstance(e, int) else dram[bass.ds(e, 1)].rearrange("a b c -> (a b) c")

        def tiles(dram, e, sbuf):
            r = dram[e * CAP:(e + 1) * CAP, :] if isinstance(e, int) else dram[bass.ds(e * CAP, CAP), :]
            yield r[0:FULL * P, :].rearrange("(t p) c -> p t c", p=P), sbuf[:, 0:FULL, :]
            if CAP % P:
                yield r[FULL * P:CAP, :], sbuf[0:CAP % P, FULL, :]

        LOADS = 16 * len(list(tiles(disp_d, 0, xe[0])))
        ye_parts = [(slice(0, P), slice(0, FULL))] + ([(slice(0, CAP % P), slice(FULL, FULL + 1))] if CAP % P else [])

        @block.sync
        def _(sp):
            def step(e, he, q):
                p = q % 2
                if real(e + 3):
                    wait_apart(sp, k, (xeT_ps, e + 2))
                    for dram, sbuf in tiles(disp_d, e + 3, xe[1 - p]):
                        sp.dma_start(sbuf, dram).then_inc(xe_in[1 - p], 16)
                if real(e):
                    wait_apart(sp, k, (y_sb, (e + 1) * len(ye_parts)))
                    for dram, sbuf in tiles(eout_d, e, ye[p]):
                        sp.dma_start(dram, sbuf).then_inc(ye_out[p], 16)
                if real(e) and real(e + W):
                    wait_apart(sp, k, (y_ps, e + 1))
                    sp.dma_start(w1_sb[q][:, :], expert(w1, e + W)).then_inc(w_in[q], 16)
                    sp.dma_start(w2_sb[q][:, :, :], expert(w2, e + W).rearrange("(f p) c -> p f c", p=P)).then_inc(w_in[q], 16)

            pipelined(sp, step, 3, 0, E, W)
            for i in two:
                sp.wait_ge(ye_out[i], LOADS * E // 2)

        @block.tensor
        def _(pe):
            def step(e, he, q):
                p, o = q % 2, 1 - q % 2
                half = lambda d: (he * W + q + d) // 2 if isinstance(he, int) else he * (W // 2) + (q + d) // 2
                if real(e + 1):
                    qn = (q + 1) % W
                    pe.wait_ge(w_in[qn], ((he + (q + 1) // W) + 1) * 32)
                    pe.wait_ge(xeT_sb, e + 2)
                    for f in range(FC):
                        if f % 2 == 0:
                            at_least(pe, h_sb, (e + 1) * 2 - 1 + f // 2)
                        last = pe.matmul(ps_h[f // 2][:, f % 2, 0:CAP], w1_sb[qn][:, f * P:(f + 1) * P], xeT[o][:, :],
                                         start=True, stop=True)
                        if f % 2:
                            last.then_inc(h_ps, 1)
                if real(e + 2):
                    pe.wait_ge(xe_in[p], (half(2) + 1) * LOADS)
                    at_least(pe, xeT_sb, e + 2)
                    for t, n in TILES:
                        last = pe.transpose(ps_x[:, t:t + n], xe[p][0:n, t // P, :], k["ident"][0:n, 0:n])
                    last.then_inc(xeT_ps, 1)
                if real(e):
                    pe.wait_ge(h_sb, (e + 1) * 2)
                    at_least(pe, y_sb, (e - 1) * len(ye_parts))
                    for t, n in TILES:
                        for f in range(FC):
                            last = pe.matmul(ps_y[p][0:n, t // P * C:(t // P + 1) * C], hT[p][:, f, t:t + n],
                                             w2_sb[q][:, f, :], start=f == 0, stop=f == FC - 1)
                    last.then_inc(y_ps, 1)

            pipelined(pe, step, 2, 0, E, W, first=2)

        @block.scalar
        def _(act):
            def step(e, he, q):
                o = 1 - q % 2
                if real(e + 1):
                    for i in two:
                        act.wait_ge(h_ps, (e + 1) * 2 + i + 1)
                        at_least(act, y_ps, e)
                        act.activation(hT[o][:, 2 * i:2 * i + 2, :], ps_h[i][:, :, 0:CAP], ACT.Gelu_apprx_tanh).then_inc(h_sb, 1)

            pipelined(act, step, 2, 0, E, W, first=1)

        @block.gpsimd
        def _(pool):
            load_second_layer(pool, k, a, cleared, later_in)

        @block.vector
        def _(dve):
            def step(e, he, q):
                p = q % 2
                half = lambda d: (he * W + q + d) // 2 if isinstance(he, int) else he * (W // 2) + (q + d) // 2
                if real(e + 2):
                    dve.wait_ge(xeT_ps, e + 3)
                    at_least(dve, h_ps, (e + 1) * 2)
                    dve.tensor_copy(xeT[p][:, :], ps_x[:, 0:CAP]).then_inc(xeT_sb, 1)
                if real(e):
                    dve.wait_ge(y_ps, e + 1)
                    at_least(dve, ye_out[p], LOADS * half(0))
                    for r, c in ye_parts:
                        dve.tensor_copy(ye[p][r, c, :], ps_y[p][r, c.start * C:c.stop * C].rearrange("p (t c) -> p t c", c=C))\
                           .then_inc(y_sb, 1)

            pipelined(dve, step, 2, 0, E, W, first=2)


def l1_layer(nc, k, parts_d, rden_d, x1_d, eout_d, x2_d):
    STACKS = STACK_LOADS + 1

    with ExitStack() as ctx:
        sb = lambda name, shape, dt: ctx.enter_context(nc.sbuf_tensor("l1_" + name, shape, dt))
        pb = lambda name, shape, dt: ctx.enter_context(nc.psum_tensor("l1_" + name, shape, dt))
        sem = lambda name: ctx.enter_context(nc.semaphore("l1_" + name))
        two = range(2)
        w_qk_in, w_v, w_o, sums = k["w_qk_in"], k["w_v"], k["w_o"], k["sums"]
        w_qk = sb("w_qk", [P, 2 * C], FP32)
        index = sb("index", [P, NB], U32)
        eg = [sb(f"eg{i}", [P, NB, C], FP32) for i in two]
        xa = [sb(f"xa{i}", [P, NB, C], FP32) for i in two]
        y2 = sb("y2", [P, NB, C], FP32)
        x2 = [sb(f"x2_{i}", [P, NB, C], FP32) for i in two]
        xT = [sb(f"xT{i}", [P, N], FP32) for i in two]
        stats2, stats3 = sb("stats2", [P, NB, 6], FP32), sb("stats3", [P, NB, 6], FP32)
        mv2, mv3 = sb("mv2", [P, NB, 2], FP32), sb("mv3", [P, NB, 2], FP32)
        veps2, veps3 = sb("veps2", [P, NB], FP32), sb("veps3", [P, NB], FP32)
        rstd2, rstd3 = sb("rstd2", [P, NB], FP32), sb("rstd3", [P, NB], FP32)
        parts = [sb(f"parts{i}", [P, 3, 2 * N], BF16) for i in two]
        rest = sb("rest", [P, 2 * N], FP32)
        q_st, k_st = k["q_st"], k["k_st"]
        values = [sb(f"values{i}", [P, NB, H * DV], FP32) for i in two]
        neg_max = sb("neg_max", [P, NB, H], BF16)
        max_rows = [sb(f"max_rows{i}", [H // 2, N], BF16) for i in two]
        p0 = [sb(f"p0_{i}", [P, 4, N], FP32) for i in two]
        p1 = [sb(f"p1_{i}", [P, 4, P], FP32) for i in two]
        ctxs = [sb(f"ctx{i}", [P, PAIRS, N], FP32) for i in two]
        rden = sb("rden", [P, N], FP32)
        rrep = sb("rrep", [P, PAIRS, N], FP32)
        xr = [sb(f"xr{i}", [P, NB, C], FP32) for i in two]
        y3 = sb("y3", [P, NB, C], FP32)
        st0 = pb("st0", [P, 4, N], FP32)
        st1 = pb("st1", [P, 4, P], FP32)
        sm1 = pb("sm1", [P, 4, N], FP32)
        sm0 = pb("sm0", [P, 4, P], FP32)
        ps_c = pb("ps_c", [P, 2, N], FP32)
        ps_d = pb("ps_d", [P, 512], FP32)

        w_turned = sem("w_turned")
        index_set, fetched, xa_in = sem("index_set"), [sem(f"fetched{i}") for i in two], [sem(f"xa_in{i}") for i in two]
        x2_step, pow2, pow3, x3_step = (sem(n) for n in ("x2_step", "pow2", "pow3", "x3_step"))
        x2_out = [sem(f"x2_out{i}") for i in two]
        xr_in = [sem(f"xr_in{i}") for i in two]
        xT_ps, xT_sb, qk_ps, hi_sb, split_step, lo_sb = (sem(n) for n in ("xT_ps", "xT_sb", "qk_ps", "hi_sb", "split_step", "lo_sb"))
        parts_out, stacks_in, v_ps, v_sb = (sem(n) for n in ("parts_out", "stacks_in", "v_ps", "v_sb"))
        sm_ps, max_done, rows_ps, rows_sb = (sem(n) for n in ("sm_ps", "max_done", "rows_ps", "rows_sb"))
        rows_in = [sem(f"rows_in{i}") for i in two]
        st_ps, p_sb, masked, ctx_ps, ctx_sb = (sem(n) for n in ("st_ps", "p_sb", "masked", "ctx_ps", "ctx_sb"))
        rden_sb, rden_out, rrep_in, divided, wo_ps = (sem(n) for n in ("rden_sb", "rden_out", "rrep_in", "divided", "wo_ps"))
        block = ctx.enter_context(nc.Block())
        turned = lambda bank: bank[0:H // 2, :, :].rearrange("p a b -> p (a b)").bitcast(BF16)[:, 0:N]
        X2, X3, SPLIT, POW, V_OUT = 4 * NB, 1 + 3 * NB, 2, 2, 2 * NB

        def rows(dram, b):
            r = dram[b * N:(b + 1) * N, :] if isinstance(b, int) else dram[bass.ds(b * N, N), :]
            return r.rearrange("(j p) c -> p j c", p=P)

        @block.sync
        def _(sp):
            def step(b, hb, p):
                o = 1 - p
                if real(b + 1):
                    sp.wait_ge(lo_sb, b + 2)
                    sp.dma_start(parts_d.rearrange("t p n -> p t n"), parts[o][:, :, :]).then_inc(parts_out, 16)
                    wait_apart(sp, k, (parts_out, (b + 2) * 16),
                                      (st_ps, b * 2 * QUADS))
                    sp.dma_start(q_st[o][SHIFT_ROW:SHIFT_ROW + 1, :, :],
                                 k["zeros"][0:H, 0:N // 2].bitcast(BF16)).then_inc(stacks_in, 16)
                    load_stacks(sp, parts_d, q_st[o], k_st[o], stacks_in)
                    wait_apart(sp, k, (stacks_in, (b + 2) * 16 * STACKS))
                if real(b + 2):
                    wait_apart(sp, k, (x2_step, (b + 3) * X2))
                    sp.dma_start(rows(x2_d, b + 2), x2[p][:, :, :]).then_inc(x2_out[p], 16)
                if real(b):
                    wait_apart(sp, k, (x2_out[p], (hb + 1) * 16),
                                      (x3_step, (b - 2) * X3 + 1))
                    sp.dma_start(xr[p][:, :, :], rows(x2_d, b)).then_inc(xr_in[p], 16)
                if real(b + 3):
                    wait_apart(sp, k, (x2_step, (b + 1) * X2 + NB))
                    sp.dma_start(xa[o][:, :, :], rows(x1_d, b + 3)).then_inc(xa_in[o], 16)
                if real(b):
                    sp.wait_ge(rden_sb, b + 1)
                    sp.dma_start(rden_d, rden[:, :]).then_inc(rden_out, 16)
                    wait_apart(sp, k, (rden_out, (b + 1) * 16),
                                      (divided, b * QUADS))
                    src = rden_d.rearrange("(i u r) n -> u r i n", i=2, u=2)
                    for u in two:
                        for i in two:
                            sp.dma_start(rrep[u * DV:(u + 1) * DV, i:PAIRS:2, :],
                                         src[u, 0:QUADS, i, :].unsqueeze(0).broadcast_to([DV, QUADS, N])).then_inc(rrep_in, 16)

            pipelined(sp, step, 3, 1, first=2)
            for i in two:
                sp.wait_ge(x2_out[i], 16 * B // 2)

        @block.tensor
        def _(pe):
            ident, ident_bf = k["ident"], k["ident_bf"]
            pe.wait_ge(w_turned, 1)

            def values_of(b, p, n):
                j, half = divmod(n, 2)
                if n == 0:
                    at_least(pe, ctx_sb, b * QUADS)
                else:
                    pe.wait_ge(v_sb, b * V_OUT + n)
                pe.matmul(ps_c[:, :, :], xT[p][:, j * P:(j + 1) * P],
                          w_v[:, half * 512:(half + 1) * 512], start=True, stop=True).then_inc(v_ps, 1)

            def scores_by_key(b, p, j):
                if j % 2 == 0:
                    pe.wait_ge(rows_in[j // 2], (b + 1) * 16)
                if j == 0:
                    at_least(pe, xT_sb, b + 2 if real(b + 1) else B)
                    at_least(pe, split_step, (b + 1) * SPLIT + 1 if real(b + 1) else B * SPLIT)
                else:
                    pe.wait_ge(p_sb, (b * QUADS + j) * 2)
                for g in range(4):
                    h = 4 * j + g
                    last = pe.matmul(st0[:, g, :], k_st[p][:, h, 0:P], q_st[p][:, h, :], start=True, stop=True)
                last.then_inc(st_ps, 1)
                for g in range(4):
                    h = 4 * j + g
                    last = pe.matmul(st1[:, g, :], k_st[p][:, h, P:N], q_st[p][:, h, P:N], start=True, stop=True)
                last.then_inc(st_ps, 1)

            def scores_by_query(b, p, j):
                if j == 0:
                    pe.wait_ge(stacks_in, (b + 1) * 16 * STACKS)
                at_least(pe, max_done, (b * QUADS + j) * 2)
                for half in two:
                    pe.matmul(sm1[:, 2 * half:2 * half + 2, P:N], ident_bf[:, :],
                              k["causal"][:, 0:2 * P].rearrange("p (a b) -> p a b", b=P),
                              start=True, stop=False, skip_group_check=True)
                    for g in (2 * half, 2 * half + 1):
                        last = pe.matmul(sm1[:, g, :], q_st[p][:, 4 * j + g, P:N], k_st[p][:, 4 * j + g, :],
                                         start=False, stop=g % 2 == 1, skip_group_check=True)
                last.then_inc(sm_ps, 1)
                if j == 0:
                    at_least(pe, rows_sb, b * 2)
                    at_least(pe, x3_step, (b - 2) * X3 + 1)
                pe.matmul(sm0[:, :, :], ident_bf[:, :], k["causal"][:, :].rearrange("p (a b) -> p a b", b=P),
                          start=True, stop=False, skip_group_check=True)
                for g in range(4):
                    last = pe.matmul(sm0[:, g, :], q_st[p][:, 4 * j + g, 0:P], k_st[p][:, 4 * j + g, 0:P],
                                     start=False, stop=g == 3, skip_group_check=True)
                last.then_inc(sm_ps, 1)

            def maxima_by_head(b, half, bank):
                pe.wait_ge(max_done, (b * 2 + half + 1) * QUADS)
                for j in range(NB):
                    last = pe.transpose(turned(bank)[:, j * P:(j + 1) * P], neg_max[:, j, half * H // 2:(half + 1) * H // 2],
                                        ident_bf[:, :])
                last.then_inc(rows_ps, 1)

            def project(b, o, j):
                if j == 0:
                    pe.wait_ge(divided, b * QUADS)
                    if real(b):
                        pe.wait_ge(rows_sb, (b + 1) * 2)
                for i in range(PAIRS):
                    last = pe.matmul(sm0[:, j, :], ctxs[o][:, i, j * P:(j + 1) * P], w_o[:, i, :],
                                     start=i == 0, stop=i == PAIRS - 1)
                if j == NB - 1:
                    last.then_inc(wo_ps, 1)

            def context(b, p, j):
                pe.wait_ge(masked, (b * QUADS + j + 1) * 2)
                if j == 0:
                    pe.wait_ge(v_sb, (b + 1) * V_OUT)
                at_least(pe, ctx_sb, b * QUADS + j)
                for i in two:
                    for kb, pr, q0 in ((0, p0[j % 2], 0), (1, p1[j % 2], P)):
                        for u in two:
                            h = 4 * j + 2 * i + u
                            last = pe.matmul(ps_c[u * DV:(u + 1) * DV, i, q0:N], values[p][:, kb, h * DV:(h + 1) * DV],
                                             pr[:, 2 * i + u, :], start=kb == 0, stop=kb == 1)
                if j == 0:
                    at_least(pe, rden_sb, b)
                for kb, pr, q0 in ((0, p0[j % 2], 0), (1, p1[j % 2], P)):
                    for g in range(4):
                        last = pe.matmul(ps_d[32 * g:32 * g + 32, q0:N], sums[:, j, :], pr[:, g, :],
                                         start=j == 0 and kb == 0, stop=j == QUADS - 1 and kb == 1)
                last.then_inc(ctx_ps, 1)

            def step(b, hb, p):
                o = 1 - p
                if real(b):
                    scores_by_key(b, p, 1)
                    context(b, p, 0)
                    scores_by_key(b, p, 2)
                    context(b, p, 1)
                if real(b - 1):
                    project(b, o, 0)
                if real(b):
                    scores_by_key(b, p, 3)
                if real(b - 1):
                    project(b, o, 1)
                if real(b + 1):
                    scores_by_query(b + 1, o, 0)
                if real(b):
                    context(b, p, 2)
                if real(b + 1):
                    scores_by_query(b + 1, o, 1)
                if real(b):
                    context(b, p, 3)
                if real(b + 1):
                    at_least(pe, p_sb, (b + 1) * 2 * QUADS)
                    maxima_by_head(b + 1, 0, st1)
                    scores_by_query(b + 1, o, 2)
                if real(b + 2):
                    pe.wait_ge(x2_step, (b + 3) * X2)
                    at_least(pe, p_sb, (b + 1) * 2 * QUADS)
                    if real(b + 1):
                        pe.wait_ge(rows_sb, b * 2 + 3)
                    for j in range(NB):
                        last = pe.transpose(st1[:, j, :], x2[p][:, j, :], ident[:, :])
                    last.then_inc(xT_ps, 1)
                if real(b + 1):
                    values_of(b + 1, o, 0)
                if real(b + 2):
                    pe.wait_ge(xT_sb, b + 3)
                    at_least(pe, split_step, (b + 2) * SPLIT)
                    for s in two:
                        last = pe.matmul(st0[:, 2 + s, :], w_qk[:, s * C:(s + 1) * C], xT[p][:, :], start=True, stop=True)
                    last.then_inc(qk_ps, 1)
                if real(b + 1):
                    values_of(b + 1, o, 1)
                    scores_by_query(b + 1, o, 3)
                    values_of(b + 1, o, 2)
                    scores_by_key(b + 1, o, 0)
                    values_of(b + 1, o, 3)
                    maxima_by_head(b + 1, 1, sm0)

            pipelined(pe, step, 3, 1, first=2)

        @block.scalar
        def _(act):
            def exponentials(b, j):
                at_least(act, ctx_ps, b * QUADS + j - 1)
                act.wait_ge(st_ps, (b * QUADS + j) * 2 + 1)
                act.activation(p0[j % 2][:, :, :], st0[:, :, :], ACT.Exp, scale=SCALE).then_inc(p_sb, 1)
                act.wait_ge(st_ps, (b * QUADS + j) * 2 + 2)
                act.activation(p1[j % 2][:, :, :], st1[:, :, :], ACT.Exp, scale=SCALE).then_inc(p_sb, 1)

            def maxima_out(b, p, half, bank):
                act.wait_ge(rows_ps, b * 2 + half + 1)
                at_least(act, rows_in[half], b * 16)
                act.activation(max_rows[half][:, :], turned(bank), ACT.Copy).then_inc(rows_sb, 1)
                act.wait_ge(rows_sb, b * 2 + half + 1)
                heads = slice(half * H // 2, (half + 1) * H // 2)
                act.dma_start(q_st[p][SHIFT_ROW:SHIFT_ROW + 1, heads, :], max_rows[half][:, :]).then_inc(rows_in[half], 16)

            def values_out(b, p, n):
                j, half = divmod(n, 2)
                act.wait_ge(v_ps, b * V_OUT + n + 1)
                if n == 0:
                    at_least(act, ctx_ps, (b - 1) * QUADS)
                act.activation(values[p][:, j, half * 512:(half + 1) * 512],
                               ps_c[:, :, :].rearrange("p a b -> p (a b)"), ACT.Copy).then_inc(v_sb, 1)

            def context_out(b, p, j):
                act.wait_ge(ctx_ps, b * QUADS + j + 1)
                at_least(act, wo_ps, b - 1)
                act.activation(ctxs[p][:, 2 * j:2 * j + 2, :], ps_c[:, :, :], ACT.Copy).then_inc(ctx_sb, 1)

            def step(b, hb, p):
                o = 1 - p
                if real(b):
                    exponentials(b, 1)
                    context_out(b, p, 0)
                    exponentials(b, 2)
                    context_out(b, p, 1)
                    exponentials(b, 3)
                    context_out(b, p, 2)
                    context_out(b, p, 3)
                if real(b + 1):
                    maxima_out(b + 1, o, 0, st1)
                if real(b + 2):
                    act.wait_ge(xT_ps, b + 3)
                    at_least(act, v_ps, (b + 1) * V_OUT)
                    act.activation(xT[p][:, :], st1[:, 0:NB, :].rearrange("p a b -> p (a b)"), ACT.Copy).then_inc(xT_sb, 1)
                if real(b + 1):
                    values_out(b + 1, o, 0)
                if real(b + 2):
                    act.wait_ge(qk_ps, b + 3)
                    at_least(act, parts_out, (b + 1) * 16)
                    act.activation(parts[p][:, 0, :], st0[:, 2:4, :].rearrange("p a b -> p (a b)"), ACT.Copy).then_inc(hi_sb, 1)
                if real(b + 1):
                    values_out(b + 1, o, 1)
                    values_out(b + 1, o, 2)
                    exponentials(b + 1, 0)
                    values_out(b + 1, o, 3)
                    maxima_out(b + 1, o, 1, sm0)

            pipelined(act, step, 3, 1, first=2)

        @block.vector
        def _(dve):
            dve.tensor_copy(w_qk[:, :].rearrange("p (s c h) -> p s c h", s=2, h=H),
                            w_qk_in[:, :].rearrange("p (s h c) -> p s c h", s=2, c=HD)).then_inc(w_turned, 1)
            added, layer3, split = Steps(dve, x2_step, X2), Steps(dve, x3_step, X3), Steps(dve, split_step, SPLIT)

            def statistics(s, y, stats, mv, pow_sem, b):
                s.wait()
                for j in range(NB):
                    s.did(dve.bn_stats(stats[:, j, :], y[:, j, :]))
                wait_apart(dve, k, (s.sem, s.base + s.n),
                                   (pow_sem, b * POW))
                for j in range(NB):
                    s.did(dve.bn_aggr(mv[:, j, :], stats[:, j, :]))

            def normalise(s, y, mv, rstd, pow_sem, b, out):
                dve.wait_ge(pow_sem, (b + 1) * POW)
                for j in range(NB):
                    s.did(dve.tensor_scalar(out[:, j, :], y[:, j, :], mv[:, j, 0:1], rstd[:, j:j + 1], ALU.subtract, ALU.mult))
                s.end()

            def maxima(b, j):
                for n, (ps, q) in enumerate(((sm1, 1), (sm0, 0))):
                    dve.wait_ge(sm_ps, (b * QUADS + j) * 2 + n + 1)
                    if j == 0 and n == 0:
                        at_least(dve, rows_ps, b * 2)
                    dve.tensor_reduce(neg_max[:, q, 4 * j:4 * j + 4], ps[:, :, :], AX.X, ALU.max, negate=True)\
                       .then_inc(max_done, 1)

            def divide(b, p, j):
                dve.wait_ge(ctx_sb, b * QUADS + j + 1)
                dve.wait_ge(rrep_in, (b + 1) * 64)
                dve.tensor_tensor(ctxs[p][:, 2 * j:2 * j + 2, :], ctxs[p][:, 2 * j:2 * j + 2, :],
                                  rrep[:, 2 * j:2 * j + 2, :], ALU.mult).then_inc(divided, 1)

            def step(b, hb, p):
                o = 1 - p
                if real(b - 1):
                    for j in range(QUADS):
                        divide(b - 1, o, j)
                if real(b + 2):
                    s = added.batch(b + 2)
                    dve.wait_ge(xa_in[p], (hb + 2) * 16)
                    dve.wait_ge(fetched[p], (hb + 2) * 16 * NB)
                    for j in range(NB):
                        col = (b + 2) * NB + j
                        w = k["weight"][:, col:col + 1] if isinstance(b, int) else k["weight"][:, bass.ds(col, 1)]
                        s.did(dve.scalar_tensor_tensor(y2[:, j, :], eg[p][:, j, :], w, xa[p][:, j, :], ALU.mult, ALU.add))
                    statistics(s, y2, stats2, mv2, pow2, b + 2)
                    at_least(dve, x2_out[p], (hb + 1) * 16)
                    at_least(dve, xT_ps, b + 1)
                    normalise(s, y2, mv2, rstd2, pow2, b + 2, x2[p])
                if real(b - 1):
                    s = layer3.batch(b - 1)
                    dve.wait_ge(wo_ps, b)
                    dve.wait_ge(xr_in[o], 16 * (hb + p))
                    s.did(dve.tensor_tensor(y3[:, :, :], sm0[:, 0:NB, :], xr[o][:, :, :], ALU.add))
                if real(b + 1):
                    maxima(b + 1, 0)
                if real(b - 1):
                    statistics(s, y3, stats3, mv3, pow3, b - 1)
                if real(b + 1):
                    maxima(b + 1, 1)
                if real(b - 1):
                    cols = slice((b - 1) * NB, b * NB) if isinstance(b, int) else bass.ds((b - 1) * NB, NB)
                    normalise(s, y3, mv3, rstd3, pow3, b - 1, k["x3"][:, cols, :])
                if real(b):
                    dve.wait_ge(ctx_ps, (b + 1) * QUADS)
                    at_least(dve, rden_out, b * 16)
                    dve.reciprocal(rden[:, :], ps_d[:, 0:N]).then_inc(rden_sb, 1)
                if real(b + 1):
                    maxima(b + 1, 2)
                if real(b + 2):
                    s = split.batch(b + 2)
                    dve.wait_ge(hi_sb, b + 3)
                    at_least(dve, lo_sb, b + 2)
                    s.did(dve.tensor_tensor(rest[:, :], st0[:, 2:4, :].rearrange("p a b -> p (a b)"), parts[p][:, 0, :], ALU.subtract))
                    s.wait()
                    s.did(dve.tensor_copy(parts[p][:, 1, :], rest[:, :]))
                    s.end()
                if real(b + 1):
                    maxima(b + 1, 3)

            pipelined(dve, step, 3, 1, first=2)

        @block.gpsimd
        def _(pool):
            def root(pow_sem, step_sem, done, mv, veps, rstd, b):
                wait_apart(pool, k, (step_sem, done))
                pool.tensor_scalar(veps[:, :], mv[:, :, 1], EPS_LN, None, ALU.add).then_inc(pow_sem, 1)
                pool.wait_ge(pow_sem, b * POW + 1)
                pool.tensor_tensor(rstd[:, :], veps[:, :], k["minus_half"][:, 0:NB], ALU.pow).then_inc(pow_sem, 1)

            def mask(b, j):
                for n, pr in enumerate((p0[j % 2], p1[j % 2])):
                    wait_apart(pool, k, (p_sb, (b * QUADS + j) * 2 + n + 1))
                    pool.affine_select(out=pr[:, :, 0:P], in_=pr[:, :, 0:P], compare_op=ALU.is_ge, fill=0.0, base=0,
                                       pattern=[[0, 4], [1, P]], channel_multiplier=-1).then_inc(masked, 1)

            def step(b, hb, p):
                o = 1 - p
                if real(b + 3):
                    at_least(pool, x2_step, (b + 1) * X2 + NB)
                    at_least(pool, fetched[p], 16 * NB * (hb + 2))
                    cols = slice((b + 3) * NB, (b + 4) * NB) if isinstance(b, int) else bass.ds((b + 3) * NB, NB)
                    pool.tensor_copy(index[:, :], k["fetch"][:, cols]).then_inc(index_set, 1)
                    wait_apart(pool, k, (index_set, b + 4))
                    for j in range(NB):
                        pool.indirect_dma_start(out=eg[o][:, j, :], out_offset=None, in_=eout_d,
                                                in_offset=bass.IndirectOffsetOnAxis(ap=index[:, j:j + 1], axis=0))\
                            .then_inc(fetched[o], 16)
                if real(b):
                    mask(b, 1)
                if real(b + 2):
                    root(pow2, x2_step, (b + 2) * X2 + 3 * NB, mv2, veps2, rstd2, b + 2)
                if real(b):
                    mask(b, 2)
                    mask(b, 3)
                if real(b - 1):
                    root(pow3, x3_step, (b - 1) * X3 + 1 + 2 * NB, mv3, veps3, rstd3, b - 1)
                if real(b + 2):
                    pool.wait_ge(split_step, (b + 3) * SPLIT)
                    pool.tensor_tensor(parts[p][:, 2, :], rest[:, :], parts[p][:, 1, :], ALU.subtract).then_inc(lo_sb, 1)
                if real(b + 1):
                    mask(b + 1, 0)

            pipelined(pool, step, 3, 1)


def coupling_layer(nc, k, out, debug=None):
    CYCLES, HALVES, GROUPS, GB = 3, 2, 4, 4
    W = GB * P
    HB = GROUPS * GB
    BATCHES = HB // NB
    F2, F3 = C // 2, C // 4
    Q = C // 4

    with ExitStack() as ctx:
        sb = lambda name, shape, dt: ctx.enter_context(nc.sbuf_tensor("cn_" + name, shape, dt))
        pb = lambda name, shape, dt: ctx.enter_context(nc.psum_tensor("cn_" + name, shape, dt))
        sem = lambda name: ctx.enter_context(nc.semaphore("cn_" + name))
        two = range(2)
        x3 = k["x3"]
        cur = sb("cur", [P, HALVES * HB, C], FP32)
        (w1, w2, w3, w4), (b1, b2, b3, b4) = k["cn_w"], k["cn_b"]
        (g1, g2, g3), (gb1, gb2, gb3), spread = k["gc_w"], k["gc_b"], k["spread"]
        g3_rep = sb("g3_rep", [F3, P], FP32)
        spread_g, spread_t = sb("spread_g", [P, 1], FP32), sb("spread_t", [P, 1], FP32)
        xT = [sb(f"xT{i}", [P, W], FP32) for i in two]
        h1 = [sb(f"h1_{i}", [P, W], FP32) for i in range(GROUPS)]
        h2 = [sb(f"h2_{i}", [P, W], FP32) for i in two]
        h3 = sb("h3", [P, W], FP32)
        tanh_t = sb("tanh_t", [P, HB], FP32)
        coupling, minus_coupling = sb("coupling", [P, HB], FP32), sb("minus_coupling", [P, HB], FP32)
        context = sb("context", [P, HALVES, BATCHES], FP32)
        gh1, gh2 = sb("gh1", [F2, BATCHES], FP32), sb("gh2", [F3, BATCHES], FP32)
        tanh_g = sb("tanh_g", [P, BATCHES], FP32)
        base = sb("base", [P, HALVES, BATCHES], FP32)
        aside = [sb(f"aside{i}", [P, GB, 2, Q], FP32) for i in two]
        y = sb("y", [P, HALVES * HB, C], FP32)
        stats, mv = sb("stats", [P, HALVES * HB, 6], FP32), sb("mv", [P, HALVES * HB, 2], FP32)
        veps, rstd, shift = (sb(n, [P, HALVES * HB], FP32) for n in ("veps", "rstd", "shift"))
        result = sb("result", [P, HALVES * HB, C], FP32)
        ps_t = [pb(f"ps_t{i}", [P, W], FP32) for i in two]
        ps_1 = [pb(f"ps_1{i}", [P, W], FP32) for i in two]
        ps_2 = [pb(f"ps_2{i}", [P, W], FP32) for i in two]
        ps_3 = pb("ps_3", [P, W], FP32)
        ps_z = pb("ps_z", [P, W], FP32)
        t_ps, xT_sb, h1_ps, h1_sb = (sem(n) for n in ("t_ps", "xT_sb", "h1_ps", "h1_sb"))
        h2_ps, h2_sb, h3_ps, h3_sb, z_ps, tanh_sb = (sem(n) for n in ("h2_ps", "h2_sb", "h3_ps", "h3_sb", "z_ps", "tanh_sb"))
        setup, summed, g_ps, g_sb, base_set = (sem(n) for n in ("setup", "summed", "g_ps", "g_sb", "base_set"))
        coupled, aside_set, middle_moved, moved = (sem(n) for n in ("coupled", "aside_set", "middle_moved", "moved"))
        added, moved_last, stat_step, root_set, shift_set = (sem(n) for n in ("added", "moved_last", "stat_step", "root_set", "shift_set"))
        normed, stored = [sem(f"normed{i}") for i in range(HALVES * GROUPS)], sem("stored")
        block = ctx.enter_context(nc.Block())
        STAT = 3
        BY_ACT = 6
        SETUP = 5
        G = 3

        @block.sync
        def _(sp):
            if debug:
                sp.dma_start(debug["x3"].rearrange("(b p) c -> p b c", p=P), x3[:, :, :]).then_inc(stored, 16)
                sp.wait_ge(stored, 16)
            for g in range(HALVES * GROUPS):
                sp.wait_ge(normed[g], 1)
                sp.dma_start(out[g * W:(g + 1) * W, :].rearrange("(j p) c -> p j c", p=P),
                             result[:, g * GB:(g + 1) * GB, :]).then_inc(stored, 16)
            sp.wait_ge(stored, 16 * (HALVES * GROUPS + (1 if debug else 0)))


        @block.tensor
        def _(pe):
            def turn(n, s, src, g):
                at_least(pe, moved, (n - 2) * GROUPS + g + 1)
                at_least(pe, xT_sb, n * GROUPS + g - 1)
                for j in range(GB):
                    last = pe.transpose(ps_t[g % 2][:, j * P:(j + 1) * P], src[:, s * HB + g * GB + j, :], k["ident"][:, :])
                last.then_inc(t_ps, 1)

            def layer1(n, g):
                pe.wait_ge(xT_sb, n * GROUPS + g + 1)
                at_least(pe, h1_sb, n * GROUPS + g - 1)
                pe.matmul(ps_1[g % 2][:, :], w1[:, :], xT[g % 2][:, :], start=True, stop=True).then_inc(h1_ps, 1)

            def layer2(n, i):
                pe.wait_ge(h1_sb, n * GROUPS + 2 * i + 2)
                at_least(pe, h2_sb, (n - 1) * 2 + i + 1)
                for u in two:
                    last = pe.matmul(ps_2[i][u * F2:(u + 1) * F2, :], w2[:, :], h1[2 * i + u][:, :], start=True, stop=True)
                last.then_inc(h2_ps, 1)

            def layer3(n):
                pe.wait_ge(h2_sb, n * 2 + 2)
                at_least(pe, h3_sb, n)
                for i in two:
                    last = pe.matmul(ps_3[i * F2:(i + 1) * F2, :], w3[:, :], h2[i][:, :], start=True, stop=True)
                last.then_inc(h3_ps, 1)

            def layer4(n):
                pe.wait_ge(h3_sb, n + 1)
                at_least(pe, tanh_sb, n)
                if isinstance(n, int) and n == 1:
                    pe.wait_ge(g_sb, 2 * G)
                elif isinstance(n, int) and n == 0:
                    pe.wait_ge(g_sb, G)
                for j in range(GB):
                    last = pe.matmul(ps_z[:, j:HB:GB], h3[:, j * P:(j + 1) * P], w4[:, :], start=True, stop=True)
                last.then_inc(z_ps, 1)

            def global_net(s):
                pe.wait_ge(summed, (s + 1) * GROUPS)
                at_least(pe, tanh_sb, s)
                n = s * G
                pe.matmul(ps_z[0:F2, 0:BATCHES], g1[:, :], context[:, s, :], start=True, stop=True).then_inc(g_ps, 1)
                pe.wait_ge(g_sb, n + 1)
                pe.matmul(ps_z[0:F3, 0:BATCHES], g2[:, :], gh1[:, :], start=True, stop=True).then_inc(g_ps, 1)
                pe.wait_ge(g_sb, n + 2)
                pe.matmul(ps_z[:, 0:BATCHES], g3_rep[:, :], gh2[:, :], start=True, stop=True).then_inc(g_ps, 1)

            def run(n, s, src, before=True):
                turn(n, s, src, 0)
                turn(n, s, src, 1)
                if before:
                    layer2(n - 1, 1)
                layer1(n, 0)
                turn(n, s, src, 2)
                if before:
                    layer3(n - 1)
                layer1(n, 1)
                turn(n, s, src, 3)
                if before:
                    layer4(n - 1)
                layer1(n, 2)
                layer2(n, 0)
                layer1(n, 3)

            pe.wait_ge(setup, SETUP)
            run(0, 0, x3, before=False)
            global_net(0)
            run(1, 1, x3)
            global_net(1)
            with pe.Fori(1, CYCLES) as cycle:
                for s in two:
                    run(cycle * 2 + s, s, cur)
            layer2(2 * CYCLES - 1, 1)
            layer3(2 * CYCLES - 1)
            layer4(2 * CYCLES - 1)

        @block.scalar
        def _(act):
            def gelu1(n, g):
                act.wait_ge(h1_ps, n * GROUPS + g + 1)
                at_least(act, h2_ps, (n - 1) * 2 + g // 2 + 1)
                act.activation(h1[g][:, :], ps_1[g % 2][:, :], ACT.Gelu, bias=b1[:, :]).then_inc(h1_sb, 1)

            def gelu2(n, i):
                act.wait_ge(h2_ps, n * 2 + i + 1)
                at_least(act, h3_ps, n)
                act.activation(h2[i][:, :], ps_2[i][:, :], ACT.Gelu, bias=b2[:, :]).then_inc(h2_sb, 1)

            def gelu3(n):
                act.wait_ge(h3_ps, n + 1)
                at_least(act, z_ps, n)
                act.activation(h3[:, :], ps_3[:, :], ACT.Gelu, bias=b3[:, :]).then_inc(h3_sb, 1)

            def tanh4(n):
                act.wait_ge(z_ps, n + 1)
                at_least(act, coupled, 2 * n)
                act.activation(tanh_t[:, :], ps_z[:, 0:HB], ACT.Tanh, bias=b4[:, :], scale=0.5).then_inc(tanh_sb, 1)

            def global_net(s):
                n = s * G
                act.wait_ge(g_ps, n + 1)
                act.activation(gh1[:, :], ps_z[0:F2, 0:BATCHES], ACT.Gelu, bias=gb1[:, :], scale=1.0 / N).then_inc(g_sb, 1)
                act.wait_ge(g_ps, n + 2)
                act.activation(gh2[:, :], ps_z[0:F3, 0:BATCHES], ACT.Gelu, bias=gb2[:, :]).then_inc(g_sb, 1)
                act.wait_ge(g_ps, n + 3)
                at_least(act, base_set, s)
                act.activation(tanh_g[:, :], ps_z[:, 0:BATCHES], ACT.Tanh, bias=gb3[:, :], scale=0.5).then_inc(g_sb, 1)

            def copy_out(n, g):
                act.wait_ge(t_ps, n * GROUPS + g + 1)
                at_least(act, h1_ps, n * GROUPS + g - 1)
                if isinstance(n, int) and n < HALVES:
                    at_least(act, summed, n * GROUPS + g - 1)
                act.activation(xT[g % 2][:, :], ps_t[g % 2][:, :], ACT.Copy).then_inc(xT_sb, 1)

            def run(n, s, before=True):
                copy_out(n, 0)
                copy_out(n, 1)
                if before:
                    gelu2(n - 1, 1)
                gelu1(n, 0)
                copy_out(n, 2)
                if before:
                    gelu3(n - 1)
                gelu1(n, 1)
                copy_out(n, 3)
                if before:
                    tanh4(n - 1)
                gelu1(n, 2)
                gelu2(n, 0)
                gelu1(n, 3)

            act.wait_ge(setup, SETUP)
            run(0, 0, before=False)
            global_net(0)
            run(1, 1)
            global_net(1)
            with act.Fori(1, CYCLES) as cycle:
                for s in two:
                    run(cycle * 2 + s, s)
            gelu2(2 * CYCLES - 1, 1)
            gelu3(2 * CYCLES - 1)
            tanh4(2 * CYCLES - 1)
            for group in range(BY_ACT):
                act.wait_ge(shift_set, group + 1)
                for j in range(group * GB, (group + 1) * GB):
                    last = act.activation(result[:, j, :], y[:, j, :], ACT.Identity,
                                          bias=shift[:, j:j + 1], scale=rstd[:, j:j + 1])
                last.then_inc(normed[group], 1)

        @block.vector
        def _(dve):
            dve.tensor_copy(g3_rep[:, :], g3[:, :].broadcast_to([F3, P])).then_inc(setup, 1)
            dve.tensor_scalar(b4[:, :], b4[:, :], 0.5, None, ALU.mult).then_inc(setup, 1)
            dve.tensor_scalar(gb3[:, :], gb3[:, :], 0.5, None, ALU.mult).then_inc(setup, 1)
            dve.tensor_scalar(spread_g[:, :], spread[:, :], 0.7, None, ALU.mult).then_inc(setup, 1)
            dve.tensor_scalar(spread_t[:, :], spread[:, :], 0.3, None, ALU.mult).then_inc(setup, 1)
            dve.wait_ge(setup, SETUP)

            def sums(s, g):
                dve.wait_ge(xT_sb, s * GROUPS + g + 1)
                dve.tensor_reduce(context[:, s, 2 * g:2 * g + 2], xT[g % 2][:, :].rearrange("p (b n) -> p b n", n=N),
                                  AX.X, ALU.add).then_inc(summed, 1)

            def global_part(s):
                dve.wait_ge(g_sb, (s + 1) * G)
                dve.tensor_scalar(base[:, s, :], tanh_g[:, :], spread_g[:, :], 0.1, ALU.mult, ALU.add).then_inc(base_set, 1)

            def couple(n, s):
                if isinstance(n, int) and n < HALVES:
                    dve.wait_ge(base_set, n + 1)
                dve.wait_ge(tanh_sb, n + 1)
                if n <= HALVES * (CYCLES - 1):
                    at_least(dve, moved, n * GROUPS)
                else:
                    dve.wait_ge(moved_last, (n - HALVES * (CYCLES - 1)) * GROUPS)
                dve.scalar_tensor_tensor(coupling[:, :].rearrange("p (b j) -> p b j", j=NB),
                                         tanh_t[:, :].rearrange("p (b j) -> p b j", j=NB), spread_t[:, :],
                                         base[:, s, :].unsqueeze(2).broadcast_to([P, BATCHES, NB]),
                                         ALU.mult, ALU.add).then_inc(coupled, 1)
                dve.wait_ge(coupled, 2 * n + 1)
                dve.tensor_scalar(minus_coupling[:, :], coupling[:, :], -1.0, None, ALU.mult).then_inc(coupled, 1)
                dve.wait_ge(coupled, 2 * n + 2)

            def quarters(t, b):
                return t[:, b, :].rearrange("p (q w) -> p q w", w=Q)

            def move(n, s, src, g):
                in_place = src is cur
                aside_step = (n - 2) * GROUPS + g
                if in_place:
                    at_least(dve, moved, n * GROUPS + g - 1)
                for j in range(GB):
                    t = s * HB + g * GB + j
                    b = g * GB + j
                    x = quarters(src, t)
                    to = aside[g % 2][:, j, :, :] if in_place else quarters(cur, t)[:, 0:4:3, :]
                    last = dve.scalar_tensor_tensor(to, x[:, 2:0:-1, :], coupling[:, b:b + 1], x[:, 0:4:3, :], ALU.mult, ALU.add)
                if in_place:
                    last.then_inc(aside_set, 1)
                    dve.wait_ge(aside_set, aside_step + 1)
                for j in range(GB):
                    t = s * HB + g * GB + j
                    b = g * GB + j
                    x = quarters(src, t)
                    last = dve.scalar_tensor_tensor(quarters(cur, t)[:, 1:3, :], x[:, 3::-3, :], minus_coupling[:, b:b + 1],
                                                    x[:, 1:3, :], ALU.mult, ALU.add)
                last.then_inc(middle_moved if in_place else moved, 1)

            def move_last(n, s, g):
                dve.wait_ge(added, s * GROUPS + g + 1)
                for j in range(GB):
                    t = s * HB + g * GB + j
                    b = g * GB + j
                    x, to = quarters(cur, t), quarters(y, t)
                    dve.scalar_tensor_tensor(to[:, 0:4:3, :], x[:, 2:0:-1, :], coupling[:, b:b + 1], to[:, 0:4:3, :],
                                             ALU.mult, ALU.add)
                    last = dve.scalar_tensor_tensor(to[:, 1:3, :], x[:, 3::-3, :], minus_coupling[:, b:b + 1], to[:, 1:3, :],
                                                    ALU.mult, ALU.add)
                last.then_inc(moved_last, 1)

            def statistics(group):
                blocks = slice(group * GB, (group + 1) * GB)
                s = Steps(dve, stat_step, STAT).batch(group)
                dve.wait_ge(moved_last, group + 1)
                for j in range(group * GB, (group + 1) * GB):
                    last = dve.bn_stats(stats[:, j, :], y[:, j, :])
                s.did(last)
                s.wait()
                for j in range(group * GB, (group + 1) * GB):
                    last = dve.bn_aggr(mv[:, j, :], stats[:, j, :])
                s.did(last)
                s.wait()
                s.did(dve.tensor_scalar(veps[:, blocks], mv[:, blocks, 1], EPS_LN, None, ALU.add))
                s.end()

            def shifts(group):
                blocks = slice(group * GB, (group + 1) * GB)
                dve.wait_ge(root_set, group + 1)
                dve.scalar_tensor_tensor(shift[:, blocks], mv[:, blocks, 0], -1.0, rstd[:, blocks], ALU.mult, ALU.mult)\
                   .then_inc(shift_set, 1)

            def norm(group):
                dve.wait_ge(root_set, group + 1)
                for j in range(group * GB, (group + 1) * GB):
                    last = dve.tensor_scalar(result[:, j, :], y[:, j, :], mv[:, j, 0:1], rstd[:, j:j + 1],
                                             ALU.subtract, ALU.mult)
                last.then_inc(normed[group], 1)

            for s in two:
                for g in range(GROUPS):
                    sums(s, g)
                if s == 1:
                    couple(0, 0)
                    for g in range(GROUPS):
                        move(0, 0, x3, g)
                global_part(s)
            for n in range(1, HALVES * (CYCLES - 1)):
                couple(n, n % 2)
                for g in range(GROUPS):
                    move(n, n % 2, x3 if n < HALVES else cur, g)
            for s in two:
                n = HALVES * (CYCLES - 1) + s
                couple(n, s)
                for g in range(GROUPS):
                    move_last(n, s, g)
                for g in range(GROUPS):
                    statistics(s * GROUPS + g)
                    if g > 0 and s * GROUPS + g - 1 < BY_ACT:
                        shifts(s * GROUPS + g - 1)
                if (s + 1) * GROUPS - 1 < BY_ACT:
                    shifts((s + 1) * GROUPS - 1)
            for group in range(BY_ACT, HALVES * GROUPS):
                norm(group)

        @block.gpsimd
        def _(pool):
            def put_back(n, s, g):
                pool.wait_ge(middle_moved, (n - 2) * GROUPS + g + 1)
                blocks = slice(s * HB + g * GB, s * HB + (g + 1) * GB)
                pool.tensor_copy(cur[:, blocks, :].rearrange("p b (q w) -> p b q w", w=Q)[:, :, 0:4:3, :],
                                 aside[g % 2][:, :, :, :]).then_inc(moved, 1)

            def add(s, g):
                blocks = slice(s * HB + g * GB, s * HB + (g + 1) * GB)
                pool.wait_ge(moved, (HALVES * (CYCLES - 2) + s) * GROUPS + g + 1)
                pool.tensor_tensor(y[:, blocks, :], x3[:, blocks, :], cur[:, blocks, :], ALU.add).then_inc(added, 1)

            for n in range(HALVES, HALVES * (CYCLES - 1)):
                for g in range(GROUPS):
                    put_back(n, n % 2, g)
                if n >= HALVES * (CYCLES - 2):
                    for g in range(GROUPS):
                        add(n % 2, g)
            for group in range(HALVES * GROUPS):
                blocks = slice(group * GB, (group + 1) * GB)
                pool.wait_ge(stat_step, (group + 1) * STAT)
                pool.tensor_tensor(rstd[:, blocks], veps[:, blocks], k["minus_half"][:, 0:GB], ALU.pow).then_inc(root_set, 1)


def program(nc, a, out, debug=None):
    x = a["L0_attn_x"].rearrange("b n c -> (b n) c")
    scratch = lambda name, shape, dt: nc.dram_tensor(name, shape, dt, kind="Internal").ap()
    parts_d = scratch("parts_d", [3, P, 2 * N], BF16)
    x1_d = scratch("x1_d", [T, C], FP32) if not debug else debug["x1"]
    disp_d = scratch("disp_d", [SLOTS + T, C], FP32)
    eout_d = scratch("eout_d", [SLOTS, C], FP32) if not debug else debug["eout"]
    x2_d = scratch("x2_d", [T, C], FP32) if not debug else debug["x2"]
    rden_d = scratch("rden_d", [P, N], FP32)
    with ExitStack() as ctx:
        sb = lambda name, shape, dt: ctx.enter_context(nc.sbuf_tensor(name, shape, dt))
        k = {
            "ident": sb("ident", [P, P], FP32), "ident_bf": sb("ident_bf", [P, P], BF16),
            "tri_bf": sb("tri_bf", [P, P], BF16), "ones_bf": sb("ones_bf", [P, P], BF16),
            "ones": sb("ones", [P, P], FP32), "causal": sb("causal", [P, 4 * P], BF16),
            "zeros": sb("zeros", [P, 5 * C], FP32), "minus_half": sb("minus_half", [P, 4], FP32),
            "three_halves": sb("three_halves", [P, 2 * NB * H], FP32), "eps_rms": sb("eps_rms", [P, 2 * NB * H], FP32),
            "backwards": sb("backwards", [P, E], FP32), "gate_T": sb("gate_T", [P, E], FP32),
            "slots_before": sb("slots_before", [P, E], FP32), "slots_end": sb("slots_end", [P, E], FP32),
            "dump": sb("dump", [P, NB], FP32), "qks": sb("qks", [P, HD], FP32),
            "minus_bound": sb("minus_bound", [P, 1], FP32),
            "w1": [sb(f"w1_{i}", [P, FF], FP32) for i in range(4)],
            "w2": [sb(f"w2_{i}", [P, FC, C], FP32) for i in range(4)],
            "w_in": [ctx.enter_context(nc.semaphore(f"expert_in{i}")) for i in range(4)],
            "constants_set": ctx.enter_context(nc.semaphore("constants_set")),
            "fetch": sb("fetch", [P, T // P], U32), "weight": sb("weight", [P, T // P], FP32),
            "q_st": [sb(f"q_st{i}", [P, H, N], BF16) for i in range(2)],
            "k_st": [sb(f"k_st{i}", [P, H, N], BF16) for i in range(2)],
            **second_layer_weights(sb),
            "x3": sb("x3", [P, T // P, C], FP32),
        }
        constants(nc, k, a["L0_ffn_gate_w"], a["L0_attn_q_scale"], a["L0_attn_k_scale"])
        l0_layer(nc, k, x, a["L0_attn_Wqkv"], a["L0_attn_Wproj"], a["L0_attn_bproj"],
                 a["L0_ffn_w1"], a["L0_ffn_w2"], parts_d, x1_d, disp_d)
        experts(nc, k, a, disp_d, eout_d)
        l1_layer(nc, k, parts_d, rden_d, x1_d, eout_d, x2_d)
        coupling_layer(nc, k, out, debug)


_INS = ['L0_attn_x', 'L0_attn_Wqkv', 'L0_attn_Wproj', 'L0_attn_bproj',
        'L0_attn_q_scale', 'L0_attn_k_scale', 'L0_ffn_gate_w', 'L0_ffn_w1',
        'L0_ffn_w2', 'L1_attn_Wq', 'L1_attn_Wk', 'L1_attn_Wv',
        'L1_attn_Wo', 'L1_ffn_cn_w1', 'L1_ffn_cn_b1', 'L1_ffn_cn_w2',
        'L1_ffn_cn_b2', 'L1_ffn_cn_w3', 'L1_ffn_cn_b3', 'L1_ffn_cn_w4',
        'L1_ffn_cn_b4', 'L1_ffn_gc_w1', 'L1_ffn_gc_b1', 'L1_ffn_gc_w2',
        'L1_ffn_gc_b2', 'L1_ffn_gc_w3', 'L1_ffn_gc_b3', 'L1_ffn_adaptive_range']


def kernel(**inputs):
    import numpy as np
    import concourse.bacc as bacc
    from concourse.bass_utils import run_bass_kernel_spmd

    nc = bacc.Bacc("TRN2", target_bir_lowering=False, num_devices=1)
    arrays, tensors = {}, {}
    for name in _INS:
        array = np.ascontiguousarray(inputs[name])
        arrays[f"in_{name}_dram"] = array
        tensors[name] = nc.dram_tensor(f"in_{name}_dram", array.shape, mybir.dt.from_np(array.dtype), kind="ExternalInput").ap()
    out = nc.dram_tensor("out_0_dram", (B, N, C), FP32, kind="ExternalOutput").ap()
    program(nc, tensors, out.rearrange("b n c -> (b n) c"))
    result = run_bass_kernel_spmd(nc, [arrays], core_ids=[0])
    return result.results[0]["out_0_dram"]
```
